# Optimizing a Trainium2 kernel written in Bass

```python
import numpy as np
import jax
import jax.numpy as jnp

def _softmax(x, axis=-1):
    return jax.nn.softmax(x, axis=axis)
def _gelu(x):
    return jax.nn.gelu(x, approximate=True)
def _silu(x):
    return jax.nn.silu(x)
def _sigmoid(x):
    return jax.nn.sigmoid(x)
def _layernorm(x, axis=-1, eps=1e-5):
    m = jnp.mean(x, axis=axis, keepdims=True)
    v = jnp.var(x, axis=axis, keepdims=True)
    return (x - m) / jnp.sqrt(v + eps)
def _scatter_add(tgt, idx, src, axis=0):
    return tgt.at[idx].add(src)
def _segment_sum(src, seg, n):
    return jax.ops.segment_sum(src, seg, n)

kernel_name = 'mk_adj_preln_d4_adj_256_30c2d3'

def setup_inputs(seed: int = 0):
    np.random.seed(seed)
    _w = jnp.asarray
    def _rec_inputs():
        import jax
        import jax.numpy as jnp
        _gk = jax.random.key(seed)
        x = -8.015e-05 + 0.9999 * jax.random.normal(jax.random.fold_in(_gk, 1), (16, 1024, 256), jnp.float32)
        _a = jax.random.bernoulli(jax.random.fold_in(_gk, 2), 0.015625, (16, 1024, 1024))
        _a = jnp.logical_or(_a, jnp.swapaxes(_a, -1, -2))
        _a = jnp.logical_or(_a, jnp.eye(1024, dtype=bool))
        _af = _a.astype(jnp.float32)
        _af = _af * jax.random.uniform(jax.random.fold_in(_gk, 3), (16, 1024, 1024), jnp.float32, 0.05, 0.999837)
        adj = _af
        return x, adj
    x, adj = _rec_inputs()
    def _L0_gnn_setup():
        import jax, jax.numpy as jnp
        import numpy as np
        GROUPS = [list(range(25)), [0, 1, 2, 3, 4, 5, 6, 7, 8], [0, 9, 10, 11, 12, 13, 14], [6, 7, 8, 12, 13, 14], [3, 4, 5, 9, 10, 11]]
        B, N, D_IN, D_HID = (8192, 25, 256, 512)

        def _graph_conv(x, adj, W, b):
            n = adj.shape[-1]
            A = adj + jnp.eye(n, dtype=adj.dtype)
            deg = jnp.sum(A, axis=-1)
            deg_safe = jnp.where(deg == 0, 1.0, deg)
            dinv = jnp.where(deg == 0, 0.0, deg_safe ** (-0.5))
            norm_adj = dinv[:, :, None] * A * dinv[:, None, :]
            support = jnp.einsum('bnd,de->bne', x, W)
            out = jnp.einsum('bnm,bme->bne', norm_adj, support) + b
            return jax.nn.relu(out)
        key = jax.random.key(seed)
        ks = jax.random.split(key, 7)
        s1 = float(np.sqrt(6.0 / (D_IN + D_HID)))
        s2 = float(np.sqrt(6.0 / (D_HID + D_IN)))
        return {'x': jax.random.normal(ks[0], (B, N, D_IN), dtype=jnp.float32), 'adj': jax.random.uniform(ks[1], (B, N, N), dtype=jnp.float32), 'W1': jax.random.uniform(ks[2], (5, D_IN, D_HID), jnp.float32, -s1, s1), 'b1': jnp.zeros((5, D_HID), dtype=jnp.float32), 'W2': jax.random.uniform(ks[3], (5, D_HID, D_IN), jnp.float32, -s2, s2), 'b2': jnp.zeros((5, D_IN), dtype=jnp.float32), 'fusion_w': jnp.ones((5,), dtype=jnp.float32)}
    _L0_gnn_all = _L0_gnn_setup()
    _L0_gnn_in = {k: v for k, v in _L0_gnn_all.items() if k in ('W1', 'b1', 'W2', 'b2', 'fusion_w', )}
    del _L0_gnn_all

    def _L1_gnn_setup():
        import jax, jax.numpy as jnp
        import numpy as np
        key = jax.random.key(seed)
        k1, k2, k3, k4 = jax.random.split(key, 4)
        B, N, F_in, F_out = (8, 2048, 256, 256)
        x = jax.random.normal(k1, (B, N, F_in), dtype=jnp.float32)
        adj = jax.random.uniform(k2, (B, N, N), dtype=jnp.float32)
        stdv = 1.0 / np.sqrt(F_out)
        weight = jax.random.uniform(k3, (F_in, F_out), dtype=jnp.float32, minval=-stdv, maxval=stdv)
        bias = jax.random.uniform(k4, (F_out,), dtype=jnp.float32, minval=-stdv, maxval=stdv)
        return {'x': x, 'adj': adj, 'weight': weight, 'bias': bias}
    _L1_gnn_all = _L1_gnn_setup()
    _L1_gnn_in = {k: v for k, v in _L1_gnn_all.items() if k in ('weight', 'bias', )}
    del _L1_gnn_all

    def _L2_gnn_setup():
        import jax, jax.numpy as jnp
        import numpy as np
        B, N, F_IN, F_OUT = (32, 1024, 256, 256)
        EPS = 1e-08
        key = jax.random.key(seed)
        k1, k2, k3 = jax.random.split(key, 3)
        x = jax.random.normal(k1, (B, N, F_IN), dtype=jnp.float32)
        adj = jax.random.uniform(k2, (B, N, N), dtype=jnp.float32)
        fan_in, fan_out = (2 * F_IN, F_OUT)
        limit = float(np.sqrt(6.0 / (fan_in + fan_out)))
        weight = jax.random.uniform(k3, (2 * F_IN, F_OUT), minval=-limit, maxval=limit, dtype=jnp.float32)
        bias = jnp.zeros((F_OUT,), dtype=jnp.float32)
        return {'x': x, 'adj': adj, 'weight': weight, 'bias': bias}
    _L2_gnn_all = _L2_gnn_setup()
    _L2_gnn_in = {k: v for k, v in _L2_gnn_all.items() if k in ('weight', 'bias', )}
    del _L2_gnn_all

    def _L3_gnn_setup():
        import jax, jax.numpy as jnp
        import numpy as np
        B, N, D, H = (8, 2048, 256, 1024)
        RMS_EPS = 1e-06

        def _rmsnorm(h, w, eps=RMS_EPS):
            var = jnp.mean(jnp.square(h), axis=-1, keepdims=True)
            return h * jax.lax.rsqrt(var + eps) * w
        key = jax.random.key(seed)
        ks = jax.random.split(key, 5)
        x = jax.random.normal(ks[0], (B, N, D), dtype=jnp.float32)
        adjacency = jax.random.uniform(ks[1], (B, N, N), dtype=jnp.float32)
        epsilon = jnp.zeros((), dtype=jnp.float32)
        W1 = jax.random.normal(ks[2], (D, H), dtype=jnp.float32) * (1.0 / np.sqrt(D))
        b1 = jnp.zeros((H,), dtype=jnp.float32)
        rms_weight = jnp.ones((H,), dtype=jnp.float32)
        W2 = jax.random.normal(ks[3], (H, D), dtype=jnp.float32) * (1.0 / np.sqrt(H))
        b2 = jnp.zeros((D,), dtype=jnp.float32)
        return {'x': x, 'adjacency': adjacency, 'epsilon': epsilon, 'W1': W1, 'b1': b1, 'rms_weight': rms_weight, 'W2': W2, 'b2': b2}
    _L3_gnn_all = _L3_gnn_setup()
    _L3_gnn_in = {k: v for k, v in _L3_gnn_all.items() if k in ('epsilon', 'W1', 'b1', 'rms_weight', 'W2', 'b2', )}
    del _L3_gnn_all

    return {
        "x": x,
        "adj": adj,
        "L0_gnn_W1": _L0_gnn_in["W1"],
        "L0_gnn_b1": _L0_gnn_in["b1"],
        "L0_gnn_W2": _L0_gnn_in["W2"],
        "L0_gnn_b2": _L0_gnn_in["b2"],
        "L0_gnn_fusion_w": _L0_gnn_in["fusion_w"],
        "L1_gnn_weight": _L1_gnn_in["weight"],
        "L1_gnn_bias": _L1_gnn_in["bias"],
        "L2_gnn_weight": _L2_gnn_in["weight"],
        "L2_gnn_bias": _L2_gnn_in["bias"],
        "L3_gnn_epsilon": _L3_gnn_in["epsilon"],
        "L3_gnn_W1": _L3_gnn_in["W1"],
        "L3_gnn_b1": _L3_gnn_in["b1"],
        "L3_gnn_rms_weight": _L3_gnn_in["rms_weight"],
        "L3_gnn_W2": _L3_gnn_in["W2"],
        "L3_gnn_b2": _L3_gnn_in["b2"],
    }

def reference(x, adj, L0_gnn_W1, L0_gnn_b1, L0_gnn_W2, L0_gnn_b2, L0_gnn_fusion_w, L1_gnn_weight, L1_gnn_bias, L2_gnn_weight, L2_gnn_bias, L3_gnn_epsilon, L3_gnn_W1, L3_gnn_b1, L3_gnn_rms_weight, L3_gnn_W2, L3_gnn_b2):
    import jax
    import jax.numpy as jnp
    def _L0_gnn_ref(x, adj, W1, b1, W2, b2, fusion_w):
        import jax, jax.numpy as jnp
        import numpy as np
        GROUPS = [list(range(25)), [0, 1, 2, 3, 4, 5, 6, 7, 8], [0, 9, 10, 11, 12, 13, 14], [6, 7, 8, 12, 13, 14], [3, 4, 5, 9, 10, 11]]
        B, N, D_IN, D_HID = (8192, 25, 256, 512)

        def _graph_conv(x, adj, W, b):
            n = adj.shape[-1]
            A = adj + jnp.eye(n, dtype=adj.dtype)
            deg = jnp.sum(A, axis=-1)
            deg_safe = jnp.where(deg == 0, 1.0, deg)
            dinv = jnp.where(deg == 0, 0.0, deg_safe ** (-0.5))
            norm_adj = dinv[:, :, None] * A * dinv[:, None, :]
            support = jnp.einsum('bnd,de->bne', x, W)
            out = jnp.einsum('bnm,bme->bne', norm_adj, support) + b
            return jax.nn.relu(out)
        norm_w = jax.nn.softmax(fusion_w)
        fused = jnp.zeros_like(x)
        for g, idx_list in enumerate(GROUPS):
            idx = jnp.asarray(idx_list)
            x_g = x[:, idx, :]
            adj_g = adj[:, idx][:, :, idx]
            h = _graph_conv(x_g, adj_g, W1[g], b1[g])
            out_g = _graph_conv(h, adj_g, W2[g], b2[g])
            fused = fused.at[:, idx, :].add(norm_w[g] * out_g)
        return fused

    def _L1_gnn_ref(x, adj, weight, bias):
        import jax, jax.numpy as jnp
        import numpy as np
        support = jnp.einsum('bni,io->bno', x, weight)
        out = jnp.einsum('bnm,bmo->bno', adj, support)
        return out + bias

    def _L2_gnn_ref(x, adj, weight, bias):
        import jax, jax.numpy as jnp
        import numpy as np
        B, N, F_IN, F_OUT = (32, 1024, 256, 256)
        EPS = 1e-08
        adj_norm = adj / (jnp.sum(adj, axis=-1, keepdims=True) + EPS)
        h_neigh = jnp.einsum('bnm,bmf->bnf', adj_norm, x)
        h_concat = jnp.concatenate([x, h_neigh], axis=-1)
        h = jnp.einsum('bnk,ko->bno', h_concat, weight) + bias
        return jax.nn.relu(h)

    def _L3_gnn_ref(x, adjacency, epsilon, W1, b1, rms_weight, W2, b2):
        import jax, jax.numpy as jnp
        import numpy as np
        B, N, D, H = (8, 2048, 256, 1024)
        RMS_EPS = 1e-06

        def _rmsnorm(h, w, eps=RMS_EPS):
            var = jnp.mean(jnp.square(h), axis=-1, keepdims=True)
            return h * jax.lax.rsqrt(var + eps) * w
        neighbor_sum = jnp.einsum('bnm,bmd->bnd', adjacency, x)
        agg = epsilon * x + neighbor_sum
        h = jnp.einsum('bnd,dh->bnh', agg, W1) + b1
        h = jax.nn.silu(_rmsnorm(h, rms_weight))
        out = jnp.einsum('bnh,hd->bnd', h, W2) + b2
        return out

    h = jnp.maximum(_layernorm(x, axis=-1), 0.0)
    x = x + _L0_gnn_ref(h, adj, L0_gnn_W1, L0_gnn_b1, L0_gnn_W2, L0_gnn_b2, L0_gnn_fusion_w)
    h = jnp.maximum(_layernorm(x, axis=-1), 0.0)
    x = x + _L1_gnn_ref(h, adj, L1_gnn_weight, L1_gnn_bias)
    h = jnp.maximum(_layernorm(x, axis=-1), 0.0)
    x = x + _L2_gnn_ref(h, adj, L2_gnn_weight, L2_gnn_bias)
    h = jnp.maximum(_layernorm(x, axis=-1), 0.0)
    x = x + _L3_gnn_ref(h, adj, L3_gnn_epsilon, L3_gnn_W1, L3_gnn_b1, L3_gnn_rms_weight, L3_gnn_W2, L3_gnn_b2)
    return x


_drawn_inputs = setup_inputs


def setup_inputs(seed=0):
    import zlib

    import numpy as np

    out = dict(_drawn_inputs(seed))
    spreads = {'L0_gnn_b1': (0.0, 0.8),
     'L0_gnn_b2': (0.0, 0.8),
     'L0_gnn_fusion_w': (1.0, 0.6),
     'L2_gnn_bias': (0.0, 0.49),
     'L3_gnn_b1': (0.0, 0.8),
     'L3_gnn_rms_weight': (1.0, 0.2),
     'L3_gnn_b2': (0.0, 0.346)}
    factors = {'L0_gnn_W1': 8.0, 'L0_gnn_W2': 8.0, 'L1_gnn_bias': 7.111}
    for name, (base, spread) in spreads.items():
        noise = np.random.default_rng([zlib.crc32(name.encode()), seed]).standard_normal(out[name].shape)
        drawn = base * np.exp(spread * noise) if base else spread * noise
        out[name] = jnp.asarray(drawn.astype(out[name].dtype))
    for name, factor in factors.items():
        out[name] = (out[name] * factor).astype(out[name].dtype)
    return out
```

```python
import numpy as np
import concourse.bass as bass
from concourse import mybir
from contextlib import ExitStack

GROUPS = [list(range(25)), [0, 1, 2, 3, 4, 5, 6, 7, 8], [0, 9, 10, 11, 12, 13, 14], [6, 7, 8, 12, 13, 14],
          [3, 4, 5, 9, 10, 11]]
SPACES = [(25, 4, [0]), (15, 8, [1, 2, 3, 4])]


def shape_constants():
    consts = {"identity": np.eye(128, dtype=np.float32)}
    for s, (nodes, per_tile, groups) in enumerate(SPACES):
        rows = nodes * per_tile
        pair = np.zeros((rows, len(groups), rows), np.float32)
        member = np.zeros((rows, len(groups)), np.float32)
        for n, g in enumerate(groups):
            for q in range(per_tile):
                at = [q * nodes + v for v in GROUPS[g]]
                pair[np.ix_(at, [n], at)] = 1.0
                member[at, n] = 1.0
        consts[f"pair_mask_{s}"] = pair
        consts[f"member_mask_{s}"] = member
    return consts


def gnn_stack(nc, t_in, out, scratch):
    f32, f32r = mybir.dt.float32, mybir.dt.float32r
    ALU, ACT, AX = mybir.AluOpType, mybir.ActivationFunctionType, mybir.AxisListType
    x_d, adj_d = t_in["x"], t_in["adj"]
    B, N, D = x_d.shape
    H = t_in["L3_gnn_W1"].shape[1]
    H0 = t_in["L0_gnn_W1"].shape[2]
    P = 128
    NT = N // P
    ND = D // P
    NH = H // P
    HALF = N // 2
    TH = NT // 2
    CH = 2 * P
    NC = N // CH
    LN_EPS, DEG_EPS, RMS_EPS = 1e-5, 1e-8, 1e-6
    F0 = SPACES[0][0]

    ctx = ExitStack()
    with ctx:
        def sb(name, shape, dt=f32, scope=ctx):
            return scope.enter_context(nc.sbuf_tensor(name, shape, dt))

        def sem(name):
            return ctx.enter_context(nc.semaphore(name))

        wa_hi, wa_lo = sb("wa_hi", [P, ND, D], f32r), sb("wa_lo", [P, ND, D], f32r)
        wb_hi, wb_lo = sb("wb_hi", [P, 2 * ND, D], f32r), sb("wb_lo", [P, 2 * ND, D], f32r)
        w1_hi, w1_lo = sb("w1_hi", [P, ND, H], f32r), sb("w1_lo", [P, ND, H], f32r)
        w2_hi, w2_lo = sb("w2_hi", [P, NH, D], f32r), sb("w2_lo", [P, NH, D], f32r)
        ident = sb("ident", [P, P])
        eps_ident = sb("eps_ident", [P, P])
        ones = sb("ones", [P, P])
        bias1, bias2, bias3 = (sb(n, [P, D]) for n in ("bias1", "bias2", "bias3"))
        b1_col, rmsw_col = sb("b1_col", [P, NH]), sb("rmsw_col", [P, NH])
        minus_half = sb("minus_half", [P, 8])
        epsilon_col = sb("epsilon_col", [P, 1])

        ps = ctx.enter_context(nc.psum_tensor("ps", [P, 8, 512], f32))
        AGG, RING, HID, DOWN = (0, 1, 2), (3, 4), (5, 6), 7

        early = ExitStack()
        stage_a, stage_b = sb("stage_a", [P, ND, D], scope=early), sb("stage_b", [P, 2 * ND, D], scope=early)
        stage_1, stage_2 = sb("stage_1", [P, ND, H], scope=early), sb("stage_2", [P, NH, D], scope=early)
        NG, NK0 = len(GROUPS), H0 // P
        v_w1 = sb("v_w1", [P, 2, ND, H0], scope=early)
        v_w2 = sb("v_w2", [P, 2, NK0, D], scope=early)
        v_b1 = sb("v_b1", [P, NG, NK0], scope=early)
        v_b2 = sb("v_b2", [P, NG, D], scope=early)
        v_fw = sb("v_fw", [P, 4, NG], scope=early)
        v_red = sb("v_red", [P, 4], scope=early)
        V = []
        for s, (nodes, per_tile, groups) in enumerate(SPACES):
            rows, tiles, ng = nodes * per_tile, B // per_tile, len(groups)
            V.append(dict(
                rows=rows, tiles=tiles, ng=ng, nodes=nodes, per_tile=per_tile, groups=groups,
                x=sb(f"v_x{s}", [rows, tiles, D], scope=early), acc=sb(f"v_acc{s}", [rows, tiles, D], scope=early),
                h=sb(f"v_h{s}", [rows, tiles, D], scope=early),
                adj=sb(f"v_adj{s}", [rows, tiles, rows], scope=early),
                mask=sb(f"v_mask{s}", [rows, ng, rows], scope=early), member=sb(f"v_member{s}", [rows, ng], scope=early),
                ag=sb(f"v_ag{s}", [rows, ng, tiles, rows], scope=early),
                an_t=sb(f"v_an_t{s}", [rows, ng, tiles, rows], scope=early),
                deg=sb(f"v_deg{s}", [rows, 4, ng * tiles], scope=early),
                st=sb(f"v_st{s}", [rows, tiles, 6], scope=early), mv=sb(f"v_mv{s}", [rows, tiles, 2], scope=early),
                rs=sb(f"v_rs{s}", [rows, 2, tiles], scope=early), wm=sb(f"v_wm{s}", [rows, ng], scope=early)))
        VR = max(v["rows"] for v in V)
        VC = max(v["rows"] * v["tiles"] for v in V)
        VT = max(v["tiles"] for v in V)
        v_yt = sb("v_yt", [P, ND, VC], scope=early)
        v_hid = sb("v_hid", [P, NK0, VC], scope=early)
        v_s2 = sb("v_s2", [VR, VT, D], scope=early)
        v_u = sb("v_u", [VR, 2, D], scope=early)
        early.close()

        adj_hi, adj_lo = sb("adj_hi", [P, NT, N], f32r), sb("adj_lo", [P, NT, N], f32r)
        raw = sb("raw", [P, 2, N])
        x = sb("x_rows", [P, NT, D])
        tail = sb("tail", [P, NT, D])
        h_hi, h_lo = sb("h_hi", [P, NT, D], f32r), sb("h_lo", [P, NT, D], f32r)
        y = sb("y", [P, TH, D])
        pt_hi, pt_lo = sb("pt_hi", [P, ND, HALF], f32r), sb("pt_lo", [P, ND, HALF], f32r)
        ht_hi, ht_lo = sb("ht_hi", [P, ND, HALF], f32r), sb("ht_lo", [P, ND, HALF], f32r)
        agg = sb("agg", [P, ND, N])
        ac_hi, ac_lo = sb("ac_hi", [P, ND, CH], f32r), sb("ac_lo", [P, ND, CH], f32r)
        hid = sb("hid", [P, NH, CH])
        sq_sum, sq = sb("sq_sum", [P, 2, CH]), sb("sq", [P, 2, CH])
        act_hi, act_lo = sb("act_hi", [P, 2, 2, CH], f32r), sb("act_lo", [P, 2, 2, CH], f32r)
        rdiag = sb("rdiag", [P, CH])
        fixed = sb("fixed", [P, P])
        st, mv = sb("st", [P, NT, 6]), sb("mv", [P, NT, 2])
        ve, rstd = sb("ve", [P, TH]), sb("rstd", [P, TH])
        deg, inv_deg = sb("deg", [P, 2, NT]), sb("inv_deg", [P, NT])
        msq, rms = sb("msq", [P, 2]), sb("rms", [P, 2])

        def f(view):
            return view.bitcast(f32)

        w_in, w_hi_ok, w_ok = sem("w_in"), sem("w_hi_ok"), sem("w_ok")
        const_in, vectors_in, const_ok = sem("const_in"), sem("vectors_in"), sem("const_ok")
        v_x_in, v_adj_zero, v_adj_in = sem("v_x_in"), sem("v_adj_zero"), sem("v_adj_in")
        v_w_in = [sem("v_w_in0"), sem("v_w_in1")]
        v_dve, v_pool, v_act = sem("v_dve"), sem("v_pool"), sem("v_act")
        v_fw_sub, v_fw_exp = sem("v_fw_sub"), sem("v_fw_exp")
        v_deg_pow, v_deg_safe, v_var_ok, v_rstd = sem("v_deg_pow"), sem("v_deg_safe"), sem("v_var_ok"), sem("v_rstd")
        v_ag_ok, v_tr, v_ant = sem("v_ag_ok"), sem("v_tr"), sem("v_ant")
        v_h_ok, v_y_mm, v_y_ok = sem("v_h_ok"), sem("v_y_mm"), sem("v_y_ok")
        v_hid_mm, v_hid_ok = sem("v_hid_mm"), sem("v_hid_ok")
        v_ring_mm, v_ring_free = sem("v_ring_mm"), sem("v_ring_free")
        v_acc_in, v_stored, v_done = sem("v_acc_in"), sem("v_stored"), sem("v_done")

        x_in = sem("x_in")
        adj_in = [sem("adj_in0"), sem("adj_in1")]
        tr_mm, adj_hi_ok = sem("tr_mm"), sem("adj_hi_ok")
        ring_free = sem("ring_free")
        rowsum_ok = sem("rowsum_ok")
        deg_ok, inv_ok = sem("deg_ok"), sem("inv_ok")
        bn_ok, stats_ok = sem("bn_ok"), sem("stats_ok")
        ve_ok, rstd_ok = sem("ve_ok"), sem("rstd_ok")
        y_ok, h_hi_ok, h_ok = sem("y_ok"), sem("h_hi_ok"), sem("h_ok")
        hs_ok = sem("hs_ok")
        agg_mm = sem("agg_mm")
        pt_hi_ok, pt_ok = sem("pt_hi_ok"), sem("pt_ok")
        agg_ok = sem("agg_ok")
        ht_mm, ht_hi_ok = sem("ht_mm"), sem("ht_hi_ok")
        w_mm = sem("w_mm")
        relu_ok = sem("relu_ok")
        xb_ok, tail_ok = sem("xb_ok"), sem("tail_ok")
        fix_ok = sem("fix_ok")
        ac_hi_ok, ac_ok = sem("ac_hi_ok"), sem("ac_ok")
        up_mm, hid_ok, sq_ok = sem("up_mm"), sem("hid_ok"), sem("sq_ok")
        sum_ok = sem("sum_ok")
        col_mm, msq_ok, rms_ok, rdiag_ok, bcast_mm = (sem(n) for n in ("col_mm", "msq_ok", "rms_ok", "rdiag_ok", "bcast_mm"))
        scaled_ok = sem("scaled_ok")
        silu_ok, act_hi_ok, act_ok, down_mm = (sem(n) for n in ("silu_ok", "act_hi_ok", "act_ok", "down_mm"))
        res_ok, stored = sem("res_ok"), sem("stored")

        waits_apart = {e.engine: sem(f"waits_apart_{n}") for n, e in (("sp", nc.sync), ("dve", nc.vector), ("pool", nc.gpsimd))}

        X_DMAS = 3
        RING_USES = 28
        PAIRS = NH // 2

        def upto(graph, per_graph, n):
            return graph * per_graph + n

        def ring_use(graph, n):
            return graph * RING_USES + 8 + n

        ring_of = {("w", 1, 0): 8, ("w", 1, 1): 10, ("ht", 2, 0): 12, ("w", 2, 0): 14, ("ht", 2, 1): 16,
                   ("w", 2, 1): 18}

        def tr_use(graph, tile, g):
            return ring_use(graph, 2 * tile + g - 8)

        COST = {"agg2": 1.3, "agg1": 0.65, "tr": 0.45, "w1": 1.3, "w2": 2.6, "ht": 0.45}

        def mlp_steps(chunk, part):
            up = [(0.6, ("chunk_split", chunk))] + [(1.4, ("up", chunk, p)) for p in range(PAIRS)]
            down = [(2.6, ("sumsq", chunk)), (3.2, ("bcast", chunk)), (1.3, ("scale", chunk))]
            for p in range(PAIRS + 2):
                if p < PAIRS:
                    down.append((1.0 if p else 0.6, ("act", chunk, p)))
                if p >= 2:
                    down.append((0.5, ("down", chunk, p - 2)))
            down.append((0.2, ("result", chunk)))
            return {"up": up, "down": down, "all": up + down}[part]

        def front_steps(nxt):
            o = []
            for L in (1, 2, 3):
                last = L == 3
                o += [("split", L, 0), ("split", L, 1)]
                if L > 1:
                    o += [("w", L - 1, 1, 0), ("w", L - 1, 1, 1)]
                    o += [("stats", L, t) for t in range(TH, NT)] if L == 1 else []
                    o += [("rstd", L, 1)]
                for m in range(NT):
                    if m + 2 < TH:
                        o.append(("split", L, m + 2))
                    if L == 2 and m == 1:
                        o += [("hs", 0), ("ht", 0)]
                    if m == 2:
                        o += [("norm", L, t) for t in range(TH, NT)]
                        o += [("split", L, TH)]
                    if TH - 1 <= m < NT - 2:
                        o.append(("split", L, m + 2))
                    if m == NT - 2:
                        pass
                    if last and m % 2 == 0:
                        o.append(("fix", m))
                        o.append(("fix", m + 1))
                    o.append(("agg2", L, m))
                    if L == 1:
                        o.append(("tr", 0, TH + m // 2, m % 2))
                o.append(("pt", L, 0, 0))
                o.append(("pt", L, 0, 1))
                if L == 1:
                    o += [("deg",)]
                    o += [("xb", t) for t in range(NT)]
                if L == 2:
                    o += [("hs", 1)]
                if last:
                    o += [("tail", t) for t in range(NT)] + [("load_x",)] * nxt
                for m in range(NT):
                    o.append(("agg1", L, 0, m))
                    if last and nxt:
                        o.append(("tr", 1, m // 4, (m // 2) % 2)) if m % 2 == 0 else None
                    if not last and m == 4:
                        o += [("w", L, 0, 0), ("w", L, 0, 1)]
                        if L == 2:
                            o += [("ht", 1)]
                        o += [("rstd", L + 1, 0)] + [("norm", L + 1, t) for t in range(TH)]
                o.append(("pt", L, 1, 0))
                for m in range(NT):
                    o.append(("agg1", L, 1, m))
                    if last and nxt and m % 2 == 0:
                        o.append(("tr", 1, 2 + m // 4, (m // 2) % 2))
                o.append(("pt", L, 1, 1))
                if last and nxt:
                    o += [("stats", 1, t) for t in range(NT)]
                    o += [("rstd", 1, 0)] + [("norm", 1, t) for t in range(TH)] + [("rstd", 1, 1)]
            return o

        def body_steps(with_tail, nxt):
            others = []
            if with_tail:
                others = mlp_steps(0, "down")
                for c in range(1, NC):
                    others += mlp_steps(c, "all")
            merged, gap = [], 0.0
            for step in front_steps(nxt):
                if step[0] == "tail" and step[1] == 0:
                    merged += [(s, 1) for _, s in others]
                    others = []
                merged.append((step, 0))
                gap += COST.get(step[0] if step[0] != "w" else f"w{step[1]}", 0.0)
                while others and gap >= others[0][0]:
                    gap -= others[0][0]
                    merged.append((others.pop(0)[1], 1))
            assert not others
            return merged + [(s, 0) for _, s in mlp_steps(0, "up")]

        def epilogue_steps():
            others = mlp_steps(0, "down")
            for c in range(1, NC):
                others += mlp_steps(c, "all")
            return [(s, 1) for _, s in others]

        def prologue_steps():
            return [("load_x",)] + [("tr", 1, t, g) for t in range(TH) for g in range(2)] + \
                [("stats", 1, t) for t in range(NT)] + \
                [("rstd", 1, 0)] + [("norm", 1, t) for t in range(TH)] + [("rstd", 1, 1)]

        def run(engine, do):
            for step in prologue_steps():
                do(step, -1, None, True)
            for step, age in body_steps(False, True):
                do(step, 0, 0 - age, True)
            if B > 3:
                with engine.Fori(1, B - 1) as i:
                    for step, age in body_steps(True, True):
                        do(step, i, i - age, False)
            else:
                for i in range(1, B - 1):
                    for step, age in body_steps(True, True):
                        do(step, i, i - age, False)
            for step, age in body_steps(True, False):
                do(step, B - 1, B - 1 - age, False)
            for step, age in epilogue_steps():
                do(step, B, B - age, False)

        def wait_apart(engine, semaphore, value):
            engine.wait_ge(semaphore, value)
            engine.sem_inc(waits_apart[engine.engine], 1)

        def bank(n, width=512):
            return ps[:, n, 0:width]

        def agg_group(L, c, d):
            return 4 * (L - 1) + 2 * c + d

        block = ctx.enter_context(nc.Block())

        @block.sync
        def _(sp):
            for s, v in enumerate(V):
                for g in range(B):
                    t, q = divmod(g, v["per_tile"])
                    at = slice(q * v["nodes"], (q + 1) * v["nodes"])
                    sp.dma_start(v["x"][at, t, :], x_d[g, 0:v["nodes"], :]).then_inc(v_x_in, 16)
            sp.dma_start(ident[:, :], t_in["identity"]).then_inc(const_in, 16)
            for s, v in enumerate(V):
                sp.dma_start(v["mask"][:, :, :], t_in[f"pair_mask_{s}"]).then_inc(const_in, 16)
                sp.dma_start(v["member"][:, :], t_in[f"member_mask_{s}"]).then_inc(const_in, 16)
            sp.wait_ge(v_adj_zero, len(V))
            for s, v in enumerate(V):
                for g in range(B):
                    t, q = divmod(g, v["per_tile"])
                    at = slice(q * v["nodes"], (q + 1) * v["nodes"])
                    sp.dma_start(v["adj"][at, t, at], adj_d[g, 0:v["nodes"], 0:v["nodes"]]).then_inc(v_adj_in, 16)

            def load_group(n):
                sp.dma_start(v_w1[:, n % 2], t_in["L0_gnn_W1"][n].rearrange("(d p) e -> p d e", p=P)).then_inc(v_w_in[n % 2], 16)
                sp.dma_start(v_w2[:, n % 2], t_in["L0_gnn_W2"][n].rearrange("(k p) e -> p k e", p=P)).then_inc(v_w_in[n % 2], 16)

            load_group(0)
            load_group(1)
            for tile_, name in ((stage_a, "L1_gnn_weight"), (stage_b, "L2_gnn_weight"), (stage_1, "L3_gnn_W1"),
                                (stage_2, "L3_gnn_W2")):
                sp.dma_start(tile_[:, :, :], t_in[name].rearrange("(d p) e -> p d e", p=P)).then_inc(w_in, 16)
            group_at = 0
            for s, v in enumerate(V):
                for n in range(v["ng"]):
                    group_at += 1
                    if group_at + 1 < NG:
                        sp.wait_ge(v_done, group_at)
                        load_group(group_at + 1)
                sp.wait_ge(v_done, group_at)
                for g in range(B):
                    t, q = divmod(g, v["per_tile"])
                    at = slice(q * v["nodes"], (q + 1) * v["nodes"])
                    sp.dma_start(scratch[g, 0:v["nodes"], :], v["acc"][at, t, :]).then_inc(v_stored, 16)
                if s + 1 < len(V):
                    w = V[s + 1]
                    sp.wait_ge(v_stored, 16 * B * (s + 1))
                    for g in range(B):
                        t, q = divmod(g, w["per_tile"])
                        at = slice(q * w["nodes"], (q + 1) * w["nodes"])
                        sp.dma_start(w["acc"][at, t, :], scratch[g, 0:w["nodes"], :]).then_inc(v_acc_in, 16)
            sp.wait_ge(v_stored, 16 * B * len(V))
            sp.wait_ge(w_ok, 4)

            def load_adj(graph, tile, first):
                s = tile % 2
                if not first:
                    before = graph * 2 * NT + 2 * (tile - 2) + 2
                    wait_apart(sp, tr_mm, before)
                    wait_apart(sp, rowsum_ok, graph * NT + tile - 1)
                sp.dma_start(raw[:, s, :], adj_d[graph, tile * P:(tile + 1) * P, :] if isinstance(graph, int)
                             else adj_d[bass.ds(graph, 1), tile * P:(tile + 1) * P, :].rearrange("a p n -> (a p) n")
                             ).then_inc(adj_in[s], 16)

            def rows(tensor, graph, lo, hi):
                if isinstance(graph, int):
                    return tensor[graph, lo:hi, :]
                return tensor[bass.ds(graph, 1), lo:hi, :].rearrange("a p n -> (a p) n")

            def do(step, i, j, first):
                kind = step[0]
                nxt = i + 1
                if kind == "load_x":
                    if not (first and isinstance(i, int) and i < 0):
                        wait_apart(sp, tail_ok, upto(i, NT, NT))
                    sp.dma_start(x[0:F0, 0, :], rows(scratch, nxt, 0, F0)).then_inc(x_in, 16)
                    sp.dma_start(x[F0:P, 0, :], rows(x_d, nxt, F0, P)).then_inc(x_in, 16)
                    sp.dma_start(x[:, 1:NT, :], rows(x_d, nxt, P, N).rearrange("(t p) d -> p t d", p=P)).then_inc(x_in, 16)
                elif kind == "tr":
                    _, ahead, tile, g = step
                    if g == 1:
                        graph = i + ahead
                        if isinstance(i, int) and i == -1 and tile < 1:
                            load_adj(0, 0, True)
                            load_adj(0, 1, True)
                        if tile + 2 < NT:
                            load_adj(graph, tile + 2, False)
                        elif isinstance(graph, int) and graph == B - 1:
                            pass
                        else:
                            load_adj(graph + 1, tile + 2 - NT, False)
                elif kind == "result":
                    c = step[1]
                    wait_apart(sp, res_ok, upto(j, NC, c + 1))
                    sp.dma_start(rows(out, j, c * CH, (c + 1) * CH).rearrange("(t p) d -> p t d", p=P),
                                 tail[:, 2 * c:2 * c + 2, :]).then_inc(stored, 16)

            run(sp, do)
            sp.wait_ge(stored, 16 * NC * B)

        @block.gpsimd
        def _(pool):
            for v in V:
                nc.gpsimd.memset(v["adj"][:, :, :], 0.0).then_inc(v_adj_zero, 1)
            nc.gpsimd.memset(ones[:, :], 1.0).then_inc(const_ok, 1)
            nc.gpsimd.memset(minus_half[:, :], -0.5).then_inc(const_ok, 1)
            with nc.allow_non_contiguous_dma(reason="small vectors, once"):
                for col, src in ((b1_col, "L3_gnn_b1"), (rmsw_col, "L3_gnn_rms_weight")):
                    pool.dma_start(col[:, :], t_in[src].rearrange("(k p) -> p k", p=P)).then_inc(vectors_in, 16)
                pool.dma_start(v_b1[:, :, :], t_in["L0_gnn_b1"].rearrange("g (k p) -> p g k", p=P)).then_inc(vectors_in, 16)
                for row, src in ((bias1, "L1_gnn_bias"), (bias2, "L2_gnn_bias"), (bias3, "L3_gnn_b2")):
                    pool.dma_start(row[:, :], t_in[src].rearrange("(a n) -> a n", a=1).broadcast_to([P, D])).then_inc(vectors_in, 16)
                pool.dma_start(v_b2[:, :, :].rearrange("p g n -> p (g n)"),
                               t_in["L0_gnn_b2"].rearrange("(a g) n -> a (g n)", a=1).broadcast_to([P, NG * D])).then_inc(vectors_in, 16)
                pool.dma_start(v_fw[:, 0, :], t_in["L0_gnn_fusion_w"].rearrange("(a n) -> a n", a=1).broadcast_to([P, NG])).then_inc(vectors_in, 16)
                pool.dma_start(epsilon_col[:, :], t_in["L3_gnn_epsilon"].rearrange("(a n) -> a n", a=1).broadcast_to([P, 1])).then_inc(vectors_in, 16)
            pool.wait_ge(const_ok, 2)
            for s, v in enumerate(V):
                r, n = v["rows"], v["ng"] * v["tiles"]
                pool.wait_ge(v_var_ok, s + 1)
                for t in range(v["tiles"]):
                    last = nc.gpsimd.tensor_tensor(v["rs"][:, 1, t:t + 1], v["rs"][:, 0, t:t + 1], minus_half[0:r, 0:1], ALU.pow)
                last.then_inc(v_rstd, 1)
                pool.wait_ge(v_deg_safe, s + 1)
                for k in range(0, n, 8):
                    m = min(8, n - k)
                    last = nc.gpsimd.tensor_tensor(v["deg"][:, 2, k:k + m], v["deg"][:, 1, k:k + m], minus_half[0:r, 0:m], ALU.pow)
                last.then_inc(v_deg_pow, 1)
            pool.wait_ge(v_stored, 16 * B * len(V))
            pool.wait_ge(w_ok, 4)

            def do(step, i, j, first):
                kind = step[0]
                pro = isinstance(i, int) and i < 0
                if kind == "rstd":
                    _, L, half = step
                    b = i + 1 if L == 1 else i
                    wait_apart(pool, stats_ok, upto(b, 3 * NT, (L - 1) * NT + (half + 1) * TH))
                    k = 2 * (L - 1) + half
                    nc.gpsimd.tensor_scalar(ve[:, :], mv[:, half * TH:(half + 1) * TH, 1], LN_EPS, None, ALU.add).then_inc(ve_ok, 1)
                    pool.wait_ge(ve_ok, upto(b, 6, k + 1))
                    if not (pro and half == 0):
                        pool.wait_ge(y_ok, upto(b, 3 * NT, (L - 1) * NT + half * TH))
                    nc.gpsimd.tensor_tensor(rstd[:, :], ve[:, :], minus_half[:, 0:TH], ALU.pow).then_inc(rstd_ok, 1)
                elif kind == "norm":
                    _, L, t = step
                    half = t // TH
                    b = i + 1 if (L == 1 and half == 0) else i
                    n = (L - 1) * NT + t
                    if t % TH == 0:
                        wait_apart(pool, rstd_ok, upto(b, 6, 2 * (L - 1) + half + 1))
                        if L == 3 and half == 0 or L == 2 and half == 1:
                            wait_apart(pool, ht_mm, upto(b, 4, 4 if L == 3 else 2))
                    if not (pro and n < TH):
                        wait_apart(pool, h_ok, upto(b, 3 * NT, n - TH + 1))
                    nc.gpsimd.tensor_scalar(y[:, t % TH, :], x[:, t, :], mv[:, t, 0:1], rstd[:, t % TH:t % TH + 1],
                                            ALU.subtract, ALU.mult).then_inc(y_ok, 1)
                elif kind == "hs":
                    half = step[1]
                    if half == 0:
                        pool.wait_ge(deg_ok, upto(i, 1, 1))
                    for t in range(half * TH, (half + 1) * TH):
                        wait_apart(pool, h_ok, upto(i, 3 * NT, NT + t + 1))
                        nc.gpsimd.tensor_scalar(y[:, t % TH, :], y[:, t % TH, :], 0.0, deg[:, 1, t:t + 1],
                                                ALU.max, ALU.mult).then_inc(hs_ok, 1)
                elif kind == "xb":
                    t = step[1]
                    pool.wait_ge(y_ok, upto(i, 3 * NT, t + 1))
                    nc.gpsimd.tensor_tensor(x[:, t, :], x[:, t, :], bias1[:, :], ALU.add).then_inc(xb_ok, 1)
                elif kind == "tail":
                    t = step[1]
                    if not first:
                        pool.wait_ge(stored, upto(i, 16 * NC, 0))
                    pool.wait_ge(y_ok, upto(i, 3 * NT, 2 * NT + t + 1))
                    nc.gpsimd.tensor_tensor(tail[:, t, :], x[:, t, :], bias3[:, :], ALU.add).then_inc(tail_ok, 1)
                elif kind == "up":
                    _, c, p = step
                    if p > 0:
                        n = upto(j, 3 * NC, 3 * c + p)
                        pool.wait_ge(sq_ok, upto(j, PAIRS * NC, PAIRS * c + p + 1))
                        if p > 1:
                            pool.wait_ge(sum_ok, n - 1)
                        nc.gpsimd.tensor_tensor(sq_sum[:, :, :], sq_sum[:, :, :], sq[:, :, :], ALU.add).then_inc(sum_ok, 1)
                elif kind == "bcast":
                    c = step[1]
                    pool.wait_ge(msq_ok, upto(j, NC, c + 1))
                    nc.gpsimd.tensor_tensor(rms[:, :], msq[:, :], minus_half[:, 0:2], ALU.pow).then_inc(rms_ok, 1)

            run(pool, do)

        @block.scalar
        def _(act):
            act.wait_ge(v_fw_sub, 1)
            nc.scalar.activation(v_fw[:, 1, :], v_fw[:, 0, :], ACT.Exp, bias=v_red[:, 1:2], accum_out=v_red[:, 2:3]).then_inc(v_fw_exp, 1)
            act.wait_ge(w_in, 64)
            for hi, st_ in ((wa_hi, stage_a), (wb_hi, stage_b), (w1_hi, stage_1), (w2_hi, stage_2)):
                nc.scalar.activation(hi[:, :, :], st_[:, :, :], ACT.Copy).then_inc(w_hi_ok, 1)
            done_tr = 0
            gidx = 0
            for s, v in enumerate(V):
                r, tiles = v["rows"], v["tiles"]
                for n in range(v["ng"] * tiles):
                    done_tr += 1
                    act.wait_ge(v_tr, done_tr)
                    g, t = divmod(n, tiles)
                    nc.scalar.activation(v["an_t"][:, g, t, :], ps[0:r, done_tr % 2, 0:r], ACT.Copy,
                                         scale=v["deg"][:, 3, n:n + 1]).then_inc(v_ant, 1)
                for n in range(v["ng"]):
                    g = v["groups"][n]
                    cols = r * tiles
                    for d in range(ND):
                        act.wait_ge(v_y_mm, ND * gidx + d + 1)
                        if gidx:
                            act.wait_ge(v_hid_mm, NK0 * gidx)
                        nc.scalar.activation(v_yt[:, d, 0:cols], ps[:, 2 + d, 0:cols], ACT.Copy).then_inc(v_y_ok, 1)
                    for k in range(NK0):
                        act.wait_ge(v_hid_mm, NK0 * gidx + k + 1)
                        if gidx:
                            act.wait_ge(v_done, gidx)
                        nc.scalar.activation(v_hid[:, k, 0:cols], ps[:, 4 + k % 2, 0:cols], ACT.Relu,
                                             bias=v_b1[:, g, k:k + 1]).then_inc(v_hid_ok, 1)
                    gidx += 1
            act.wait_ge(v_stored, 16 * B * len(V))
            act.wait_ge(w_ok, 4)

            def do(step, i, j, first):
                kind = step[0]
                pro = isinstance(i, int) and i < 0
                if kind == "tr":
                    _, ahead, tile, g = step
                    b = i + ahead
                    n = 2 * tile + g
                    act.wait_ge(tr_mm, upto(b, 2 * NT, n + 1))
                    if not pro and g == 0 and tile % TH == 0:
                        if ahead:
                            act.wait_ge(agg_mm, upto(i, 12, 10))
                        elif not first:
                            act.wait_ge(agg_mm, upto(i, 12, 0))
                    nc.scalar.activation(adj_hi[:, g * TH:(g + 1) * TH, tile * P:(tile + 1) * P],
                                         bank(RING[n % 2]).rearrange("p (a b) -> p a b", b=P), ACT.Copy).then_inc(adj_hi_ok, 1)
                elif kind == "split":
                    _, L, t = step
                    n = (L - 1) * NT + t
                    act.wait_ge(y_ok, upto(i, 3 * NT, n + 1))
                    if t == 0 and not (first and L == 1):
                        act.wait_ge(agg_mm, upto(i, 12, 4 * (L - 1)))
                    nc.scalar.activation(h_hi[:, t, :], y[:, t % TH, :], ACT.Relu).then_inc(h_hi_ok, 1)
                elif kind == "pt":
                    _, L, c, d = step
                    n = agg_group(L, c, d)
                    act.wait_ge(agg_mm, upto(i, 12, n + 1))
                    if L < 3:
                        if c == 1:
                            act.wait_ge(w_mm, upto(i, 8, 4 * (L - 1) + 2))
                        elif L == 2:
                            act.wait_ge(w_mm, upto(i, 8, 4))
                        elif not first:
                            act.wait_ge(w_mm, upto(i, 8, 0))
                        nc.scalar.activation(pt_hi[:, d, :], bank(AGG[n % 3]), ACT.Copy).then_inc(pt_hi_ok, 1)
                    else:
                        if not first and c == 0 and d == 0:
                            act.wait_ge(ac_ok, upto(i, NC, 0))
                        nc.scalar.activation(agg[:, d, c * HALF:(c + 1) * HALF], bank(AGG[n % 3]), ACT.Copy).then_inc(agg_ok, 1)
                elif kind == "ht":
                    c = step[1]
                    for d in range(ND):
                        act.wait_ge(ht_mm, upto(i, 4, 2 * c + d + 1))
                        if c == 1:
                            act.wait_ge(w_mm, upto(i, 8, 6))
                        elif not first:
                            act.wait_ge(w_mm, upto(i, 8, 0))
                        nc.scalar.activation(ht_hi[:, d, :], bank(RING[d]), ACT.Copy).then_inc(ht_hi_ok, 1)
                elif kind == "up":
                    _, c, p = step
                    n = PAIRS * c + p
                    act.wait_ge(up_mm, upto(j, PAIRS * NC, n + 1))
                    if not (isinstance(j, int) and j == 0 and c == 0):
                        act.wait_ge(act_ok, upto(j, PAIRS * NC, n - PAIRS + p * 0 + 1))
                    src = bank(HID[p % 2]).rearrange("p (a b) -> p a b", b=CH)
                    for q in range(2):
                        k = 2 * p + q
                        last = nc.scalar.activation(hid[:, k, :], src[:, q, :], ACT.Identity, bias=b1_col[:, k:k + 1])
                    last.then_inc(hid_ok, 1)
                    if p == 0:
                        if not (isinstance(j, int) and j == 0 and c == 0):
                            act.wait_ge(col_mm, upto(j, NC, c))
                    elif p > 1:
                        act.wait_ge(sum_ok, upto(j, 3 * NC, 3 * c + p - 1))
                    dst = sq if p else sq_sum
                    for q in range(2):
                        k = 2 * p + q
                        last = nc.scalar.activation(dst[:, q, :], src[:, q, :], ACT.Square, bias=b1_col[:, k:k + 1])
                    last.then_inc(sq_ok, 1)
                elif kind == "act":
                    _, c, p = step
                    act.wait_ge(scaled_ok, upto(j, 2 * NC, 2 * c + p // 2 + 1))
                    for q in range(2):
                        k = 2 * p + q
                        last = nc.scalar.activation(hid[:, k, :], hid[:, k, :], ACT.Silu, scale=rmsw_col[:, k:k + 1])
                    last.then_inc(silu_ok, 1)

            run(act, do)

        @block.vector
        def _(dve):
            vd = [0]

            def link(ins):
                vd[0] += 1
                ins.then_inc(v_dve, 1)
                dve.wait_ge(v_dve, vd[0])

            dve.wait_ge(const_in, 16 * (1 + 2 * len(V)))
            dve.wait_ge(vectors_in, 16 * 9)
            nc.vector.reduce_max(v_red[:, 0:1], v_fw[:, 0, :], axis=AX.X)
            link(nc.vector.tensor_scalar(eps_ident[:, :], ident[:, :], epsilon_col[:, 0:1], None, ALU.mult))
            nc.vector.tensor_scalar(v_red[:, 1:2], v_red[:, 0:1], -1.0, None, ALU.mult).then_inc(v_fw_sub, 1)
            dve.wait_ge(v_x_in, 16 * B * len(V))
            for s, v in enumerate(V):
                for t in range(v["tiles"]):
                    last = nc.vector.bn_stats(v["st"][:, t, :], v["x"][:, t, :])
                link(last)
                for t in range(v["tiles"]):
                    last = nc.vector.bn_aggr(v["mv"][:, t, :], v["st"][:, t, :])
                link(last)
                nc.vector.tensor_scalar(v["rs"][:, 0, :], v["mv"][:, :, 1], LN_EPS, None, ALU.add).then_inc(v_var_ok, 1)
            dve.wait_ge(v_adj_in, 16 * B * len(V))
            for s, v in enumerate(V):
                r, tiles, ng = v["rows"], v["tiles"], v["ng"]
                adj0, ag, dg = v["adj"], v["ag"], v["deg"]
                link(nc.vector.tensor_tensor(adj0[:, :, :], adj0[:, :, :], ident[0:r, 0:r].unsqueeze(1).broadcast_to([r, tiles, r]), ALU.add))
                for n in range(ng):
                    last = nc.vector.tensor_tensor(ag[:, n, :, :], adj0[:, :, :], v["mask"][:, n, :].unsqueeze(1).broadcast_to([r, tiles, r]), ALU.mult)
                link(last)
                agf = ag[:, :, :, :].rearrange("p g t m -> p (g t) m")
                link(nc.vector.reduce_sum(dg[:, 0, :], agf, axis=AX.X))
                link(nc.vector.tensor_scalar(dg[:, 3, :], dg[:, 0, :], 0.0, None, ALU.is_equal))
                nc.vector.tensor_tensor(dg[:, 1, :], dg[:, 0, :], dg[:, 3, :], ALU.add).then_inc(v_deg_safe, 1)
                dve.wait_ge(v_deg_safe, s + 1)
                link(nc.vector.tensor_scalar(dg[:, 0, :], dg[:, 3, :], -1.0, 1.0, ALU.mult, ALU.add))
                dve.wait_ge(v_deg_pow, s + 1)
                link(nc.vector.tensor_tensor(dg[:, 3, :], dg[:, 2, :], dg[:, 0, :], ALU.mult))
                nc.vector.tensor_tensor(agf, agf, dg[:, 3, :].unsqueeze(2).broadcast_to([r, ng * tiles, r]), ALU.mult).then_inc(v_ag_ok, 1)
                dve.wait_ge(v_rstd, s + 1)
                for t in range(tiles):
                    last = nc.vector.tensor_scalar(v["h"][:, t, :], v["x"][:, t, :], v["mv"][:, t, 0:1], v["rs"][:, 1, t:t + 1],
                                                   ALU.subtract, ALU.mult)
                link(last)
                if s == 0:
                    nc.vector.tensor_copy(v["acc"][:, :, :], v["x"][:, :, :])
                nc.vector.tensor_scalar(v["h"][:, :, :], v["h"][:, :, :], 0.0, None, ALU.max).then_inc(v_h_ok, 1)
            dve.wait_ge(v_fw_exp, 1)
            link(nc.vector.reciprocal(v_red[:, 3:4], v_red[:, 2:3]))
            link(nc.vector.tensor_scalar(v_fw[:, 3, :], v_fw[:, 1, :], v_red[:, 3:4], None, ALU.mult))
            for v in V:
                g0, ng, r = v["groups"][0], v["ng"], v["rows"]
                last = nc.vector.tensor_tensor(v["wm"][:, :], v["member"][:, :], v_fw[0:r, 3, g0:g0 + ng], ALU.mult)
            link(last)
            for n, (hi, lo, st_) in enumerate(((wa_hi, wa_lo, stage_a), (wb_hi, wb_lo, stage_b), (w1_hi, w1_lo, stage_1), (w2_hi, w2_lo, stage_2))):
                dve.wait_ge(w_hi_ok, n + 1)
                nc.vector.tensor_tensor(lo[:, :, :], st_[:, :, :], f(hi[:, :, :]), ALU.subtract).then_inc(w_ok, 1)
            use, gidx = 0, 0
            for s, v in enumerate(V):
                r, tiles = v["rows"], v["tiles"]
                if s:
                    dve.wait_ge(v_acc_in, 16 * B)
                for n in range(v["ng"]):
                    g = v["groups"][n]
                    for t in range(tiles):
                        use += 1
                        dve.wait_ge(v_ring_mm, use)
                        nc.vector.tensor_copy(v_s2[0:r, t, :], ps[0:r, 6 + use % 2, 0:D]).then_inc(v_ring_free, 1)
                    for t in range(tiles):
                        use += 1
                        dve.wait_ge(v_ring_mm, use)
                        nc.vector.tensor_tensor(v_u[0:r, t % 2, :], ps[0:r, 6 + use % 2, 0:D], v_b2[0:r, g, :], ALU.add).then_inc(v_ring_free, 1)
                        dve.wait_ge(v_ring_free, use)
                        link(nc.vector.tensor_scalar(v_u[0:r, t % 2, :], v_u[0:r, t % 2, :], 0.0, v["wm"][:, n:n + 1], ALU.max, ALU.mult))
                        last = nc.vector.tensor_tensor(v["acc"][:, t, :], v["acc"][:, t, :], v_u[0:r, t % 2, :], ALU.add)
                        if t + 1 < tiles:
                            link(last)
                    gidx += 1
                    last.then_inc(v_done, 1)
                    dve.wait_ge(v_done, gidx)
            dve.wait_ge(v_stored, 16 * B * len(V))

            def do(step, i, j, first):
                kind = step[0]
                pro = isinstance(i, int) and i < 0
                if kind == "tr":
                    _, ahead, tile, g = step
                    b = i + ahead
                    n = 2 * tile + g
                    if g == 0:
                        dve.wait_ge(adj_in[tile % 2], upto(b, 16 * TH, 16 * (tile // 2 + 1)))
                        if tile == 0 and not pro:
                            dve.wait_ge(deg_ok, upto(b, 1, 0))
                        nc.vector.reduce_sum(deg[:, 0, tile:tile + 1], raw[:, tile % 2, :], axis=AX.X).then_inc(rowsum_ok, 1)
                    dve.wait_ge(adj_hi_ok, upto(b, 2 * NT, n + 1))
                    nc.vector.tensor_tensor(adj_lo[:, g * TH:(g + 1) * TH, tile * P:(tile + 1) * P],
                                            bank(RING[n % 2]).rearrange("p (a b) -> p a b", b=P),
                                            f(adj_hi[:, g * TH:(g + 1) * TH, tile * P:(tile + 1) * P]), ALU.subtract).then_inc(ring_free, 1)
                elif kind == "deg":
                    dve.wait_ge(rowsum_ok, upto(i, NT, NT))
                    if not first:
                        dve.wait_ge(hs_ok, upto(i, NT, 0))
                    nc.vector.tensor_scalar(deg[:, 1, :], deg[:, 0, :], DEG_EPS, None, ALU.add).then_inc(deg_ok, 1)
                    dve.wait_ge(deg_ok, upto(i, 1, 1))
                    nc.vector.reciprocal(inv_deg[:, :], deg[:, 1, :]).then_inc(inv_ok, 1)
                    dve.wait_ge(inv_ok, upto(i, 1, 1))
                elif kind == "stats":
                    _, L, t = step
                    b = i + 1 if L == 1 else i
                    n = (L - 1) * NT + t
                    if L == 1 and t == 0:
                        dve.wait_ge(x_in, upto(b, 16 * X_DMAS, 16 * X_DMAS))
                    layer_stats(b, n, t, pro)
                elif kind == "split":
                    _, L, t = step
                    n = (L - 1) * NT + t
                    dve.wait_ge(h_hi_ok, upto(i, 3 * NT, n + 1))
                    nc.vector.scalar_tensor_tensor(out=h_lo[:, t, :], in0=y[:, t % TH, :], scalar=0.0, in1=f(h_hi[:, t, :]),
                                                   op0=ALU.max, op1=ALU.subtract).then_inc(h_ok, 1)
                elif kind == "pt":
                    _, L, c, d = step
                    if L < 3:
                        n = agg_group(L, c, d)
                        dve.wait_ge(pt_hi_ok, upto(i, 8, n + 1))
                        nc.vector.tensor_tensor(pt_lo[:, d, :], bank(AGG[n % 3]), f(pt_hi[:, d, :]), ALU.subtract).then_inc(pt_ok, 1)
                elif kind == "ht":
                    c = step[1]
                    for d in range(ND):
                        dve.wait_ge(ht_hi_ok, upto(i, 4, 2 * c + d + 1))
                        nc.vector.tensor_tensor(ht_lo[:, d, :], bank(RING[d]), f(ht_hi[:, d, :]), ALU.subtract).then_inc(ring_free, 1)
                elif kind == "w":
                    _, L, c, p = step
                    u = ring_use(i, ring_of["w", L, c] + p)
                    dve.wait_ge(w_mm, upto(i, 8, 4 * (L - 1) + 2 * c + p + 1))
                    t0 = c * TH + 2 * p
                    o = bank(RING[p]).rearrange("p (a b) -> p a b", b=D)
                    if L == 1:
                        dve.wait_ge(xb_ok, upto(i, NT, t0 + 2))
                        nc.vector.tensor_tensor(x[:, t0:t0 + 2, :], o, x[:, t0:t0 + 2, :], ALU.add).then_inc(ring_free, 1)
                    else:
                        for q in range(2):
                            last = nc.vector.scalar_tensor_tensor(out=o[:, q, :], in0=o[:, q, :], scalar=inv_deg[:, t0 + q:t0 + q + 1],
                                                                  in1=bias2[:, :], op0=ALU.mult, op1=ALU.add)
                        last.then_inc(relu_ok, 1)
                        dve.wait_ge(relu_ok, upto(i, NT // 2, t0 // 2 + 1))
                        dve.wait_ge(y_ok, upto(i, 3 * NT, NT + t0 + 2))
                        nc.vector.scalar_tensor_tensor(out=x[:, t0:t0 + 2, :], in0=o, scalar=0.0, in1=x[:, t0:t0 + 2, :],
                                                       op0=ALU.max, op1=ALU.add).then_inc(ring_free, 1)
                    dve.wait_ge(ring_free, u + 1)
                    for q in range(2):
                        layer_stats(i, L * NT + t0 + q, t0 + q, False)
                elif kind == "fix":
                    t = step[1]
                    dh, dl = adj_hi[:, t, t * P:(t + 1) * P], adj_lo[:, t, t * P:(t + 1) * P]
                    n = upto(i, 4 * NT, 4 * t)
                    if t == 0:
                        dve.wait_ge(agg_mm, upto(i, 12, 8))
                    nc.vector.tensor_tensor(fixed[:, :], f(dh), f(dl), ALU.add).then_inc(fix_ok, 1)
                    dve.wait_ge(fix_ok, n + 1)
                    nc.vector.tensor_tensor(fixed[:, :], fixed[:, :], eps_ident[:, :], ALU.add).then_inc(fix_ok, 1)
                    dve.wait_ge(fix_ok, n + 2)
                    nc.vector.tensor_copy(dh, fixed[:, :]).then_inc(fix_ok, 1)
                    dve.wait_ge(fix_ok, n + 3)
                    nc.vector.tensor_tensor(dl, fixed[:, :], f(dh), ALU.subtract).then_inc(fix_ok, 1)
                    dve.wait_ge(fix_ok, n + 4)
                elif kind == "chunk_split":
                    c = step[1]
                    if c % 2 == 0:
                        dve.wait_ge(agg_ok, upto(j, 4, 2 * (c // 2) + 2))
                    if c == 0 and not (isinstance(j, int) and j == 0):
                        dve.wait_ge(rms_ok, upto(j, NC, 0))
                        dve.wait_ge(bcast_mm, upto(j, NC, 0))
                    if not (isinstance(j, int) and j == 0 and c == 0):
                        dve.wait_ge(up_mm, upto(j, PAIRS * NC, PAIRS * c))
                    src = agg[:, :, c * CH:(c + 1) * CH]
                    nc.vector.tensor_copy(ac_hi[:, :, :], src).then_inc(ac_hi_ok, 1)
                    dve.wait_ge(ac_hi_ok, upto(j, NC, c + 1))
                    nc.vector.tensor_tensor(ac_lo[:, :, :], src, f(ac_hi[:, :, :]), ALU.subtract).then_inc(ac_ok, 1)
                elif kind == "sumsq":
                    c = step[1]
                    dve.wait_ge(col_mm, upto(j, NC, c + 1))
                    if c > 0:
                        dve.wait_ge(rms_ok, upto(j, NC, c))
                    nc.vector.tensor_scalar(msq[:, :], bank(HID[0], 2), 1.0 / H, RMS_EPS, ALU.mult, ALU.add).then_inc(msq_ok, 1)
                elif kind == "bcast":
                    c = step[1]
                    dve.wait_ge(rms_ok, upto(j, NC, c + 1))
                    if c > 0:
                        dve.wait_ge(bcast_mm, upto(j, NC, c))
                    for q in range(2):
                        last = nc.vector.tensor_scalar(rdiag[:, q * P:(q + 1) * P], ident[:, :], rms[:, q:q + 1], None, ALU.mult)
                    last.then_inc(rdiag_ok, 1)
                elif kind == "scale":
                    c = step[1]
                    dve.wait_ge(bcast_mm, upto(j, NC, c + 1))
                    dve.wait_ge(hid_ok, upto(j, PAIRS * NC, PAIRS * (c + 1)))
                    for q in range(2):
                        part = hid[:, q * NH // 2:(q + 1) * NH // 2, :]
                        nc.vector.tensor_tensor(part, part, bank(HID[1], CH).unsqueeze(1).broadcast_to([P, NH // 2, CH]),
                                                ALU.mult).then_inc(scaled_ok, 1)
                elif kind == "act":
                    _, c, p = step
                    n = PAIRS * c + p
                    dve.wait_ge(silu_ok, upto(j, PAIRS * NC, n + 1))
                    if p >= 2:
                        dve.wait_ge(down_mm, upto(j, PAIRS * NC, n - 1))
                    src = hid[:, 2 * p:2 * p + 2, :]
                    nc.vector.tensor_copy(act_hi[:, p % 2], src).then_inc(act_hi_ok, 1)
                    dve.wait_ge(act_hi_ok, upto(j, PAIRS * NC, n + 1))
                    nc.vector.tensor_tensor(act_lo[:, p % 2], src, f(act_hi[:, p % 2]), ALU.subtract).then_inc(act_ok, 1)
                elif kind == "result":
                    c = step[1]
                    dve.wait_ge(down_mm, upto(j, PAIRS * NC, PAIRS * (c + 1)))
                    dve.wait_ge(tail_ok, upto(j, NT, 2 * c + 2))
                    t2 = tail[:, 2 * c:2 * c + 2, :]
                    nc.vector.tensor_tensor(t2, bank(DOWN).rearrange("p (a b) -> p a b", b=D), t2, ALU.add).then_inc(res_ok, 1)

            def layer_stats(b, n, t, pro):
                if not pro and n == 0:
                    dve.wait_ge(y_ok, upto(b, 3 * NT, 0))
                nc.vector.bn_stats(st[:, t, :], x[:, t, :]).then_inc(bn_ok, 1)
                wait_apart(dve, bn_ok, upto(b, 3 * NT, n + 1))
                nc.vector.bn_aggr(mv[:, t, :], st[:, t, :]).then_inc(stats_ok, 1)

            run(dve, do)

        @block.tensor
        def _(pe):
            pe.wait_ge(const_in, 16 * (1 + 2 * len(V)))
            pe.wait_ge(const_ok, 2)
            done_tr, gidx, use = 0, 0, 0
            for s, v in enumerate(V):
                r, tiles = v["rows"], v["tiles"]
                cols = r * tiles
                pe.wait_ge(v_ag_ok, s + 1)
                for n in range(v["ng"] * tiles):
                    done_tr += 1
                    if done_tr > 2:
                        pe.wait_ge(v_ant, done_tr - 2)
                    g, t = divmod(n, tiles)
                    nc.tensor.transpose(ps[0:r, done_tr % 2, 0:r], v["ag"][:, g, t, :], ident[0:r, 0:r]).then_inc(v_tr, 1)
                pe.wait_ge(v_h_ok, s + 1)
                pe.wait_ge(v_ant, done_tr)
                for n in range(v["ng"]):
                    for d in range(ND):
                        for t in range(tiles):
                            last = nc.tensor.matmul(ps[:, 2 + d, t * r:(t + 1) * r], v["h"][:, t, d * P:(d + 1) * P], v["an_t"][:, n, t, :],
                                                    start=True, stop=True)
                        last.then_inc(v_y_mm, 1)
                    pe.wait_ge(v_w_in[gidx % 2], 32 * (gidx // 2 + 1))
                    pe.wait_ge(v_y_ok, ND * (gidx + 1))
                    for k in range(NK0):
                        if NK0 * gidx + k >= 2:
                            pe.wait_ge(v_hid_ok, NK0 * gidx + k - 1)
                        for d in range(ND):
                            last = nc.tensor.matmul(ps[:, 4 + k % 2, 0:cols], v_w1[:, gidx % 2, d, k * P:(k + 1) * P], v_yt[:, d, 0:cols],
                                                    start=(d == 0), stop=(d == ND - 1))
                        last.then_inc(v_hid_mm, 1)
                    pe.wait_ge(v_hid_ok, NK0 * (gidx + 1))
                    for t in range(tiles):
                        use += 1
                        if use > 2:
                            pe.wait_ge(v_ring_free, use - 2)
                        for k in range(NK0):
                            last = nc.tensor.matmul(ps[0:r, 6 + use % 2, 0:D], v_hid[:, k, t * r:(t + 1) * r], v_w2[:, gidx % 2, k, :],
                                                    start=(k == 0), stop=(k == NK0 - 1))
                        last.then_inc(v_ring_mm, 1)
                    for t in range(tiles):
                        use += 1
                        pe.wait_ge(v_ring_free, max(use - 2, use - 1 - t - (tiles - 1 - t)))
                        nc.tensor.matmul(ps[0:r, 6 + use % 2, 0:D], v["an_t"][:, n, t, :], v_s2[0:r, t, :], start=True, stop=True).then_inc(v_ring_mm, 1)
                    gidx += 1
            pe.wait_ge(v_stored, 16 * B * len(V))
            pe.wait_ge(w_ok, 4)

            def three(o, w_hi, w_lo, m_hi, m_lo, start, stop, skip=False):
                nc.tensor.matmul(o, w_hi, m_hi, start=start, stop=False, skip_group_check=skip)
                nc.tensor.matmul(o, w_hi, m_lo, start=False, stop=False, skip_group_check=skip)
                return nc.tensor.matmul(o, w_lo, m_hi, start=False, stop=stop, skip_group_check=skip)

            def ring_wait(u):
                if not (isinstance(u, int) and u < 2):
                    pe.wait_ge(ring_free, u - 1)

            def agg_free(i, L, c, d, first):
                n = agg_group(L, c, d) - 3
                if n >= 8:
                    pe.wait_ge(agg_ok, upto(i, 4, n - 7))
                elif n >= 0:
                    pe.wait_ge(pt_ok, upto(i, 8, n + 1))
                elif not first:
                    pe.wait_ge(agg_ok, upto(i, 4, n + 1) if not isinstance(i, int) else 4 * i + n + 1)

            def agg_unit(L, c, d, m):
                rhs = slice(c * HALF, (c + 1) * HALF)
                w = slice(d * P, (d + 1) * P)
                return three(bank(AGG[agg_group(L, c, d) % 3]), h_hi[:, m, w], h_lo[:, m, w], adj_hi[:, m, rhs], adj_lo[:, m, rhs],
                             m == 0, m == NT - 1)

            def do(step, i, j, first):
                kind = step[0]
                if kind == "tr":
                    _, ahead, tile, g = step
                    b = i + ahead
                    if g == 0:
                        pe.wait_ge(adj_in[tile % 2], upto(b, 16 * TH, 16 * (tile // 2 + 1)))
                    ring_wait(tr_use(b, tile, g))
                    for q in range(TH):
                        m = g * TH + q
                        last = nc.tensor.transpose(bank(RING[g])[:, q * P:(q + 1) * P], raw[:, tile % 2, m * P:(m + 1) * P], ident[:, :])
                    last.then_inc(tr_mm, 1)
                elif kind == "agg2":
                    _, L, m = step
                    pe.wait_ge(h_ok, upto(i, 3 * NT, (L - 1) * NT + m + 1))
                    if m == 0 and L == 1:
                        pe.wait_ge(ring_free, ring_use(i, 0))
                    if L == 3 and m < TH:
                        pe.wait_ge(fix_ok, upto(i, 4 * NT, 4 * m + 4))
                    for d in range(ND):
                        if m == 0:
                            agg_free(i, L, 0, d, first)
                        last = agg_unit(L, 0, d, m)
                        if m == NT - 1:
                            last.then_inc(agg_mm, 1)
                elif kind == "agg1":
                    _, L, d, m = step
                    if m == 0:
                        if L == 1 and d == 0:
                            pe.wait_ge(ring_free, ring_use(i, 8))
                        agg_free(i, L, 1, d, first)
                        if L == 3 and d == 0:
                            pe.wait_ge(fix_ok, upto(i, 4 * NT, 4 * NT))
                    last = agg_unit(L, 1, d, m)
                    if m == NT - 1:
                        last.then_inc(agg_mm, 1)
                elif kind == "ht":
                    c = step[1]
                    pe.wait_ge(hs_ok, upto(i, NT, (c + 1) * TH))
                    for d in range(ND):
                        ring_wait(ring_use(i, ring_of["ht", 2, c] + d))
                        for q in range(TH):
                            last = nc.tensor.transpose(bank(RING[d])[:, q * P:(q + 1) * P], y[:, q, d * P:(d + 1) * P], ident[:, :])
                        last.then_inc(ht_mm, 1)
                elif kind == "w":
                    _, L, c, p = step
                    if p == 0:
                        pe.wait_ge(pt_ok, upto(i, 8, 4 * (L - 1) + 2 * c + 2))
                        if L == 2:
                            pe.wait_ge(ring_free, ring_use(i, ring_of["ht", 2, c] + 2))
                    ring_wait(ring_use(i, ring_of["w", L, c] + p))
                    for q in range(2):
                        o = bank(RING[p])[:, q * D:(q + 1) * D]
                        at = slice((2 * p + q) * P, (2 * p + q + 1) * P)
                        for d in range(ND):
                            if L == 1:
                                last = three(o, pt_hi[:, d, at], pt_lo[:, d, at], wa_hi[:, d, :], wa_lo[:, d, :], d == 0, d == ND - 1)
                            else:
                                three(o, ht_hi[:, d, at], ht_lo[:, d, at], wb_hi[:, d, :], wb_lo[:, d, :], d == 0, False)
                                last = three(o, pt_hi[:, d, at], pt_lo[:, d, at], wb_hi[:, ND + d, :], wb_lo[:, ND + d, :], False, d == ND - 1)
                    last.then_inc(w_mm, 1)
                elif kind == "up":
                    _, c, p = step
                    zero = isinstance(j, int) and j == 0 and c == 0
                    if p == 0:
                        pe.wait_ge(ac_ok, upto(j, NC, c + 1))
                        if not zero:
                            pe.wait_ge(msq_ok, upto(j, NC, c))
                            if c == 0:
                                pe.wait_ge(res_ok, upto(j, NC, 0))
                    elif p == 1:
                        if not zero:
                            pe.wait_ge(scaled_ok, upto(j, 2 * NC, 2 * c))
                    else:
                        pe.wait_ge(sq_ok, upto(j, PAIRS * NC, PAIRS * c + p - 1))
                    for q in range(2):
                        k = 2 * p + q
                        o = bank(HID[p % 2])[:, q * CH:(q + 1) * CH]
                        for d in range(ND):
                            last = three(o, w1_hi[:, d, k * P:(k + 1) * P], w1_lo[:, d, k * P:(k + 1) * P], ac_hi[:, d, :], ac_lo[:, d, :],
                                         d == 0, d == ND - 1)
                    last.then_inc(up_mm, 1)
                elif kind == "sumsq":
                    c = step[1]
                    pe.wait_ge(sum_ok, upto(j, 3 * NC, 3 * (c + 1)))
                    for q in range(2):
                        for a in range(2):
                            last = nc.tensor.matmul(bank(HID[0])[:, q:q + 1], sq_sum[:, a, q * P:(q + 1) * P], ones[:, 0:1],
                                                    start=(a == 0), stop=(a == 1))
                    last.then_inc(col_mm, 1)
                elif kind == "bcast":
                    c = step[1]
                    pe.wait_ge(rdiag_ok, upto(j, NC, c + 1))
                    nc.tensor.matmul(bank(HID[1], CH), ones[:, :], rdiag[:, :], start=True, stop=True).then_inc(bcast_mm, 1)
                elif kind == "down":
                    _, c, p = step
                    n = PAIRS * c + p
                    if p == 0 and c > 0:
                        pe.wait_ge(res_ok, upto(j, NC, c))
                    pe.wait_ge(act_ok, upto(j, PAIRS * NC, n + 1))
                    for a in range(2):
                        k = 2 * p + a
                        for q in range(2):
                            at = slice(q * P, (q + 1) * P)
                            last = three(bank(DOWN)[:, q * D:(q + 1) * D], act_hi[:, p % 2, a, at], act_lo[:, p % 2, a, at],
                                         w2_hi[:, k, :], w2_lo[:, k, :], k == 0 and q == 0, k == NH - 1, skip=True)
                    last.then_inc(down_mm, 1)

            run(pe, do)


_INS = ["x", "adj", "L0_gnn_W1", "L0_gnn_b1", "L0_gnn_W2", "L0_gnn_b2", "L0_gnn_fusion_w", "L1_gnn_weight", "L1_gnn_bias",
        "L2_gnn_weight", "L2_gnn_bias", "L3_gnn_epsilon", "L3_gnn_W1", "L3_gnn_b1", "L3_gnn_rms_weight", "L3_gnn_W2",
        "L3_gnn_b2"]


def build(nc, arrays):
    f32 = mybir.dt.float32
    t_in = {n: nc.dram_tensor(f"in_{n}", a.shape, f32, kind="ExternalInput").ap() for n, a in arrays.items()}
    shape = arrays["x"].shape
    out = nc.dram_tensor("out_x", shape, f32, kind="ExternalOutput").ap()
    scratch = nc.dram_tensor("scratch_rows", (shape[0], SPACES[0][0], shape[2]), f32, kind="Internal").ap()
    gnn_stack(nc, t_in, out, scratch)


def kernel(**inputs):
    import concourse.bacc as bacc
    from concourse.bass_utils import run_bass_kernel_spmd

    arrays = {n: np.ascontiguousarray(inputs[n]) for n in _INS}
    arrays["L3_gnn_epsilon"] = arrays["L3_gnn_epsilon"].reshape(1)
    arrays.update(shape_constants())
    nc = bacc.Bacc("TRN2", target_bir_lowering=False, num_devices=1)
    build(nc, arrays)
    r = run_bass_kernel_spmd(nc, [{f"in_{n}": a for n, a in arrays.items()}], core_ids=[0])
    return r.results[0]["out_x"]
```

```python
import numpy as np
import concourse.bass as bass
from concourse import mybir
from contextlib import ExitStack

GROUPS = [list(range(25)), [0, 1, 2, 3, 4, 5, 6, 7, 8], [0, 9, 10, 11, 12, 13, 14], [6, 7, 8, 12, 13, 14],
          [3, 4, 5, 9, 10, 11]]
SPACES = [(25, 4, [0]), (15, 8, [1, 2, 3, 4])]


def shape_constants():
    consts = {"identity": np.eye(128, dtype=np.float32)}
    for s, (nodes, per_tile, groups) in enumerate(SPACES):
        rows = nodes * per_tile
        pair = np.zeros((rows, len(groups), rows), np.float32)
        member = np.zeros((rows, len(groups)), np.float32)
        for n, g in enumerate(groups):
            for q in range(per_tile):
                at = [q * nodes + v for v in GROUPS[g]]
                pair[np.ix_(at, [n], at)] = 1.0
                member[at, n] = 1.0
        consts[f"pair_mask_{s}"] = pair
        consts[f"member_mask_{s}"] = member
    return consts


def gnn_stack(nc, t_in, out, scratch):
    f32, f32r = mybir.dt.float32, mybir.dt.float32r
    ALU, ACT, AX = mybir.AluOpType, mybir.ActivationFunctionType, mybir.AxisListType
    x_d, adj_d = t_in["x"], t_in["adj"]
    B, N, D = x_d.shape
    H = t_in["L3_gnn_W1"].shape[1]
    H0 = t_in["L0_gnn_W1"].shape[2]
    P = 128
    NT = N // P
    ND = D // P
    NH = H // P
    HALF = N // 2
    TH = NT // 2
    CH = 2 * P
    NC = N // CH
    LN_EPS, DEG_EPS, RMS_EPS = 1e-5, 1e-8, 1e-6
    F0 = SPACES[0][0]

    ctx = ExitStack()
    with ctx:
        def sb(name, shape, dt=f32, scope=ctx):
            return scope.enter_context(nc.sbuf_tensor(name, shape, dt))

        def sem(name):
            return ctx.enter_context(nc.semaphore(name))

        wa_hi, wa_lo = sb("wa_hi", [P, ND, D], f32r), sb("wa_lo", [P, ND, D], f32r)
        wb_hi, wb_lo = sb("wb_hi", [P, 2 * ND, D], f32r), sb("wb_lo", [P, 2 * ND, D], f32r)
        w1_hi, w1_lo = sb("w1_hi", [P, ND, H], f32r), sb("w1_lo", [P, ND, H], f32r)
        w2_hi, w2_lo = sb("w2_hi", [P, NH, D], f32r), sb("w2_lo", [P, NH, D], f32r)
        ident = sb("ident", [P, P])
        ones = sb("ones", [P, 1])
        bias1, bias2, bias3 = (sb(n, [P, D]) for n in ("bias1", "bias2", "bias3"))
        b1_col, rmsw_col = sb("b1_col", [P, NH]), sb("rmsw_col", [P, NH])
        minus_half = sb("minus_half", [P, 8])
        epsilon_col = sb("epsilon_col", [P, 1])

        ps = ctx.enter_context(nc.psum_tensor("ps", [P, 8, 512], f32))
        AGG, RING, HID, DOWN = (0, 1, 2), (3, 4), (5, 6), 7

        early = ExitStack()
        stage_a, stage_b = sb("stage_a", [P, ND, D], scope=early), sb("stage_b", [P, 2 * ND, D], scope=early)
        stage_1, stage_2 = sb("stage_1", [P, ND, H], scope=early), sb("stage_2", [P, NH, D], scope=early)
        NG, NK0 = len(GROUPS), H0 // P
        v_w1 = sb("v_w1", [P, 2, ND, H0], scope=early)
        v_w2 = sb("v_w2", [P, 2, NK0, D], scope=early)
        v_b1 = sb("v_b1", [P, NG, NK0], scope=early)
        v_b2 = sb("v_b2", [P, NG, D], scope=early)
        v_fw = sb("v_fw", [P, 4, NG], scope=early)
        v_red = sb("v_red", [P, 4], scope=early)
        V = []
        for s, (nodes, per_tile, groups) in enumerate(SPACES):
            rows, tiles, ng = nodes * per_tile, B // per_tile, len(groups)
            V.append(dict(
                rows=rows, tiles=tiles, ng=ng, nodes=nodes, per_tile=per_tile, groups=groups,
                x=sb(f"v_x{s}", [rows, tiles, D], scope=early), acc=sb(f"v_acc{s}", [rows, tiles, D], scope=early),
                h=sb(f"v_h{s}", [rows, tiles, D], scope=early),
                adj=sb(f"v_adj{s}", [rows, tiles, rows], scope=early),
                mask=sb(f"v_mask{s}", [rows, ng, rows], scope=early), member=sb(f"v_member{s}", [rows, ng], scope=early),
                ag=sb(f"v_ag{s}", [rows, ng, tiles, rows], scope=early),
                an_t=sb(f"v_an_t{s}", [rows, ng, tiles, rows], scope=early),
                deg=sb(f"v_deg{s}", [rows, 4, ng * tiles], scope=early),
                st=sb(f"v_st{s}", [rows, tiles, 6], scope=early), mv=sb(f"v_mv{s}", [rows, tiles, 2], scope=early),
                rs=sb(f"v_rs{s}", [rows, 2, tiles], scope=early), wm=sb(f"v_wm{s}", [rows, ng], scope=early)))
        VR = max(v["rows"] for v in V)
        VC = max(v["rows"] * v["tiles"] for v in V)
        VT = max(v["tiles"] for v in V)
        v_yt = sb("v_yt", [P, ND, VC], scope=early)
        v_hid = sb("v_hid", [P, NK0, VC], scope=early)
        v_s2 = sb("v_s2", [VR, VT, D], scope=early)
        v_u = sb("v_u", [VR, 2, D], scope=early)
        early.close()

        adj_hi, adj_lo = sb("adj_hi", [P, NT, N], f32r), sb("adj_lo", [P, NT, N], f32r)
        raw = sb("raw", [P, 2, N])
        x = sb("x_rows", [P, NT, D])
        tail = sb("tail", [P, NT, D])
        h_hi, h_lo = sb("h_hi", [P, NT, D], f32r), sb("h_lo", [P, NT, D], f32r)
        y = sb("y", [P, TH, D])
        pt_hi, pt_lo = sb("pt_hi", [P, ND, HALF], f32r), sb("pt_lo", [P, ND, HALF], f32r)
        ht_hi, ht_lo = sb("ht_hi", [P, ND, HALF], f32r), sb("ht_lo", [P, ND, HALF], f32r)
        agg = sb("agg", [P, ND, N])
        ac_hi, ac_lo = sb("ac_hi", [P, ND, CH], f32r), sb("ac_lo", [P, ND, CH], f32r)
        hid = sb("hid", [P, NH, CH])
        sq_sum, sq = sb("sq_sum", [P, CH]), sb("sq", [P, 2, CH])
        act_hi, act_lo = sb("act_hi", [P, 2, 2, CH], f32r), sb("act_lo", [P, 2, 2, CH], f32r)
        rms_rows = sb("rms_rows", [P, 2, P])
        hs = sb("hs", [P, 2, D])
        fixed = sb("fixed", [P, 2, P])
        st, mv = sb("st", [P, NT, 6]), sb("mv", [P, NT, 2])
        ve, rstd = sb("ve", [P, TH]), sb("rstd", [P, TH])
        deg, inv_deg = sb("deg", [P, 2, NT]), sb("inv_deg", [P, NT])
        msq, rms = sb("msq", [P, 2]), sb("rms", [P, 2])

        def f(view):
            return view.bitcast(f32)

        w_in, w_hi_ok, w_ok = sem("w_in"), sem("w_hi_ok"), sem("w_ok")
        const_in, vectors_in, const_ok = sem("const_in"), sem("vectors_in"), sem("const_ok")
        v_x_in, v_adj_zero, v_adj_in = sem("v_x_in"), sem("v_adj_zero"), sem("v_adj_in")
        v_w_in = [sem("v_w_in0"), sem("v_w_in1")]
        v_dve, v_pool, v_act = sem("v_dve"), sem("v_pool"), sem("v_act")
        v_fw_sub, v_fw_exp = sem("v_fw_sub"), sem("v_fw_exp")
        v_deg_pow, v_deg_safe, v_var_ok, v_rstd = sem("v_deg_pow"), sem("v_deg_safe"), sem("v_var_ok"), sem("v_rstd")
        v_ag_ok, v_tr, v_ant = sem("v_ag_ok"), sem("v_tr"), sem("v_ant")
        v_h_ok, v_y_mm, v_y_ok = sem("v_h_ok"), sem("v_y_mm"), sem("v_y_ok")
        v_hid_mm, v_hid_ok = sem("v_hid_mm"), sem("v_hid_ok")
        v_ring_mm, v_ring_free = sem("v_ring_mm"), sem("v_ring_free")
        v_acc_in, v_stored, v_done = sem("v_acc_in"), sem("v_stored"), sem("v_done")

        x_in = [sem("x_in0"), sem("x_in1")]
        adj_in = [sem("adj_in0"), sem("adj_in1")]
        tr_mm, adj_hi_ok = sem("tr_mm"), sem("adj_hi_ok")
        ring_free = sem("ring_free")
        rowsum_ok = sem("rowsum_ok")
        deg_ok, inv_ok = sem("deg_ok"), sem("inv_ok")
        bn_ok, stats_ok = sem("bn_ok"), sem("stats_ok")
        ve_ok, rstd_ok = sem("ve_ok"), sem("rstd_ok")
        y_ok, h_hi_ok, h_ok = sem("y_ok"), sem("h_hi_ok"), sem("h_ok")
        hs_ok = sem("hs_ok")
        agg_mm = sem("agg_mm")
        pt_hi_ok, pt_ok = sem("pt_hi_ok"), sem("pt_ok")
        agg_ok = sem("agg_ok")
        ht_mm, ht_hi_ok = sem("ht_mm"), sem("ht_hi_ok")
        w_mm = sem("w_mm")
        relu_ok = sem("relu_ok")
        xb_ok, tail_ok = sem("xb_ok"), sem("tail_ok")
        fsum_ok = sem("fsum_ok")
        fix_hi_ok, fix_ok = sem("fix_hi_ok"), sem("fix_ok")
        ac_hi_ok, ac_ok = sem("ac_hi_ok"), sem("ac_ok")
        up_mm, hid_ok, sq_ok = sem("up_mm"), sem("hid_ok"), sem("sq_ok")
        sum_ok = sem("sum_ok")
        col_mm, msq_ok, rms_ok, rms_rows_ok, bcast_mm = (sem(n) for n in ("col_mm", "msq_ok", "rms_ok", "rms_rows_ok", "bcast_mm"))
        scaled_ok = sem("scaled_ok")
        silu_ok, act_hi_ok, act_ok, down_mm = (sem(n) for n in ("silu_ok", "act_hi_ok", "act_ok", "down_mm"))
        res_ok, stored = sem("res_ok"), sem("stored")

        waits_apart = {e.engine: sem(f"waits_apart_{n}") for n, e in (("sp", nc.sync), ("dve", nc.vector), ("pool", nc.gpsimd))}

        X_DMAS = 3
        RING_USES = 28
        PAIRS = NH // 2

        def upto(graph, per_graph, n):
            return graph * per_graph + n

        def ring_use(graph, n):
            return graph * RING_USES + 8 + n

        ring_of = {("w", 1, 0): 8, ("w", 1, 1): 10, ("ht", 2, 0): 12, ("w", 2, 0): 14, ("ht", 2, 1): 16,
                   ("w", 2, 1): 18}

        def tr_use(graph, tile, g):
            return ring_use(graph, 2 * tile + g - 8)

        COST = {"agg2": 1.3, "agg1": 0.65, "tr": 0.45, "w1": 1.3, "w2": 2.6, "ht": 0.45, "fill": 2.4}

        def mlp_steps(c, part):
            up = [(0.6, ("chunk_split", c))] + [(1.4, ("up", c, p)) for p in range(PAIRS)]
            down = [(2.4, ("sumsq", c)), (0.8, ("rms", c)), (1.3, ("rms_rows", c)), (0.9, ("bcast", c)),
                    (0.3, ("scale", c, 0)), (0.1, ("silu", c, 0)), (0.1, ("scale", c, 1)), (0.6, ("silu", c, 1)),
                    (0.6, ("act", c, 0)), (0.1, ("scale", c, 2)), (0.6, ("silu", c, 2)), (0.6, ("act", c, 1)),
                    (0.3, ("down", c, 0)), (0.1, ("scale", c, 3)), (0.6, ("silu", c, 3)), (0.3, ("act", c, 2)),
                    (0.3, ("down", c, 1)), (0.6, ("act", c, 3)), (0.3, ("down", c, 2)), (0.6, ("down", c, 3)),
                    (0.1, ("result", c))]
            return {"up": up, "down": down, "all": up + down}[part]

        def front_steps(nxt):
            o = []
            for L in (1, 2, 3):
                last = L == 3
                o += [("split", L, 0), ("split", L, 1)]
                if L > 1:
                    o += [("fill",), ("w", L - 1, 1, 0), ("split", L, 2)]
                    o += [("fix", 0), ("fix", 1)] * last
                    o += [("sum_fix", 2), ("sum_fix", 3)] * last
                    o += [("w", L - 1, 1, 1), ("split", L, 3), ("rstd", L, 1)]
                    o += [("fix", 2), ("fix", 3), ("sum_fix", 4), ("sum_fix", 5)] * last
                    o += [("hs", 0)] * (L == 2)
                else:
                    o += [("split", L, 2), ("split", L, 3)]
                for m in range(NT):
                    if L == 2 and m == 1:
                        o += [("ht", 0), ("hs", 1)]
                    if m == 1:
                        o += [("norm", L, t) for t in range(TH, NT)]
                    if m == 2:
                        o += [("split", L, t) for t in (TH, TH + 1)]
                    if m == 4:
                        o += [("split", L, t) for t in (TH + 2, TH + 3)]
                    if L == 2 and m == 3:
                        o.append(("ht", 1))
                    if last and m in (4, 6):
                        o += [("fix", m), ("fix", m + 1)] + [("sum_fix", 6), ("sum_fix", 7)] * (m == 4)
                    o.append(("agg2", L, m))
                    if L == 1:
                        o.append(("tr", 0, TH + m // 2, m % 2))
                    if last and nxt and m == 3:
                        o += [("tail", t) for t in range(TH)] + [("load_x", 0)]
                o += [("pt", L, 0, 0), ("pt", L, 0, 1)]
                if L == 1:
                    o += [("deg",)]
                    o += [("xb", t) for t in range(NT)]
                if last:
                    o += [("mlp_before",)]
                    o += [("tail", t) for t in range(0 if not nxt else TH, NT)] + [("load_x", 1)] * nxt
                for d in range(ND):
                    for m in range(NT):
                        o.append(("agg1", L, d, m))
                        if last and nxt and m % 2 == 0:
                            o.append(("tr", 1, 2 * d + m // 4, (m // 2) % 2))
                        if last and nxt and d == 1:
                            o += [("stats", 1, m)] * (m < TH)
                        if not last and d == 0 and m in (4, 5):
                            o.append(("w", L, 0, m - 4))
                            if m == 5:
                                o += [("rstd", L + 1, 0)]
                        if L == 2 and d == 0 and m >= 5:
                            o.append({5: ("hs", 2), 6: ("ht", 2), 7: ("hs", 3)}[m])
                        if not last and d == 0 and m == 7:
                            o += [("norm", L + 1, t) for t in range(TH)]
                        if L == 2 and d == 1 and m == 1:
                            o += [("ht", 3), ("sum_fix", 0), ("sum_fix", 1)]
                    o.append(("pt", L, 1, d))
                if last and nxt:
                    o += [("rstd", 1, 0)] + [("norm", 1, t) for t in range(TH)]
                    o += [("stats", 1, t) for t in range(TH, NT)] + [("rstd", 1, 1)]
            return o

        def merge(front, others, age, until=None):
            end = next((n for n, step in enumerate(front) if step == until), len(front))
            cost = [COST.get(step[0] if step[0] != "w" else f"w{step[1]}", 0.0) for step in front]
            scale = sum(cost[:end]) / max(sum(g for g, _ in others), 1e-9) * 0.98
            merged, gap, others = [], 0.0, list(others)
            for n, step in enumerate(front):
                if n == end:
                    merged += [(s, age) for _, s in others]
                    others = []
                if step[0] not in ("fill", "mlp_before"):
                    merged.append((step, 0))
                gap += cost[n]
                while others and gap >= others[0][0] * scale:
                    gap -= others[0][0] * scale
                    merged.append((others.pop(0)[1], age))
            return merged + [(s, age) for _, s in others]

        def body_steps(with_tail, nxt):
            others = mlp_steps(0, "down") if with_tail else []
            for c in range(1, NC if with_tail else 0):
                others += mlp_steps(c, "all")
            front = front_steps(nxt)
            cut = front.index(("mlp_before",))
            return merge(front[:cut], others, 1) + merge(front[cut:], mlp_steps(0, "up"), 0)

        def epilogue_steps():
            others = mlp_steps(0, "down")
            for c in range(1, NC):
                others += mlp_steps(c, "all")
            return [(s, 1) for _, s in others]

        def prologue_steps():
            return [("load_x", 0), ("load_x", 1)] + [("tr", 1, t, g) for t in range(TH) for g in range(2)] + \
                [("stats", 1, t) for t in range(NT)] + \
                [("rstd", 1, 0)] + [("norm", 1, t) for t in range(TH)] + [("rstd", 1, 1)]

        def run(engine, do):
            for step in prologue_steps():
                do(step, -1, None, True)
            for step, age in body_steps(False, True):
                do(step, 0, 0 - age, True)
            if B > 3:
                with engine.Fori(1, B - 1) as i:
                    for step, age in body_steps(True, True):
                        do(step, i, i - age, False)
            else:
                for i in range(1, B - 1):
                    for step, age in body_steps(True, True):
                        do(step, i, i - age, False)
            for step, age in body_steps(True, False):
                do(step, B - 1, B - 1 - age, False)
            for step, age in epilogue_steps():
                do(step, B, B - age, False)

        def wait_apart(engine, semaphore, value):
            engine.wait_ge(semaphore, value)
            engine.sem_inc(waits_apart[engine.engine], 1)

        def bank(n, width=512):
            return ps[:, n, 0:width]

        def agg_group(L, c, d):
            return 4 * (L - 1) + 2 * c + d

        block = ctx.enter_context(nc.Block())

        @block.sync
        def _(sp):
            for s, v in enumerate(V):
                for g in range(B):
                    t, q = divmod(g, v["per_tile"])
                    at = slice(q * v["nodes"], (q + 1) * v["nodes"])
                    sp.dma_start(v["x"][at, t, :], x_d[g, 0:v["nodes"], :]).then_inc(v_x_in, 16)
            sp.dma_start(ident[:, :], t_in["identity"]).then_inc(const_in, 16)
            for s, v in enumerate(V):
                sp.dma_start(v["mask"][:, :, :], t_in[f"pair_mask_{s}"]).then_inc(const_in, 16)
                sp.dma_start(v["member"][:, :], t_in[f"member_mask_{s}"]).then_inc(const_in, 16)
            sp.wait_ge(v_adj_zero, len(V))
            for s, v in enumerate(V):
                for g in range(B):
                    t, q = divmod(g, v["per_tile"])
                    at = slice(q * v["nodes"], (q + 1) * v["nodes"])
                    sp.dma_start(v["adj"][at, t, at], adj_d[g, 0:v["nodes"], 0:v["nodes"]]).then_inc(v_adj_in, 16)

            def load_group(n):
                sp.dma_start(v_w1[:, n % 2], t_in["L0_gnn_W1"][n].rearrange("(d p) e -> p d e", p=P)).then_inc(v_w_in[n % 2], 16)
                sp.dma_start(v_w2[:, n % 2], t_in["L0_gnn_W2"][n].rearrange("(k p) e -> p k e", p=P)).then_inc(v_w_in[n % 2], 16)

            load_group(0)
            load_group(1)
            for tile_, name in ((stage_a, "L1_gnn_weight"), (stage_b, "L2_gnn_weight"), (stage_1, "L3_gnn_W1"),
                                (stage_2, "L3_gnn_W2")):
                sp.dma_start(tile_[:, :, :], t_in[name].rearrange("(d p) e -> p d e", p=P)).then_inc(w_in, 16)
            group_at = 0
            for s, v in enumerate(V):
                for n in range(v["ng"]):
                    group_at += 1
                    if group_at + 1 < NG:
                        sp.wait_ge(v_done, group_at)
                        load_group(group_at + 1)
                sp.wait_ge(v_done, group_at)
                for g in range(B):
                    t, q = divmod(g, v["per_tile"])
                    at = slice(q * v["nodes"], (q + 1) * v["nodes"])
                    sp.dma_start(scratch[g, 0:v["nodes"], :], v["acc"][at, t, :]).then_inc(v_stored, 16)
                if s + 1 < len(V):
                    w = V[s + 1]
                    sp.wait_ge(v_stored, 16 * B * (s + 1))
                    for g in range(B):
                        t, q = divmod(g, w["per_tile"])
                        at = slice(q * w["nodes"], (q + 1) * w["nodes"])
                        sp.dma_start(w["acc"][at, t, :], scratch[g, 0:w["nodes"], :]).then_inc(v_acc_in, 16)
            sp.wait_ge(v_stored, 16 * B * len(V))
            sp.wait_ge(w_ok, 4)

            def load_adj(graph, tile, first):
                s = tile % 2
                if not first:
                    before = graph * 2 * NT + 2 * (tile - 2) + 2
                    wait_apart(sp, tr_mm, before)
                    wait_apart(sp, rowsum_ok, graph * NT + tile - 1)
                sp.dma_start(raw[:, s, :], adj_d[graph, tile * P:(tile + 1) * P, :] if isinstance(graph, int)
                             else adj_d[bass.ds(graph, 1), tile * P:(tile + 1) * P, :].rearrange("a p n -> (a p) n")
                             ).then_inc(adj_in[s], 16)

            def rows(tensor, graph, lo, hi):
                if isinstance(graph, int):
                    return tensor[graph, lo:hi, :]
                return tensor[bass.ds(graph, 1), lo:hi, :].rearrange("a p n -> (a p) n")

            def do(step, i, j, first):
                kind = step[0]
                nxt = i + 1
                if kind == "load_x":
                    half = step[1]
                    if not (first and isinstance(i, int) and i < 0):
                        wait_apart(sp, tail_ok, upto(i, NT, (half + 1) * TH))
                    if half == 0:
                        sp.dma_start(x[0:F0, 0, :], rows(scratch, nxt, 0, F0)).then_inc(x_in[0], 16)
                        sp.dma_start(x[F0:P, 0, :], rows(x_d, nxt, F0, P)).then_inc(x_in[0], 16)
                        sp.dma_start(x[:, 1:TH, :], rows(x_d, nxt, P, HALF).rearrange("(t p) d -> p t d", p=P)).then_inc(x_in[0], 16)
                    else:
                        sp.dma_start(x[:, TH:NT, :], rows(x_d, nxt, HALF, N).rearrange("(t p) d -> p t d", p=P)).then_inc(x_in[1], 16)
                elif kind == "tr":
                    _, ahead, tile, g = step
                    if g == 1:
                        graph = i + ahead
                        if isinstance(i, int) and i == -1 and tile < 1:
                            load_adj(0, 0, True)
                            load_adj(0, 1, True)
                        if tile + 2 < NT:
                            load_adj(graph, tile + 2, False)
                        elif isinstance(graph, int) and graph == B - 1:
                            pass
                        else:
                            load_adj(graph + 1, tile + 2 - NT, False)
                elif kind == "result":
                    c = step[1]
                    if not (isinstance(j, int) and j == 0 and c == 0):
                        if c > 0:
                            wait_apart(sp, stored, upto(j, 16 * NC, 16 * c))
                    wait_apart(sp, res_ok, upto(j, NC, c + 1))
                    sp.dma_start(rows(out, j, c * CH, (c + 1) * CH).rearrange("(t p) d -> p t d", p=P),
                                 tail[:, 2 * c:2 * c + 2, :]).then_inc(stored, 16)

            run(sp, do)
            sp.wait_ge(stored, 16 * NC * B)

        @block.gpsimd
        def _(pool):
            for v in V:
                nc.gpsimd.memset(v["adj"][:, :, :], 0.0).then_inc(v_adj_zero, 1)
            nc.gpsimd.memset(ones[:, :], 1.0).then_inc(const_ok, 1)
            nc.gpsimd.memset(minus_half[:, :], -0.5).then_inc(const_ok, 1)
            with nc.allow_non_contiguous_dma(reason="small vectors, once"):
                for col, src in ((b1_col, "L3_gnn_b1"), (rmsw_col, "L3_gnn_rms_weight")):
                    pool.dma_start(col[:, :], t_in[src].rearrange("(k p) -> p k", p=P)).then_inc(vectors_in, 16)
                pool.dma_start(v_b1[:, :, :], t_in["L0_gnn_b1"].rearrange("g (k p) -> p g k", p=P)).then_inc(vectors_in, 16)
                for row, src in ((bias1, "L1_gnn_bias"), (bias2, "L2_gnn_bias"), (bias3, "L3_gnn_b2")):
                    pool.dma_start(row[:, :], t_in[src].rearrange("(a n) -> a n", a=1).broadcast_to([P, D])).then_inc(vectors_in, 16)
                pool.dma_start(v_b2[:, :, :].rearrange("p g n -> p (g n)"),
                               t_in["L0_gnn_b2"].rearrange("(a g) n -> a (g n)", a=1).broadcast_to([P, NG * D])).then_inc(vectors_in, 16)
                pool.dma_start(v_fw[:, 0, :], t_in["L0_gnn_fusion_w"].rearrange("(a n) -> a n", a=1).broadcast_to([P, NG])).then_inc(vectors_in, 16)
                pool.dma_start(epsilon_col[:, :], t_in["L3_gnn_epsilon"].rearrange("(a n) -> a n", a=1).broadcast_to([P, 1])).then_inc(vectors_in, 16)
            pool.wait_ge(const_ok, 2)
            for s, v in enumerate(V):
                r, n = v["rows"], v["ng"] * v["tiles"]
                pool.wait_ge(v_var_ok, s + 1)
                for t in range(v["tiles"]):
                    last = nc.gpsimd.tensor_tensor(v["rs"][:, 1, t:t + 1], v["rs"][:, 0, t:t + 1], minus_half[0:r, 0:1], ALU.pow)
                last.then_inc(v_rstd, 1)
                pool.wait_ge(v_deg_safe, s + 1)
                for k in range(0, n, 8):
                    m = min(8, n - k)
                    last = nc.gpsimd.tensor_tensor(v["deg"][:, 2, k:k + m], v["deg"][:, 1, k:k + m], minus_half[0:r, 0:m], ALU.pow)
                last.then_inc(v_deg_pow, 1)
            pool.wait_ge(v_stored, 16 * B * len(V))
            pool.wait_ge(w_ok, 4)

            def do(step, i, j, first):
                kind = step[0]
                pro = isinstance(i, int) and i < 0
                if kind == "rstd":
                    _, L, half = step
                    b = i + 1 if L == 1 else i
                    wait_apart(pool, stats_ok, upto(b, 3 * NT, (L - 1) * NT + (half + 1) * TH))
                    k = 2 * (L - 1) + half
                    if not (pro and half == 0):
                        wait_apart(pool, rstd_ok, upto(b, 6, k))
                    nc.gpsimd.tensor_scalar(ve[:, :], mv[:, half * TH:(half + 1) * TH, 1], LN_EPS, None, ALU.add).then_inc(ve_ok, 1)
                    pool.wait_ge(ve_ok, upto(b, 6, k + 1))
                    if not (pro and half == 0):
                        pool.wait_ge(y_ok, upto(b, 3 * NT, (L - 1) * NT + half * TH))
                    nc.gpsimd.tensor_tensor(rstd[:, :], ve[:, :], minus_half[:, 0:TH], ALU.pow).then_inc(rstd_ok, 1)
                elif kind == "hs":
                    pair = step[1]
                    if pair == 0:
                        wait_apart(pool, deg_ok, upto(i, 1, 1))
                    if pair > 0 or not first:
                        wait_apart(pool, ht_mm, upto(i, TH, pair))
                    wait_apart(pool, y_ok, upto(i, 3 * NT, NT + 2 * pair + 2))
                    for t in (2 * pair, 2 * pair + 1):
                        nc.gpsimd.tensor_scalar(hs[:, t % 2, :], y[:, t % TH, :], 0.0, deg[:, 1, t:t + 1],
                                                ALU.max, ALU.mult).then_inc(hs_ok, 1)
                elif kind == "sum_fix":
                    t = step[1]
                    n = upto(i, 3 * NT, 3 * t)
                    if t >= 2 or not first:
                        wait_apart(pool, fix_ok, upto(i, NT, t - 1))
                    dh, dl = adj_hi[:, t, t * P:(t + 1) * P], adj_lo[:, t, t * P:(t + 1) * P]
                    fx = fixed[:, t % 2, :]
                    nc.gpsimd.tensor_scalar(fx, ident[:, :], epsilon_col[:, 0:1], None, ALU.mult).then_inc(fsum_ok, 1)
                    for q, part in enumerate((f(dh), f(dl))):
                        pool.wait_ge(fsum_ok, n + q + 1)
                        nc.gpsimd.tensor_tensor(fx, fx, part, ALU.add).then_inc(fsum_ok, 1)
                elif kind == "xb":
                    t = step[1]
                    pool.wait_ge(y_ok, upto(i, 3 * NT, t + 1))
                    nc.gpsimd.tensor_tensor(x[:, t, :], x[:, t, :], bias1[:, :], ALU.add).then_inc(xb_ok, 1)
                elif kind == "tail":
                    t = step[1]
                    if not first and t % 2 == 0:
                        pool.wait_ge(stored, upto(i - 1, 16 * NC, 16 * (t // 2 + 1)))
                    pool.wait_ge(y_ok, upto(i, 3 * NT, 2 * NT + t + 1))
                    nc.gpsimd.tensor_tensor(tail[:, t, :], x[:, t, :], bias3[:, :], ALU.add).then_inc(tail_ok, 1)
                elif kind == "up":
                    _, c, p = step
                    n = upto(j, 2 * PAIRS * NC, 2 * (PAIRS * c + p))
                    pool.wait_ge(sq_ok, upto(j, PAIRS * NC, PAIRS * c + p + 1))
                    if p == 0:
                        if not (isinstance(j, int) and j == 0 and c == 0):
                            pool.wait_ge(col_mm, upto(j, NC, c))
                        nc.gpsimd.tensor_tensor(sq_sum[:, :], sq[:, 0, :], sq[:, 1, :], ALU.add).then_inc(sum_ok, 2)
                    else:
                        for q in range(2):
                            pool.wait_ge(sum_ok, n + q)
                            nc.gpsimd.tensor_tensor(sq_sum[:, :], sq_sum[:, :], sq[:, q, :], ALU.add).then_inc(sum_ok, 1)
                elif kind == "rms":
                    c = step[1]
                    pool.wait_ge(msq_ok, upto(j, NC, c + 1))
                    if c > 0:
                        pool.wait_ge(rms_rows_ok, upto(j, NC, c))
                    nc.gpsimd.tensor_tensor(rms[:, :], msq[:, :], minus_half[:, 0:2], ALU.pow).then_inc(rms_ok, 1)

            run(pool, do)

        @block.scalar
        def _(act):
            act.wait_ge(v_fw_sub, 1)
            nc.scalar.activation(v_fw[:, 1, :], v_fw[:, 0, :], ACT.Exp, bias=v_red[:, 1:2], accum_out=v_red[:, 2:3]).then_inc(v_fw_exp, 1)
            act.wait_ge(w_in, 64)
            for hi, st_ in ((wa_hi, stage_a), (wb_hi, stage_b), (w1_hi, stage_1), (w2_hi, stage_2)):
                nc.scalar.activation(hi[:, :, :], st_[:, :, :], ACT.Copy).then_inc(w_hi_ok, 1)
            done_tr = 0
            gidx = 0
            for s, v in enumerate(V):
                r, tiles = v["rows"], v["tiles"]
                for n in range(v["ng"] * tiles):
                    done_tr += 1
                    act.wait_ge(v_tr, done_tr)
                    g, t = divmod(n, tiles)
                    nc.scalar.activation(v["an_t"][:, g, t, :], ps[0:r, done_tr % 2, 0:r], ACT.Copy,
                                         scale=v["deg"][:, 3, n:n + 1]).then_inc(v_ant, 1)
                for n in range(v["ng"]):
                    g = v["groups"][n]
                    cols = r * tiles
                    for d in range(ND):
                        act.wait_ge(v_y_mm, ND * gidx + d + 1)
                        if gidx:
                            act.wait_ge(v_hid_mm, NK0 * gidx)
                        nc.scalar.activation(v_yt[:, d, 0:cols], ps[:, 2 + d, 0:cols], ACT.Copy).then_inc(v_y_ok, 1)
                    for k in range(NK0):
                        act.wait_ge(v_hid_mm, NK0 * gidx + k + 1)
                        if gidx:
                            act.wait_ge(v_done, gidx)
                        nc.scalar.activation(v_hid[:, k, 0:cols], ps[:, 4 + k % 2, 0:cols], ACT.Relu,
                                             bias=v_b1[:, g, k:k + 1]).then_inc(v_hid_ok, 1)
                    gidx += 1
            act.wait_ge(v_stored, 16 * B * len(V))
            act.wait_ge(w_ok, 4)

            def do(step, i, j, first):
                kind = step[0]
                pro = isinstance(i, int) and i < 0
                if kind == "tr":
                    _, ahead, tile, g = step
                    b = i + ahead
                    n = 2 * tile + g
                    act.wait_ge(tr_mm, upto(b, 2 * NT, n + 1))
                    if not pro and g == 0 and tile % TH == 0:
                        if ahead:
                            act.wait_ge(agg_mm, upto(i, 12, 10))
                        elif not first:
                            act.wait_ge(agg_mm, upto(i, 12, 0))
                    nc.scalar.activation(adj_hi[:, g * TH:(g + 1) * TH, tile * P:(tile + 1) * P],
                                         bank(RING[n % 2]).rearrange("p (a b) -> p a b", b=P), ACT.Copy).then_inc(adj_hi_ok, 1)
                elif kind == "split":
                    _, L, t = step
                    n = (L - 1) * NT + t
                    act.wait_ge(y_ok, upto(i, 3 * NT, n + 1))
                    if t == 0 and not (first and L == 1):
                        act.wait_ge(agg_mm, upto(i, 12, 4 * (L - 1)))
                    nc.scalar.activation(h_hi[:, t, :], y[:, t % TH, :], ACT.Relu).then_inc(h_hi_ok, 1)
                elif kind == "pt":
                    _, L, c, d = step
                    n = agg_group(L, c, d)
                    act.wait_ge(agg_mm, upto(i, 12, n + 1))
                    if L < 3:
                        if c == 1:
                            act.wait_ge(w_mm, upto(i, 8, 4 * (L - 1) + 2))
                        elif L == 2:
                            act.wait_ge(w_mm, upto(i, 8, 4))
                        elif not first:
                            act.wait_ge(w_mm, upto(i, 8, 0))
                        nc.scalar.activation(pt_hi[:, d, :], bank(AGG[n % 3]), ACT.Copy).then_inc(pt_hi_ok, 1)
                    else:
                        if not first and c == 0 and d == 0:
                            act.wait_ge(ac_ok, upto(i, NC, 0))
                        nc.scalar.activation(agg[:, d, c * HALF:(c + 1) * HALF], bank(AGG[n % 3]), ACT.Copy).then_inc(agg_ok, 1)
                elif kind == "ht" and step[1] % 2:
                    c = step[1] // 2
                    act.wait_ge(ht_mm, upto(i, TH, 2 * c + 2))
                    if c == 1:
                        act.wait_ge(w_mm, upto(i, 8, 6))
                    elif not first:
                        act.wait_ge(w_mm, upto(i, 8, 0))
                    for d in range(ND):
                        nc.scalar.activation(ht_hi[:, d, :], bank(RING[d]), ACT.Copy).then_inc(ht_hi_ok, 1)
                elif kind == "up":
                    _, c, p = step
                    n = PAIRS * c + p
                    act.wait_ge(up_mm, upto(j, PAIRS * NC, n + 1))
                    if not (isinstance(j, int) and j == 0 and c == 0):
                        act.wait_ge(act_ok, upto(j, PAIRS * NC, n - PAIRS + p * 0 + 1))
                    src = bank(HID[p % 2]).rearrange("p (a b) -> p a b", b=CH)
                    for q in range(2):
                        k = 2 * p + q
                        last = nc.scalar.activation(hid[:, k, :], src[:, q, :], ACT.Identity, bias=b1_col[:, k:k + 1])
                    last.then_inc(hid_ok, 1)
                    if not (isinstance(j, int) and j == 0 and n == 0):
                        act.wait_ge(sum_ok, upto(j, 2 * PAIRS * NC, 2 * n))
                    for q in range(2):
                        k = 2 * p + q
                        last = nc.scalar.activation(sq[:, q, :], src[:, q, :], ACT.Square, bias=b1_col[:, k:k + 1])
                    last.then_inc(sq_ok, 1)
                elif kind == "fix":
                    t = step[1]
                    act.wait_ge(fsum_ok, upto(i, 3 * NT, 3 * t + 3))
                    if t == 0:
                        act.wait_ge(agg_mm, upto(i, 12, 8))
                    nc.scalar.activation(adj_hi[:, t, t * P:(t + 1) * P], fixed[:, t % 2, :], ACT.Copy).then_inc(fix_hi_ok, 1)
                elif kind == "silu":
                    _, c, p = step
                    n = PAIRS * c + p
                    act.wait_ge(scaled_ok, upto(j, PAIRS * NC, n + 1))
                    for q in range(2):
                        k = 2 * p + q
                        last = nc.scalar.activation(hid[:, k, :], hid[:, k, :], ACT.Silu, scale=rmsw_col[:, k:k + 1])
                    last.then_inc(silu_ok, 1)
                    act.wait_ge(silu_ok, upto(j, PAIRS * NC, n + 1))
                    if p >= 2:
                        act.wait_ge(down_mm, upto(j, PAIRS * NC, n - 1))
                    elif c > 0:
                        act.wait_ge(down_mm, upto(j, PAIRS * NC, PAIRS * c))
                    nc.scalar.activation(act_hi[:, p % 2], hid[:, 2 * p:2 * p + 2, :], ACT.Copy).then_inc(act_hi_ok, 1)

            run(act, do)

        @block.vector
        def _(dve):
            vd = [0]

            def link(ins):
                vd[0] += 1
                ins.then_inc(v_dve, 1)
                dve.wait_ge(v_dve, vd[0])

            dve.wait_ge(const_in, 16 * (1 + 2 * len(V)))
            dve.wait_ge(vectors_in, 16 * 9)
            link(nc.vector.reduce_max(v_red[:, 0:1], v_fw[:, 0, :], axis=AX.X))
            dve.wait_ge(const_ok, 2)
            nc.vector.tensor_scalar(v_red[:, 1:2], v_red[:, 0:1], -1.0, None, ALU.mult).then_inc(v_fw_sub, 1)
            dve.wait_ge(v_x_in, 16 * B * len(V))
            for s, v in enumerate(V):
                for t in range(v["tiles"]):
                    last = nc.vector.bn_stats(v["st"][:, t, :], v["x"][:, t, :])
                link(last)
                for t in range(v["tiles"]):
                    last = nc.vector.bn_aggr(v["mv"][:, t, :], v["st"][:, t, :])
                link(last)
                nc.vector.tensor_scalar(v["rs"][:, 0, :], v["mv"][:, :, 1], LN_EPS, None, ALU.add).then_inc(v_var_ok, 1)
            dve.wait_ge(v_adj_in, 16 * B * len(V))
            for s, v in enumerate(V):
                r, tiles, ng = v["rows"], v["tiles"], v["ng"]
                adj0, ag, dg = v["adj"], v["ag"], v["deg"]
                link(nc.vector.tensor_tensor(adj0[:, :, :], adj0[:, :, :], ident[0:r, 0:r].unsqueeze(1).broadcast_to([r, tiles, r]), ALU.add))
                for n in range(ng):
                    last = nc.vector.tensor_tensor(ag[:, n, :, :], adj0[:, :, :], v["mask"][:, n, :].unsqueeze(1).broadcast_to([r, tiles, r]), ALU.mult)
                link(last)
                agf = ag[:, :, :, :].rearrange("p g t m -> p (g t) m")
                link(nc.vector.reduce_sum(dg[:, 0, :], agf, axis=AX.X))
                link(nc.vector.tensor_scalar(dg[:, 3, :], dg[:, 0, :], 0.0, None, ALU.is_equal))
                nc.vector.tensor_tensor(dg[:, 1, :], dg[:, 0, :], dg[:, 3, :], ALU.add).then_inc(v_deg_safe, 1)
                dve.wait_ge(v_deg_safe, s + 1)
                link(nc.vector.tensor_scalar(dg[:, 0, :], dg[:, 3, :], -1.0, 1.0, ALU.mult, ALU.add))
                dve.wait_ge(v_deg_pow, s + 1)
                link(nc.vector.tensor_tensor(dg[:, 3, :], dg[:, 2, :], dg[:, 0, :], ALU.mult))
                nc.vector.tensor_tensor(agf, agf, dg[:, 3, :].unsqueeze(2).broadcast_to([r, ng * tiles, r]), ALU.mult).then_inc(v_ag_ok, 1)
                dve.wait_ge(v_rstd, s + 1)
                for t in range(tiles):
                    last = nc.vector.tensor_scalar(v["h"][:, t, :], v["x"][:, t, :], v["mv"][:, t, 0:1], v["rs"][:, 1, t:t + 1],
                                                   ALU.subtract, ALU.mult)
                link(last)
                if s == 0:
                    nc.vector.tensor_copy(v["acc"][:, :, :], v["x"][:, :, :])
                nc.vector.tensor_scalar(v["h"][:, :, :], v["h"][:, :, :], 0.0, None, ALU.max).then_inc(v_h_ok, 1)
            dve.wait_ge(v_fw_exp, 1)
            link(nc.vector.reciprocal(v_red[:, 3:4], v_red[:, 2:3]))
            link(nc.vector.tensor_scalar(v_fw[:, 3, :], v_fw[:, 1, :], v_red[:, 3:4], None, ALU.mult))
            for v in V:
                g0, ng, r = v["groups"][0], v["ng"], v["rows"]
                last = nc.vector.tensor_tensor(v["wm"][:, :], v["member"][:, :], v_fw[0:r, 3, g0:g0 + ng], ALU.mult)
            link(last)
            for n, (hi, lo, st_) in enumerate(((wa_hi, wa_lo, stage_a), (wb_hi, wb_lo, stage_b), (w1_hi, w1_lo, stage_1), (w2_hi, w2_lo, stage_2))):
                dve.wait_ge(w_hi_ok, n + 1)
                nc.vector.tensor_tensor(lo[:, :, :], st_[:, :, :], f(hi[:, :, :]), ALU.subtract).then_inc(w_ok, 1)
            use, gidx = 0, 0
            for s, v in enumerate(V):
                r, tiles = v["rows"], v["tiles"]
                if s:
                    dve.wait_ge(v_acc_in, 16 * B)
                for n in range(v["ng"]):
                    g = v["groups"][n]
                    for t in range(tiles):
                        use += 1
                        dve.wait_ge(v_ring_mm, use)
                        nc.vector.tensor_copy(v_s2[0:r, t, :], ps[0:r, 6 + use % 2, 0:D]).then_inc(v_ring_free, 1)
                    for t in range(tiles):
                        use += 1
                        dve.wait_ge(v_ring_mm, use)
                        nc.vector.tensor_tensor(v_u[0:r, t % 2, :], ps[0:r, 6 + use % 2, 0:D], v_b2[0:r, g, :], ALU.add).then_inc(v_ring_free, 1)
                        dve.wait_ge(v_ring_free, use)
                        link(nc.vector.tensor_scalar(v_u[0:r, t % 2, :], v_u[0:r, t % 2, :], 0.0, v["wm"][:, n:n + 1], ALU.max, ALU.mult))
                        last = nc.vector.tensor_tensor(v["acc"][:, t, :], v["acc"][:, t, :], v_u[0:r, t % 2, :], ALU.add)
                        if t + 1 < tiles:
                            link(last)
                    gidx += 1
                    last.then_inc(v_done, 1)
                    dve.wait_ge(v_done, gidx)
            dve.wait_ge(v_stored, 16 * B * len(V))

            def do(step, i, j, first):
                kind = step[0]
                pro = isinstance(i, int) and i < 0
                if kind == "tr":
                    _, ahead, tile, g = step
                    b = i + ahead
                    n = 2 * tile + g
                    if g == 0:
                        dve.wait_ge(adj_in[tile % 2], upto(b, 16 * TH, 16 * (tile // 2 + 1)))
                        if tile == 0 and not pro:
                            dve.wait_ge(deg_ok, upto(b, 1, 0))
                        nc.vector.reduce_sum(deg[:, 0, tile:tile + 1], raw[:, tile % 2, :], axis=AX.X).then_inc(rowsum_ok, 1)
                    dve.wait_ge(adj_hi_ok, upto(b, 2 * NT, n + 1))
                    nc.vector.tensor_tensor(adj_lo[:, g * TH:(g + 1) * TH, tile * P:(tile + 1) * P],
                                            bank(RING[n % 2]).rearrange("p (a b) -> p a b", b=P),
                                            f(adj_hi[:, g * TH:(g + 1) * TH, tile * P:(tile + 1) * P]), ALU.subtract).then_inc(ring_free, 1)
                elif kind == "deg":
                    dve.wait_ge(rowsum_ok, upto(i, NT, NT))
                    if not first:
                        dve.wait_ge(hs_ok, upto(i, NT, 0))
                    nc.vector.tensor_scalar(deg[:, 1, :], deg[:, 0, :], DEG_EPS, None, ALU.add).then_inc(deg_ok, 1)
                    dve.wait_ge(deg_ok, upto(i, 1, 1))
                    nc.vector.reciprocal(inv_deg[:, :], deg[:, 1, :]).then_inc(inv_ok, 1)
                    dve.wait_ge(inv_ok, upto(i, 1, 1))
                elif kind == "stats":
                    _, L, t = step
                    if t % 2 == 0:
                        b = i + 1
                        if t == 0:
                            dve.wait_ge(x_in[0], upto(b, 16 * X_DMAS, 16 * X_DMAS))
                        if t == TH:
                            dve.wait_ge(x_in[1], upto(b, 16, 16))
                        layer_stats(b, t, t, pro)
                elif kind == "norm":
                    _, L, t = step
                    half = t // TH
                    b = i + 1 if (L == 1 and half == 0) else i
                    n = (L - 1) * NT + t
                    if t % TH == 0:
                        dve.wait_ge(rstd_ok, upto(b, 6, 2 * (L - 1) + half + 1))
                        if L == 2 and half == 1:
                            dve.wait_ge(hs_ok, upto(b, NT, TH))
                        if L == 3 and half == 0:
                            dve.wait_ge(hs_ok, upto(b, NT, NT))
                    if not (pro and n < TH):
                        dve.wait_ge(h_ok, upto(b, 3 * NT, n - TH + 1))
                    nc.vector.tensor_scalar(y[:, t % TH, :], x[:, t, :], mv[:, t, 0:1], rstd[:, t % TH:t % TH + 1],
                                            ALU.subtract, ALU.mult).then_inc(y_ok, 1)
                elif kind == "split":
                    _, L, t = step
                    n = (L - 1) * NT + t
                    dve.wait_ge(h_hi_ok, upto(i, 3 * NT, n + 1))
                    nc.vector.scalar_tensor_tensor(out=h_lo[:, t, :], in0=y[:, t % TH, :], scalar=0.0, in1=f(h_hi[:, t, :]),
                                                   op0=ALU.max, op1=ALU.subtract).then_inc(h_ok, 1)
                elif kind == "pt":
                    _, L, c, d = step
                    if L < 3:
                        n = agg_group(L, c, d)
                        dve.wait_ge(pt_hi_ok, upto(i, 8, n + 1))
                        nc.vector.tensor_tensor(pt_lo[:, d, :], bank(AGG[n % 3]), f(pt_hi[:, d, :]), ALU.subtract).then_inc(pt_ok, 1)
                elif kind == "ht" and step[1] % 2:
                    c = step[1] // 2
                    for d in range(ND):
                        dve.wait_ge(ht_hi_ok, upto(i, 4, 2 * c + d + 1))
                        nc.vector.tensor_tensor(ht_lo[:, d, :], bank(RING[d]), f(ht_hi[:, d, :]), ALU.subtract).then_inc(ring_free, 1)
                elif kind == "w":
                    _, L, c, p = step
                    u = ring_use(i, ring_of["w", L, c] + p)
                    dve.wait_ge(w_mm, upto(i, 8, 4 * (L - 1) + 2 * c + p + 1))
                    t0 = c * TH + 2 * p
                    o = bank(RING[p]).rearrange("p (a b) -> p a b", b=D)
                    if L == 1:
                        dve.wait_ge(xb_ok, upto(i, NT, t0 + 2))
                        nc.vector.tensor_tensor(x[:, t0:t0 + 2, :], o, x[:, t0:t0 + 2, :], ALU.add).then_inc(ring_free, 1)
                    else:
                        for q in range(2):
                            last = nc.vector.scalar_tensor_tensor(out=o[:, q, :], in0=o[:, q, :], scalar=inv_deg[:, t0 + q:t0 + q + 1],
                                                                  in1=bias2[:, :], op0=ALU.mult, op1=ALU.add)
                        last.then_inc(relu_ok, 1)
                        dve.wait_ge(relu_ok, upto(i, NT // 2, t0 // 2 + 1))
                        dve.wait_ge(y_ok, upto(i, 3 * NT, NT + t0 + 2))
                        nc.vector.scalar_tensor_tensor(out=x[:, t0:t0 + 2, :], in0=o, scalar=0.0, in1=x[:, t0:t0 + 2, :],
                                                       op0=ALU.max, op1=ALU.add).then_inc(ring_free, 1)
                    dve.wait_ge(ring_free, u + 1)
                    layer_stats(i, L * NT + t0, t0, False)
                elif kind == "fix":
                    t = step[1]
                    dh, dl = adj_hi[:, t, t * P:(t + 1) * P], adj_lo[:, t, t * P:(t + 1) * P]
                    dve.wait_ge(fix_hi_ok, upto(i, NT, t + 1))
                    nc.vector.tensor_tensor(dl, fixed[:, t % 2, :], f(dh), ALU.subtract).then_inc(fix_ok, 1)
                elif kind == "chunk_split":
                    c = step[1]
                    if c % 2 == 0:
                        dve.wait_ge(agg_ok, upto(j, 4, 2 * (c // 2) + 2))
                    if c == 0 and not (isinstance(j, int) and j == 0):
                        dve.wait_ge(rms_ok, upto(j, NC, 0))
                        dve.wait_ge(bcast_mm, upto(j, NC, 0))
                    if not (isinstance(j, int) and j == 0 and c == 0):
                        dve.wait_ge(up_mm, upto(j, PAIRS * NC, PAIRS * c))
                    src = agg[:, :, c * CH:(c + 1) * CH]
                    nc.vector.tensor_copy(ac_hi[:, :, :], src).then_inc(ac_hi_ok, 1)
                    dve.wait_ge(ac_hi_ok, upto(j, NC, c + 1))
                    nc.vector.tensor_tensor(ac_lo[:, :, :], src, f(ac_hi[:, :, :]), ALU.subtract).then_inc(ac_ok, 1)
                elif kind == "sumsq":
                    c = step[1]
                    dve.wait_ge(col_mm, upto(j, NC, c + 1))
                    if c > 0:
                        dve.wait_ge(rms_ok, upto(j, NC, c))
                    nc.vector.tensor_scalar(msq[:, :], bank(HID[0], 2), 1.0 / H, RMS_EPS, ALU.mult, ALU.add).then_inc(msq_ok, 1)
                elif kind == "rms_rows":
                    c = step[1]
                    dve.wait_ge(rms_ok, upto(j, NC, c + 1))
                    if c > 0:
                        dve.wait_ge(bcast_mm, upto(j, NC, c))
                    for q in range(2):
                        last = nc.vector.tensor_scalar(rms_rows[:, q, :], ident[:, :], 0.0, rms[:, q:q + 1], ALU.mult, ALU.add)
                    last.then_inc(rms_rows_ok, 1)
                elif kind == "scale":
                    _, c, p = step
                    dve.wait_ge(bcast_mm, upto(j, NC, c + 1))
                    dve.wait_ge(hid_ok, upto(j, PAIRS * NC, PAIRS * c + p + 1))
                    part = hid[:, 2 * p:2 * p + 2, :]
                    nc.vector.tensor_tensor(part, part, bank(HID[1], CH).unsqueeze(1).broadcast_to([P, 2, CH]), ALU.mult).then_inc(scaled_ok, 1)
                elif kind == "act":
                    _, c, p = step
                    n = PAIRS * c + p
                    dve.wait_ge(act_hi_ok, upto(j, PAIRS * NC, n + 1))
                    nc.vector.tensor_tensor(act_lo[:, p % 2], hid[:, 2 * p:2 * p + 2, :], f(act_hi[:, p % 2]), ALU.subtract).then_inc(act_ok, 1)
                elif kind == "result":
                    c = step[1]
                    dve.wait_ge(down_mm, upto(j, PAIRS * NC, PAIRS * (c + 1)))
                    dve.wait_ge(tail_ok, upto(j, NT, 2 * c + 2))
                    t2 = tail[:, 2 * c:2 * c + 2, :]
                    nc.vector.tensor_tensor(t2, bank(DOWN).rearrange("p (a b) -> p a b", b=D), t2, ALU.add).then_inc(res_ok, 1)

            def layer_stats(b, n, t, pro):
                if not pro and n == 0:
                    dve.wait_ge(y_ok, upto(b, 3 * NT, 0))
                for q in range(2):
                    last = nc.vector.bn_stats(st[:, t + q, :], x[:, t + q, :])
                last.then_inc(bn_ok, 1)
                wait_apart(dve, bn_ok, upto(b, 3 * NT // 2, n // 2 + 1))
                for q in range(2):
                    nc.vector.bn_aggr(mv[:, t + q, :], st[:, t + q, :]).then_inc(stats_ok, 1)

            run(dve, do)

        @block.tensor
        def _(pe):
            pe.wait_ge(const_in, 16 * (1 + 2 * len(V)))
            pe.wait_ge(const_ok, 2)
            done_tr, gidx, use = 0, 0, 0
            for s, v in enumerate(V):
                r, tiles = v["rows"], v["tiles"]
                cols = r * tiles
                pe.wait_ge(v_ag_ok, s + 1)
                for n in range(v["ng"] * tiles):
                    done_tr += 1
                    if done_tr > 2:
                        pe.wait_ge(v_ant, done_tr - 2)
                    g, t = divmod(n, tiles)
                    nc.tensor.transpose(ps[0:r, done_tr % 2, 0:r], v["ag"][:, g, t, :], ident[0:r, 0:r]).then_inc(v_tr, 1)
                pe.wait_ge(v_h_ok, s + 1)
                pe.wait_ge(v_ant, done_tr)
                for n in range(v["ng"]):
                    for d in range(ND):
                        for t in range(tiles):
                            last = nc.tensor.matmul(ps[:, 2 + d, t * r:(t + 1) * r], v["h"][:, t, d * P:(d + 1) * P], v["an_t"][:, n, t, :],
                                                    start=True, stop=True)
                        last.then_inc(v_y_mm, 1)
                    pe.wait_ge(v_w_in[gidx % 2], 32 * (gidx // 2 + 1))
                    pe.wait_ge(v_y_ok, ND * (gidx + 1))
                    for k in range(NK0):
                        if NK0 * gidx + k >= 2:
                            pe.wait_ge(v_hid_ok, NK0 * gidx + k - 1)
                        for d in range(ND):
                            last = nc.tensor.matmul(ps[:, 4 + k % 2, 0:cols], v_w1[:, gidx % 2, d, k * P:(k + 1) * P], v_yt[:, d, 0:cols],
                                                    start=(d == 0), stop=(d == ND - 1))
                        last.then_inc(v_hid_mm, 1)
                    pe.wait_ge(v_hid_ok, NK0 * (gidx + 1))
                    for t in range(tiles):
                        use += 1
                        if use > 2:
                            pe.wait_ge(v_ring_free, use - 2)
                        for k in range(NK0):
                            last = nc.tensor.matmul(ps[0:r, 6 + use % 2, 0:D], v_hid[:, k, t * r:(t + 1) * r], v_w2[:, gidx % 2, k, :],
                                                    start=(k == 0), stop=(k == NK0 - 1))
                        last.then_inc(v_ring_mm, 1)
                    for t in range(tiles):
                        use += 1
                        pe.wait_ge(v_ring_free, max(use - 2, use - 1 - t - (tiles - 1 - t)))
                        nc.tensor.matmul(ps[0:r, 6 + use % 2, 0:D], v["an_t"][:, n, t, :], v_s2[0:r, t, :], start=True, stop=True).then_inc(v_ring_mm, 1)
                    gidx += 1
            pe.wait_ge(v_stored, 16 * B * len(V))
            pe.wait_ge(w_ok, 4)

            def three(o, w_hi, w_lo, m_hi, m_lo, start, stop, skip=False):
                nc.tensor.matmul(o, w_hi, m_hi, start=start, stop=False, skip_group_check=skip)
                nc.tensor.matmul(o, w_hi, m_lo, start=False, stop=False, skip_group_check=skip)
                return nc.tensor.matmul(o, w_lo, m_hi, start=False, stop=stop, skip_group_check=skip)

            def ring_wait(u):
                if not (isinstance(u, int) and u < 2):
                    pe.wait_ge(ring_free, u - 1)

            def agg_free(i, L, c, d, first):
                n = agg_group(L, c, d) - 3
                if n >= 8:
                    pe.wait_ge(agg_ok, upto(i, 4, n - 7))
                elif n >= 0:
                    pe.wait_ge(pt_ok, upto(i, 8, n + 1))
                elif not first:
                    pe.wait_ge(agg_ok, upto(i, 4, n + 1) if not isinstance(i, int) else 4 * i + n + 1)

            def agg_unit(L, c, d, m):
                rhs = slice(c * HALF, (c + 1) * HALF)
                w = slice(d * P, (d + 1) * P)
                return three(bank(AGG[agg_group(L, c, d) % 3]), h_hi[:, m, w], h_lo[:, m, w], adj_hi[:, m, rhs], adj_lo[:, m, rhs],
                             m == 0, m == NT - 1)

            def do(step, i, j, first):
                kind = step[0]
                if kind == "tr":
                    _, ahead, tile, g = step
                    b = i + ahead
                    if g == 0:
                        pe.wait_ge(adj_in[tile % 2], upto(b, 16 * TH, 16 * (tile // 2 + 1)))
                    ring_wait(tr_use(b, tile, g))
                    for q in range(TH):
                        m = g * TH + q
                        last = nc.tensor.transpose(bank(RING[g])[:, q * P:(q + 1) * P], raw[:, tile % 2, m * P:(m + 1) * P], ident[:, :])
                    last.then_inc(tr_mm, 1)
                elif kind == "agg2":
                    _, L, m = step
                    pe.wait_ge(h_ok, upto(i, 3 * NT, (L - 1) * NT + m + 1))
                    if m == 0 and L == 1:
                        pe.wait_ge(ring_free, ring_use(i, 0))
                    if L == 3 and m < TH:
                        pe.wait_ge(fix_ok, upto(i, NT, m + 1))
                    for d in range(ND):
                        if m == 0:
                            agg_free(i, L, 0, d, first)
                        last = agg_unit(L, 0, d, m)
                        if m == NT - 1:
                            last.then_inc(agg_mm, 1)
                elif kind == "agg1":
                    _, L, d, m = step
                    if m == 0:
                        if L == 1 and d == 0:
                            pe.wait_ge(ring_free, ring_use(i, 8))
                        agg_free(i, L, 1, d, first)
                        if L == 3 and d == 0:
                            pe.wait_ge(fix_ok, upto(i, NT, NT))
                    last = agg_unit(L, 1, d, m)
                    if m == NT - 1:
                        last.then_inc(agg_mm, 1)
                elif kind == "ht":
                    pair = step[1]
                    c, second = divmod(pair, 2)
                    pe.wait_ge(hs_ok, upto(i, NT, 2 * pair + 2))
                    for d in range(ND):
                        if not second:
                            ring_wait(ring_use(i, ring_of["ht", 2, c] + d))
                        for q in range(2):
                            at = slice((2 * second + q) * P, (2 * second + q + 1) * P)
                            last = nc.tensor.transpose(bank(RING[d])[:, at], hs[:, q, d * P:(d + 1) * P], ident[:, :])
                    last.then_inc(ht_mm, 1)
                elif kind == "w":
                    _, L, c, p = step
                    if p == 0:
                        pe.wait_ge(pt_ok, upto(i, 8, 4 * (L - 1) + 2 * c + 2))
                        if L == 2:
                            pe.wait_ge(ring_free, ring_use(i, ring_of["ht", 2, c] + 2))
                    ring_wait(ring_use(i, ring_of["w", L, c] + p))
                    for q in range(2):
                        o = bank(RING[p])[:, q * D:(q + 1) * D]
                        at = slice((2 * p + q) * P, (2 * p + q + 1) * P)
                        for d in range(ND):
                            if L == 1:
                                last = three(o, pt_hi[:, d, at], pt_lo[:, d, at], wa_hi[:, d, :], wa_lo[:, d, :], d == 0, d == ND - 1)
                            else:
                                three(o, ht_hi[:, d, at], ht_lo[:, d, at], wb_hi[:, d, :], wb_lo[:, d, :], d == 0, False)
                                last = three(o, pt_hi[:, d, at], pt_lo[:, d, at], wb_hi[:, ND + d, :], wb_lo[:, ND + d, :], False, d == ND - 1)
                    last.then_inc(w_mm, 1)
                elif kind == "up":
                    _, c, p = step
                    zero = isinstance(j, int) and j == 0 and c == 0
                    if p == 0:
                        pe.wait_ge(ac_ok, upto(j, NC, c + 1))
                        if not zero:
                            pe.wait_ge(msq_ok, upto(j, NC, c))
                            if c == 0:
                                pe.wait_ge(res_ok, upto(j, NC, 0))
                    elif p == 1:
                        if not zero:
                            pe.wait_ge(scaled_ok, upto(j, PAIRS * NC, PAIRS * c))
                    else:
                        pe.wait_ge(sq_ok, upto(j, PAIRS * NC, PAIRS * c + p - 1))
                    for q in range(2):
                        k = 2 * p + q
                        o = bank(HID[p % 2])[:, q * CH:(q + 1) * CH]
                        for d in range(ND):
                            last = three(o, w1_hi[:, d, k * P:(k + 1) * P], w1_lo[:, d, k * P:(k + 1) * P], ac_hi[:, d, :], ac_lo[:, d, :],
                                         d == 0, d == ND - 1)
                    last.then_inc(up_mm, 1)
                elif kind == "sumsq":
                    c = step[1]
                    pe.wait_ge(sum_ok, upto(j, 2 * PAIRS * NC, 2 * PAIRS * (c + 1)))
                    for q in range(2):
                        last = nc.tensor.matmul(bank(HID[0])[:, q:q + 1], sq_sum[:, q * P:(q + 1) * P], ones[:, 0:1], start=True, stop=True)
                    last.then_inc(col_mm, 1)
                elif kind == "bcast":
                    c = step[1]
                    pe.wait_ge(rms_rows_ok, upto(j, NC, c + 1))
                    for q in range(2):
                        last = nc.tensor.matmul(bank(HID[1])[:, q * P:(q + 1) * P], rms_rows[:, q, :], ident[:, :], start=True, stop=True)
                    last.then_inc(bcast_mm, 1)
                elif kind == "down":
                    _, c, p = step
                    n = PAIRS * c + p
                    if p == 0 and c > 0:
                        pe.wait_ge(res_ok, upto(j, NC, c))
                    pe.wait_ge(act_ok, upto(j, PAIRS * NC, n + 1))
                    for a in range(2):
                        k = 2 * p + a
                        for q in range(2):
                            at = slice(q * P, (q + 1) * P)
                            last = three(bank(DOWN)[:, q * D:(q + 1) * D], act_hi[:, p % 2, a, at], act_lo[:, p % 2, a, at],
                                         w2_hi[:, k, :], w2_lo[:, k, :], k == 0 and q == 0, k == NH - 1, skip=True)
                    last.then_inc(down_mm, 1)

            run(pe, do)


_INS = ["x", "adj", "L0_gnn_W1", "L0_gnn_b1", "L0_gnn_W2", "L0_gnn_b2", "L0_gnn_fusion_w", "L1_gnn_weight", "L1_gnn_bias",
        "L2_gnn_weight", "L2_gnn_bias", "L3_gnn_epsilon", "L3_gnn_W1", "L3_gnn_b1", "L3_gnn_rms_weight", "L3_gnn_W2",
        "L3_gnn_b2"]


def build(nc, arrays):
    f32 = mybir.dt.float32
    t_in = {n: nc.dram_tensor(f"in_{n}", a.shape, f32, kind="ExternalInput").ap() for n, a in arrays.items()}
    shape = arrays["x"].shape
    out = nc.dram_tensor("out_x", shape, f32, kind="ExternalOutput").ap()
    scratch = nc.dram_tensor("scratch_rows", (shape[0], SPACES[0][0], shape[2]), f32, kind="Internal").ap()
    gnn_stack(nc, t_in, out, scratch)


def kernel(**inputs):
    import concourse.bacc as bacc
    from concourse.bass_utils import run_bass_kernel_spmd

    arrays = {n: np.ascontiguousarray(inputs[n]) for n in _INS}
    arrays["L3_gnn_epsilon"] = arrays["L3_gnn_epsilon"].reshape(1)
    arrays.update(shape_constants())
    nc = bacc.Bacc("TRN2", target_bir_lowering=False, num_devices=1)
    build(nc, arrays)
    r = run_bass_kernel_spmd(nc, [{f"in_{n}": a for n, a in arrays.items()}], core_ids=[0])
    return r.results[0]["out_x"]
```

```python
import numpy as np
import concourse.bass as bass
from concourse import mybir
from contextlib import ExitStack

GROUPS = [list(range(25)), [0, 1, 2, 3, 4, 5, 6, 7, 8], [0, 9, 10, 11, 12, 13, 14], [6, 7, 8, 12, 13, 14],
          [3, 4, 5, 9, 10, 11]]
SPACES = [(25, 4, [0]), (15, 8, [1, 2, 3, 4])]


def shape_constants():
    consts = {"identity": np.eye(128, dtype=np.float32)}
    for s, (nodes, per_tile, groups) in enumerate(SPACES):
        rows = nodes * per_tile
        pair = np.zeros((rows, len(groups), rows), np.float32)
        member = np.zeros((rows, len(groups)), np.float32)
        for n, g in enumerate(groups):
            for q in range(per_tile):
                at = [q * nodes + v for v in GROUPS[g]]
                pair[np.ix_(at, [n], at)] = 1.0
                member[at, n] = 1.0
        consts[f"pair_mask_{s}"] = pair
        consts[f"member_mask_{s}"] = member
        consts[f"self_{s}"] = np.tile(np.eye(nodes, dtype=np.float32), (per_tile, 1))
    return consts


def gnn_stack(nc, t_in, out, scratch):
    f32, f32r = mybir.dt.float32, mybir.dt.float32r
    ALU, ACT, AX = mybir.AluOpType, mybir.ActivationFunctionType, mybir.AxisListType
    x_d, adj_d = t_in["x"], t_in["adj"]
    B, N, D = x_d.shape
    H = t_in["L3_gnn_W1"].shape[1]
    H0 = t_in["L0_gnn_W1"].shape[2]
    P = 128
    NT = N // P
    ND = D // P
    NH = H // P
    HALF = N // 2
    TH = NT // 2
    CH = 2 * P
    NC = N // CH
    LN_EPS, DEG_EPS, RMS_EPS = 1e-5, 1e-8, 1e-6
    F0 = SPACES[0][0]

    ctx = ExitStack()
    with ctx:
        def sb(name, shape, dt=f32, scope=ctx):
            return scope.enter_context(nc.sbuf_tensor(name, shape, dt))

        def sem(name):
            return ctx.enter_context(nc.semaphore(name))

        wa_hi, wa_lo = sb("wa_hi", [P, ND, D], f32r), sb("wa_lo", [P, ND, D], f32r)
        wb_hi, wb_lo = sb("wb_hi", [P, 2 * ND, D], f32r), sb("wb_lo", [P, 2 * ND, D], f32r)
        w1_hi, w1_lo = sb("w1_hi", [P, ND, H], f32r), sb("w1_lo", [P, ND, H], f32r)
        w2_hi, w2_lo = sb("w2_hi", [P, NH, D], f32r), sb("w2_lo", [P, NH, D], f32r)
        ident = sb("ident", [P, P])
        ones = sb("ones", [P, 1])
        bias1, bias2, bias3 = (sb(n, [P, D]) for n in ("bias1", "bias2", "bias3"))
        b1_col, rmsw_col = sb("b1_col", [P, NH]), sb("rmsw_col", [P, NH])
        minus_half = sb("minus_half", [P, 8])
        epsilon_col = sb("epsilon_col", [P, 1])

        adj_hi, adj_lo = sb("adj_hi", [P, NT, N], f32r), sb("adj_lo", [P, NT, N], f32r)
        raw = sb("raw", [P, 2, N])
        x = sb("x_rows", [P, NT, D])
        deg, inv_deg = sb("deg", [P, 2, NT]), sb("inv_deg", [P, NT])

        ps = ctx.enter_context(nc.psum_tensor("ps", [P, 8, 512], f32))
        AGG, RING, HID, DOWN = (0, 1, 2), (3, 4), (5, 6), 7
        V_OUT, V_AGG, V_HID = (0, 1), (2, 5), (6, 7)

        early = ExitStack()
        stage_a, stage_b = sb("stage_a", [P, ND, D], scope=early), sb("stage_b", [P, 2 * ND, D], scope=early)
        stage_1, stage_2 = sb("stage_1", [P, ND, H], scope=early), x
        NG, NK0 = len(GROUPS), H0 // P
        v_w1 = sb("v_w1", [P, 2, ND, H0], scope=early)
        v_w2 = sb("v_w2", [P, 2, NK0, D], scope=early)
        v_b1 = sb("v_b1", [P, NG, NK0], scope=early)
        v_b2 = sb("v_b2", [P, NG, D], scope=early)
        v_fw = sb("v_fw", [P, 4, NG], scope=early)
        v_red = sb("v_red", [P, 4], scope=early)
        V = []
        for s, (nodes, per_tile, groups) in enumerate(SPACES):
            rows, tiles, ng = nodes * per_tile, B // per_tile, len(groups)
            V.append(dict(
                rows=rows, tiles=tiles, ng=ng, nodes=nodes, per_tile=per_tile, groups=groups,
                x=sb(f"v_x{s}", [rows, tiles, D], scope=early), acc=sb(f"v_acc{s}", [rows, tiles, D], scope=early) if s else None,
                h=sb(f"v_h{s}", [rows, tiles, D], scope=early),
                adj=sb(f"v_adj{s}", [rows, tiles, nodes], scope=early), self_=sb(f"v_self{s}", [rows, nodes], scope=early),
                mask=sb(f"v_mask{s}", [rows, ng, rows], scope=early), member=sb(f"v_member{s}", [rows, ng], scope=early),
                ag=sb(f"v_ag{s}", [rows, ng, tiles, rows], scope=early),
                an_t=sb(f"v_an_t{s}", [rows, ng, tiles, rows], scope=early),
                deg=sb(f"v_deg{s}", [rows, 4, ng * tiles], scope=early),
                st=sb(f"v_st{s}", [rows, tiles, 6], scope=early), mv=sb(f"v_mv{s}", [rows, tiles, 2], scope=early),
                rs=sb(f"v_rs{s}", [rows, 2, tiles], scope=early), wm=sb(f"v_wm{s}", [rows, ng], scope=early)))
        V[0]["acc"] = V[0]["x"]
        VR = max(v["rows"] for v in V)
        VC = max(v["rows"] * v["tiles"] for v in V)
        VT = max(v["tiles"] for v in V)
        v_yt = sb("v_yt", [P, ND, VC], scope=early)
        v_hid = sb("v_hid", [P, NK0, VC], scope=early)
        v_s2 = sb("v_s2", [VR, VT, D], scope=early)
        v_u = sb("v_u", [VR, 2, D], scope=early)
        early.close()

        tail = sb("tail", [P, NT, D])
        h_hi, h_lo = sb("h_hi", [P, NT, D], f32r), sb("h_lo", [P, NT, D], f32r)
        y = sb("y", [P, TH, D])
        pt_hi, pt_lo = sb("pt_hi", [P, ND, HALF], f32r), sb("pt_lo", [P, ND, HALF], f32r)
        ht_hi, ht_lo = sb("ht_hi", [P, ND, HALF], f32r), sb("ht_lo", [P, ND, HALF], f32r)
        agg = sb("agg", [P, ND, N])
        ac_hi, ac_lo = sb("ac_hi", [P, ND, CH], f32r), sb("ac_lo", [P, ND, CH], f32r)
        hid = sb("hid", [P, NH, CH])
        sq_sum, sq = sb("sq_sum", [P, CH]), sb("sq", [P, 2, CH])
        act_hi, act_lo = sb("act_hi", [P, 2, 2, CH], f32r), sb("act_lo", [P, 2, 2, CH], f32r)
        rms_rows = sb("rms_rows", [P, 2, P])
        hs = sb("hs", [P, 2, D])
        fixed = sb("fixed", [P, 2, P])
        st, mv = sb("st", [P, NT, 6]), sb("mv", [P, NT, 2])
        silu_once = sb("silu_once", [P, 1])
        ve, rstd = sb("ve", [P, TH]), sb("rstd", [P, TH])
        msq, rms = sb("msq", [P, 2]), sb("rms", [P, 2])

        def f(view):
            return view.bitcast(f32)

        main_weights = ((wa_hi, wa_lo, stage_a), (wb_hi, wb_lo, stage_b), (w1_hi, w1_lo, stage_1), (w2_hi, w2_lo, stage_2))

        w_in, w_hi_ok, w_ok = sem("w_in"), sem("w_hi_ok"), sem("w_ok")
        const_in, vectors_in, const_ok = sem("const_in"), sem("vectors_in"), sem("const_ok")
        v_x_in, v_adj_in = sem("v_x_in"), sem("v_adj_in")
        V_TILES = sum(v["tiles"] for v in V)
        V_CONSTS = 1 + 3 * len(V)
        v_w_in = [sem("v_w_in0"), sem("v_w_in1")]
        v_dve = sem("v_dve")
        v_fw_sub, v_fw_exp = sem("v_fw_sub"), sem("v_fw_exp")
        v_deg_pow, v_deg_safe, v_var_ok, v_rstd = sem("v_deg_pow"), sem("v_deg_safe"), sem("v_var_ok"), sem("v_rstd")
        v_ag_ok, v_tr, v_ant = sem("v_ag_ok"), sem("v_tr"), sem("v_ant")
        v_h_ok, v_y_mm, v_y_ok = sem("v_h_ok"), sem("v_y_mm"), sem("v_y_ok")
        v_hid_mm, v_hid_ok = sem("v_hid_mm"), sem("v_hid_ok")
        v_ring_mm, v_ring_free = sem("v_ring_mm"), sem("v_ring_free")
        v_acc_in, v_stored, v_done = sem("v_acc_in"), sem("v_stored"), sem("v_done")

        x_in = [sem("x_in0"), sem("x_in1")]
        adj_in = [sem("adj_in0"), sem("adj_in1")]
        tr_mm, adj_hi_ok = sem("tr_mm"), sem("adj_hi_ok")
        ring_free = sem("ring_free")
        rowsum_ok = sem("rowsum_ok")
        deg_ok, inv_ok = sem("deg_ok"), sem("inv_ok")
        bn_ok, stats_ok = sem("bn_ok"), sem("stats_ok")
        ve_ok, rstd_ok = sem("ve_ok"), sem("rstd_ok")
        y_ok, h_hi_ok, h_ok = sem("y_ok"), sem("h_hi_ok"), sem("h_ok")
        hs_ok = sem("hs_ok")
        agg_mm = sem("agg_mm")
        pt_hi_ok, pt_ok = sem("pt_hi_ok"), sem("pt_ok")
        agg_ok = sem("agg_ok")
        ht_mm, ht_hi_ok = sem("ht_mm"), sem("ht_hi_ok")
        w_mm = sem("w_mm")
        relu_ok = sem("relu_ok")
        xb_ok, tail_ok = sem("xb_ok"), sem("tail_ok")
        fsum_ok = sem("fsum_ok")
        fix_hi_ok, fix_ok = sem("fix_hi_ok"), sem("fix_ok")
        ac_hi_ok, ac_ok = sem("ac_hi_ok"), sem("ac_ok")
        up_mm, hid_ok, sq_ok = sem("up_mm"), sem("hid_ok"), sem("sq_ok")
        sum_ok = sem("sum_ok")
        col_mm, msq_ok, rms_ok, rms_rows_ok, bcast_mm = (sem(n) for n in ("col_mm", "msq_ok", "rms_ok", "rms_rows_ok", "bcast_mm"))
        scaled_ok = sem("scaled_ok")
        silu_ok, act_hi_ok, act_ok, down_mm = (sem(n) for n in ("silu_ok", "act_hi_ok", "act_ok", "down_mm"))
        res_ok, stored = sem("res_ok"), sem("stored")

        table_ok = sem("table_ok")
        waits_apart = {e.engine: sem(f"waits_apart_{n}") for n, e in (("sp", nc.sync), ("dve", nc.vector), ("pool", nc.gpsimd))}

        X_DMAS = 3
        RING_USES = 28
        PAIRS = NH // 2

        def upto(graph, per_graph, n):
            return graph * per_graph + n

        def ring_use(graph, n):
            return graph * RING_USES + 8 + n

        ring_of = {("w", 1, 0): 8, ("w", 1, 1): 10, ("ht", 2, 0): 12, ("w", 2, 0): 14, ("ht", 2, 1): 16,
                   ("w", 2, 1): 18}

        def tr_use(graph, tile, g):
            return ring_use(graph, 2 * tile + g - 8)

        COST = {"agg2": 1.3, "agg1": 0.65, "tr": 0.45, "w1": 1.3, "w2": 2.6, "ht": 0.45}

        MLP = ((0.65, "chunk_split"), ((2.51, 1.49, 1.74, 1.49), "up", 0), (1.01, "up", 1), (1.68, "up", 2),
               (1.23, "up", 3), (3.66, "rms"), ((1.16, 1.24, 1.24, 1.24), "sumsq"),
               ((1.04, 0.9, 0.88, 1.01), "rms_rows"), (1.85, "bcast"), ((0.82, 0.86, 0.84, 0.87), "scale", 0),
               (0.0, "scale", 1), ((0.15, 0.0, 0.15, 0.15), "silu", 0), (0.57, "act", 0),
               ((0.56, 0.55, 0.56, 0.56), "silu", 1), ((0.0, 0.0, 0.04, 0.01), "scale", 2), (0.7, "silu", 2),
               ((1.05, 1.17, 1.05, 1.05), "act", 1), ((0.1, 0.0, 0.0, 0.0), "silu", 3),
               ((0.0, 0.0, 0.0, 0.01), "scale", 3), ((0.58, 0.6, 0.6, 0.55), "down", 0), (0.0, "act", 2),
               ((0.3, 0.45, 0.3, 0.3), "down", 1), ((0.82, 0.87, 0.88, 0.87), "act", 3),
               ((0.27, 0.01, 0.27, 0.27), "down", 2), ((1.02, 1.02, 1.03, 1.02), "down", 3),
               ((0.26, 0.22, 0.22, 0.22), "result"))
        START = (1.24, 0, 0, 0)
        OWN = 3

        PLACE = {"split_0": (-2.0, -3.26, -2.0), "fill": (-1.95, -1.86, -1.95), "w_2": (-3.51, -1.8, -1.8),
                 "split_2": (-1.83, -1.11, -0.78), "fix_0": -2.59, "sum_fix_2": -1.57, "w_3": (-1.61, -1.5, -1.5),
                 "split_3": (-1.83, -1.11, -0.78), "rstd_1": (0.04, 0.04, 0.04), "fix_2": -1.3, "sum_fix_4": 0.44,
                 "hs_0": -0.44, "ht_0": -0.69, "hs_1": 0.77, "norm_4": (1.04, 1.04, 1.04),
                 "split_4": (1.69, 1.89, 1.72), "ht_1": 2.62, "tail_0": 3.57, "split_6": (4.1, 3.91, 4.75),
                 "fix_4": 2.2, "sum_fix_6": 2.76, "fix_6": 6.33, "tr": -1.8, "w_0": (10.49, 10.25, 10.25),
                 "w_1": (10.6, 10.96, 10.97), "rstd_0": (10.65, 12.71, 10.65), "hs_2": 11.66, "ht_2": 11.37,
                 "hs_3": 12.01, "norm_0": (13.79, 13.24, 13.32), "ht_3": 13.47, "sum_fix_0": 13.41, "tr_next": 9.14,
                 "stats_0": 12.03, "stats_2": 14.06, "rstd_next": 11.48, "norm_next": 17.15, "stats_4": 14.89,
                 "stats_6": 15.13, "rstd_next_1": 28.54}

        def mlp_steps(c):
            return [((gap[c] if isinstance(gap, (tuple, list)) else gap) + (START[c] if n == 0 else 0.0), (kind, c, *pair))
                    for n, (gap, kind, *pair) in enumerate(MLP)]

        def front_steps(nxt):
            o = []
            for L in (1, 2, 3):
                last = L == 3
                placed = []

                def put(at, *steps):
                    at = PLACE[at] if isinstance(at, str) else at
                    at = at[L - 1] if isinstance(at, (tuple, list)) else at
                    placed.extend((at, step) for step in steps)

                put("split_0", ("split", L, 0), ("split", L, 1))
                put("fill", ("fill", L))
                put("split_2", ("split", L, 2))
                put("split_3", ("split", L, 3))
                if L > 1:
                    put("w_2", ("w", L - 1, 1, 0))
                    put("w_3", ("w", L - 1, 1, 1))
                    put("rstd_1", ("rstd", L, 1))
                put("norm_4", *[("norm", L, t) for t in range(TH, NT)])
                put("split_4", ("split", L, TH), ("split", L, TH + 1))
                put("split_6", ("split", L, TH + 2), ("split", L, TH + 3))
                for m in range(NT):
                    put(m, ("agg2", L, m))
                put(7.6, ("pt", L, 0, 0), ("pt", L, 0, 1))
                for d in range(ND):
                    for m in range(NT):
                        put(8 + 4 * d + m / 2, ("agg1", L, d, m))
                    put(11.51 + 4 * d, ("pt", L, 1, d))
                if not last:
                    put("w_0", ("w", L, 0, 0))
                    put("w_1", ("w", L, 0, 1))
                    put("rstd_0", ("rstd", L + 1, 0))
                    put("norm_0", *[("norm", L + 1, t) for t in range(TH)])
                if L == 1:
                    for m in range(NT):
                        put(m + PLACE["tr"], ("tr", 0, TH + m // 2, m % 2))
                    put(7.7, ("deg",))
                    put(7.7, *[("xb", t) for t in range(NT)])
                if L == 2:
                    for pair in range(TH):
                        put(f"hs_{pair}", ("hs", pair))
                        put(f"ht_{pair}", ("ht", pair))
                    put("sum_fix_0", ("sum_fix", 0), ("sum_fix", 1))
                if last:
                    for t in range(0, NT, 2):
                        put(f"fix_{t}", ("fix", t), ("fix", t + 1))
                        if t:
                            put(f"sum_fix_{t}", ("sum_fix", t), ("sum_fix", t + 1))
                    put(7.7, ("mlp_before",))
                    if nxt:
                        put("tail_0", *[("tail", t) for t in range(TH)], ("load_x", 0))
                        put(7.8, *[("tail", t) for t in range(TH, NT)], ("load_x", 1))
                        for k in range(NT):
                            put(k + PLACE["tr_next"], ("tr", 1, k // 2, k % 2))
                        put("stats_0", ("stats", 1, 0))
                        put("stats_2", ("stats", 1, 2))
                        put("rstd_next", ("rstd", 1, 0))
                        put("norm_next", *[("norm", 1, t) for t in range(TH)])
                        put("stats_4", ("stats", 1, 4))
                        put("stats_6", ("stats", 1, 6))
                        put("rstd_next_1", ("rstd", 1, 1))
                    else:
                        put(7.8, *[("tail", t) for t in range(NT)])
                o += [step for _, step in sorted(placed, key=lambda p: p[0])]
            return o

        def merge(front, others, fill):
            cost = [fill[step[1] - 1] if step[0] == "fill" else COST.get(step[0] if step[0] != "w" else f"w{step[1]}", 0.0)
                    for step in front]
            scale = sum(cost) / max(sum(g for g, _, _ in others), 1e-9) * 0.98
            merged, gap, others = [], 0.0, list(others)
            for n, step in enumerate(front):
                if step[0] not in ("fill", "mlp_before"):
                    merged.append((step, 0))
                gap += cost[n]
                while others and gap >= others[0][0] * scale:
                    gap -= others[0][0] * scale
                    merged.append(others.pop(0)[1:])
            return merged + [o[1:] for o in others]

        FILL = (2.4, 5.04, 2.43)

        def mlp_after():
            others = mlp_steps(0)[OWN:]
            for c in range(1, NC):
                others += mlp_steps(c)
            return [(gap, step, 1) for gap, step in others]

        def body_steps(with_tail, nxt):
            front = front_steps(nxt)
            cut = front.index(("mlp_before",))
            return merge(front[:cut], mlp_after() if with_tail else [], FILL) + \
                merge(front[cut:], [(gap, step, 0) for gap, step in mlp_steps(0)[:OWN]], FILL)

        LAST_MLP = (("chunk_split", 1), ("silu", 0, 0), ("up", 1, 0), ("up", 1, 1), ("scale", 0, 0), ("scale", 0, 1),
                    ("silu", 0, 1), ("down", 0, 0), ("scale", 0, 2), ("act", 0, 0), ("act", 0, 1), ("up", 1, 2),
                    ("scale", 0, 3), ("silu", 0, 2), ("up", 1, 3), ("rms", 1), ("silu", 0, 3), ("act", 0, 2),
                    ("down", 0, 1), ("down", 0, 2), ("act", 0, 3), ("sumsq", 1), ("down", 0, 3), ("rms_rows", 1),
                    ("bcast", 1), ("result", 0))

        def epilogue_steps():
            begun = [step for _, step in mlp_steps(0)[:max(OWN, 5)]]
            o = begun[OWN:]
            for c in range(-1, NC):
                o += [(kind, c + ahead, *pair) for kind, ahead, *pair in LAST_MLP
                      if 0 <= c + ahead < NC and (kind, c + ahead, *pair) not in begun]
            return [(step, 1) for step in o]

        def first_transposes(group):
            return [("tr", 1, group - 1, g) for g in range(2)] if group else []

        def prologue_steps():
            return [("load_x", 1), ("load_x", 0)] + [("stats", 1, t) for t in range(NT)] + \
                [("rstd", 1, 0)] + [("norm", 1, t) for t in range(TH)] + [("rstd", 1, 1)]

        TURN = ("agg1", 1, 0, 2)

        def run(engine, do):
            for step in prologue_steps():
                do(step, -1, None, True)
            for step, age in body_steps(False, True):
                do(step, 0, 0 - age, True)
            steps = body_steps(True, True)
            cut = [step for step, _ in steps].index(TURN)
            if B > 3:
                for step, age in steps[:cut]:
                    do(step, 1, 1 - age, False)
                with engine.Fori(1, B - 2) as i:
                    do(("table",), i, None, False)
                    for step, age in steps[cut:]:
                        do(step, i, i - age, False)
                    for step, age in steps[:cut]:
                        do(step, i + 1, i + 1 - age, False)
                for step, age in steps[cut:]:
                    do(step, B - 2, B - 2 - age, False)
            else:
                for i in range(1, B - 1):
                    for step, age in steps:
                        do(step, i, i - age, False)
            for step, age in body_steps(True, False):
                do(step, B - 1, B - 1 - age, False)
            for step, age in epilogue_steps():
                do(step, B, B - age, False)

        def wait_apart(engine, semaphore, value):
            engine.wait_ge(semaphore, value)
            engine.sem_inc(waits_apart[engine.engine], 1)

        def bank(n, width=512):
            return ps[:, n, 0:width]

        def last_graph(j):
            return isinstance(j, int) and j == B - 1

        def hidden(j, c):
            if last_graph(j) and c % 2:
                return raw[:, :, :].rearrange("p a (b n) -> p (a b) n", n=CH), AGG
            return hid, HID

        def agg_group(L, c, d):
            return 4 * (L - 1) + 2 * c + d

        block = ctx.enter_context(nc.Block())

        @block.sync
        def _(sp):
            def load_group(n):
                sp.dma_start(v_w1[:, n % 2], t_in["L0_gnn_W1"][n].rearrange("(d p) e -> p d e", p=P)).then_inc(v_w_in[n % 2], 16)
                sp.dma_start(v_w2[:, n % 2], t_in["L0_gnn_W2"][n].rearrange("(k p) e -> p k e", p=P)).then_inc(v_w_in[n % 2], 16)

            def graph_rows(tensor, v, t):
                return tensor[t * v["per_tile"]:(t + 1) * v["per_tile"], 0:v["nodes"], :]

            def layer_0():
                for v in V:
                    for t in range(v["tiles"]):
                        sp.dma_start(v["x"][:, t, :], graph_rows(x_d, v, t)).then_inc(v_x_in, 16)
                sp.dma_start(ident[:, :], t_in["identity"]).then_inc(const_in, 16)
                for s, v in enumerate(V):
                    sp.dma_start(v["mask"][:, :, :], t_in[f"pair_mask_{s}"]).then_inc(const_in, 16)
                    sp.dma_start(v["self_"][:, :], t_in[f"self_{s}"]).then_inc(const_in, 16)
                    sp.dma_start(v["member"][:, :], t_in[f"member_mask_{s}"]).then_inc(const_in, 16)
                load_group(0)
                load_group(1)
                load_adj(0, 0, True)
                load_adj(0, 1, True)
                for tile_, name in ((stage_a, "L1_gnn_weight"), (stage_b, "L2_gnn_weight"), (stage_1, "L3_gnn_W1"),
                                    (stage_2, "L3_gnn_W2")):
                    sp.dma_start(tile_[:, :, :], t_in[name].rearrange("(d p) e -> p d e", p=P)).then_inc(w_in, 16)
                done = 0
                for s, v in enumerate(V):
                    for n in range(v["ng"]):
                        done += 1
                        for step in first_transposes(done - 1):
                            do(step, -1, None, True)
                        sp.wait_ge(v_done, done)
                        if done + 1 < NG:
                            load_group(done + 1)
                        if n == v["ng"] - 1:
                            for t in range(v["tiles"]):
                                sp.dma_start(graph_rows(scratch, v, t), v["acc"][:, t, :]).then_inc(v_stored, 16)
                    if s + 1 < len(V):
                        w = V[s + 1]
                        sp.wait_ge(v_h_ok, s + 2)
                        sp.wait_ge(v_stored, 16 * v["tiles"])
                        for t in range(w["tiles"]):
                            sp.dma_start(w["x"][:, t, :], graph_rows(scratch, w, t)).then_inc(v_acc_in, 16)

            def load_adj(graph, tile, first):
                s = tile % 2
                if not first:
                    before = graph * 2 * NT + 2 * (tile - 2) + 2
                    wait_apart(sp, tr_mm, before)
                    wait_apart(sp, rowsum_ok, graph * NT + tile - 1)
                sp.dma_start(raw[:, s, :], adj_d[graph, tile * P:(tile + 1) * P, :] if isinstance(graph, int)
                             else adj_d[bass.ds(graph, 1), tile * P:(tile + 1) * P, :].rearrange("a p n -> (a p) n")
                             ).then_inc(adj_in[s], 16)

            def rows(tensor, graph, lo, hi):
                if isinstance(graph, int):
                    return tensor[graph, lo:hi, :]
                return tensor[bass.ds(graph, 1), lo:hi, :].rearrange("a p n -> (a p) n")

            def do(step, i, j, first):
                kind = step[0]
                nxt = i + 1
                if kind == "load_x":
                    half = step[1]
                    if first and isinstance(i, int) and i < 0:
                        sp.wait_ge(w_ok, 4)
                    else:
                        wait_apart(sp, tail_ok, upto(i, NT, (half + 1) * TH))
                    if half == 0:
                        if first and isinstance(i, int) and i < 0:
                            sp.wait_ge(v_stored, 16 * V_TILES)
                        sp.dma_start(x[0:F0, 0, :], rows(scratch, nxt, 0, F0)).then_inc(x_in[0], 16)
                        sp.dma_start(x[F0:P, 0, :], rows(x_d, nxt, F0, P)).then_inc(x_in[0], 16)
                        sp.dma_start(x[:, 1:TH, :], rows(x_d, nxt, P, HALF).rearrange("(t p) d -> p t d", p=P)).then_inc(x_in[0], 16)
                    else:
                        sp.dma_start(x[:, TH:NT, :], rows(x_d, nxt, HALF, N).rearrange("(t p) d -> p t d", p=P)).then_inc(x_in[1], 16)
                elif kind == "tr":
                    _, ahead, tile, g = step
                    if g == 1:
                        graph = i + ahead
                        if tile + 2 < NT:
                            load_adj(graph, tile + 2, False)
                        elif isinstance(graph, int) and graph == B - 1:
                            pass
                        else:
                            load_adj(graph + 1, tile + 2 - NT, False)
                elif kind == "result":
                    c = step[1]
                    if not (isinstance(j, int) and j == 0 and c == 0):
                        if c > 0:
                            wait_apart(sp, stored, upto(j, 16 * NC, 16 * c))
                    wait_apart(sp, res_ok, upto(j, NC, c + 1))
                    sp.dma_start(rows(out, j, c * CH, (c + 1) * CH).rearrange("(t p) d -> p t d", p=P),
                                 tail[:, 2 * c:2 * c + 2, :]).then_inc(stored, 16)

            layer_0()
            run(sp, do)
            sp.wait_ge(stored, 16 * NC * B)

        @block.gpsimd
        def _(pool):
            nc.gpsimd.memset(ones[:, :], 1.0).then_inc(const_ok, 1)
            nc.gpsimd.memset(minus_half[:, :], -0.5).then_inc(const_ok, 1)
            with nc.allow_non_contiguous_dma(reason="small vectors, once"):
                for col, src in ((b1_col, "L3_gnn_b1"), (rmsw_col, "L3_gnn_rms_weight")):
                    pool.dma_start(col[:, :], t_in[src].rearrange("(k p) -> p k", p=P)).then_inc(vectors_in, 16)
                pool.dma_start(v_b1[:, :, :], t_in["L0_gnn_b1"].rearrange("g (k p) -> p g k", p=P)).then_inc(vectors_in, 16)
                for row, src in ((bias1, "L1_gnn_bias"), (bias2, "L2_gnn_bias"), (bias3, "L3_gnn_b2")):
                    pool.dma_start(row[:, :], t_in[src].rearrange("(a n) -> a n", a=1).broadcast_to([P, D])).then_inc(vectors_in, 16)
                pool.dma_start(v_b2[:, :, :].rearrange("p g n -> p (g n)"),
                               t_in["L0_gnn_b2"].rearrange("(a g) n -> a (g n)", a=1).broadcast_to([P, NG * D])).then_inc(vectors_in, 16)
                pool.dma_start(v_fw[:, 0, :], t_in["L0_gnn_fusion_w"].rearrange("(a n) -> a n", a=1).broadcast_to([P, NG])).then_inc(vectors_in, 16)
                pool.dma_start(epsilon_col[:, :], t_in["L3_gnn_epsilon"].rearrange("(a n) -> a n", a=1).broadcast_to([P, 1])).then_inc(vectors_in, 16)
            pool.wait_ge(const_ok, 2)
            for s, v in enumerate(V):
                r, n = v["rows"], v["ng"] * v["tiles"]
                pool.wait_ge(v_var_ok, s + 1)
                for t in range(v["tiles"]):
                    last = nc.gpsimd.tensor_tensor(v["rs"][:, 1, t:t + 1], v["rs"][:, 0, t:t + 1], minus_half[0:r, 0:1], ALU.pow)
                last.then_inc(v_rstd, 1)
                pool.wait_ge(v_deg_safe, s + 1)
                for k in range(0, n, 8):
                    m = min(8, n - k)
                    last = nc.gpsimd.tensor_tensor(v["deg"][:, 2, k:k + m], v["deg"][:, 1, k:k + m], minus_half[0:r, 0:m], ALU.pow)
                last.then_inc(v_deg_pow, 1)
            pool.wait_ge(v_stored, 16 * V_TILES)
            pool.wait_ge(w_ok, 4)

            def do(step, i, j, first):
                kind = step[0]
                pro = isinstance(i, int) and i < 0
                if kind == "rstd":
                    _, L, half = step
                    b = i + 1 if L == 1 else i
                    wait_apart(pool, stats_ok, upto(b, 3 * NT, (L - 1) * NT + (half + 1) * TH))
                    k = 2 * (L - 1) + half
                    if not (pro and half == 0):
                        wait_apart(pool, rstd_ok, upto(b, 6, k))
                    nc.gpsimd.tensor_scalar(ve[:, :], mv[:, half * TH:(half + 1) * TH, 1], LN_EPS, None, ALU.add).then_inc(ve_ok, 1)
                    pool.wait_ge(ve_ok, upto(b, 6, k + 1))
                    if not (pro and half == 0):
                        pool.wait_ge(y_ok, upto(b, 3 * NT, (L - 1) * NT + half * TH))
                    nc.gpsimd.tensor_tensor(rstd[:, :], ve[:, :], minus_half[:, 0:TH], ALU.pow).then_inc(rstd_ok, 1)
                elif kind == "hs":
                    pair = step[1]
                    if pair == 0:
                        wait_apart(pool, deg_ok, upto(i, 1, 1))
                    if pair > 0 or not first:
                        wait_apart(pool, ht_mm, upto(i, TH, pair))
                    wait_apart(pool, y_ok, upto(i, 3 * NT, NT + 2 * pair + 2))
                    for t in (2 * pair, 2 * pair + 1):
                        nc.gpsimd.tensor_scalar(hs[:, t % 2, :], y[:, t % TH, :], 0.0, deg[:, 1, t:t + 1],
                                                ALU.max, ALU.mult).then_inc(hs_ok, 1)
                elif kind == "sum_fix":
                    t = step[1]
                    n = upto(i, 3 * NT, 3 * t)
                    if t >= 2 or not first:
                        wait_apart(pool, fix_ok, upto(i, NT, t - 1))
                    dh, dl = adj_hi[:, t, t * P:(t + 1) * P], adj_lo[:, t, t * P:(t + 1) * P]
                    fx = fixed[:, t % 2, :]
                    nc.gpsimd.tensor_scalar(fx, ident[:, :], epsilon_col[:, 0:1], None, ALU.mult).then_inc(fsum_ok, 1)
                    for q, part in enumerate((f(dh), f(dl))):
                        pool.wait_ge(fsum_ok, n + q + 1)
                        nc.gpsimd.tensor_tensor(fx, fx, part, ALU.add).then_inc(fsum_ok, 1)
                elif kind == "xb":
                    t = step[1]
                    pool.wait_ge(y_ok, upto(i, 3 * NT, t + 1))
                    nc.gpsimd.tensor_tensor(x[:, t, :], x[:, t, :], bias1[:, :], ALU.add).then_inc(xb_ok, 1)
                elif kind == "tail":
                    t = step[1]
                    if not first and t % 2 == 0:
                        pool.wait_ge(stored, upto(i - 1, 16 * NC, 16 * (t // 2 + 1)))
                    pool.wait_ge(y_ok, upto(i, 3 * NT, 2 * NT + t + 1))
                    nc.gpsimd.tensor_tensor(tail[:, t, :], x[:, t, :], bias3[:, :], ALU.add).then_inc(tail_ok, 1)
                elif kind == "up":
                    _, c, p = step
                    n = upto(j, 2 * PAIRS * NC, 2 * (PAIRS * c + p))
                    pool.wait_ge(sq_ok, upto(j, PAIRS * NC, PAIRS * c + p + 1))
                    if p == 0:
                        if not (isinstance(j, int) and j == 0 and c == 0):
                            pool.wait_ge(col_mm, upto(j, NC, c))
                        nc.gpsimd.tensor_tensor(sq_sum[:, :], sq[:, 0, :], sq[:, 1, :], ALU.add).then_inc(sum_ok, 2)
                    else:
                        for q in range(2):
                            pool.wait_ge(sum_ok, n + q)
                            nc.gpsimd.tensor_tensor(sq_sum[:, :], sq_sum[:, :], sq[:, q, :], ALU.add).then_inc(sum_ok, 1)
                elif kind == "rms":
                    c = step[1]
                    pool.wait_ge(msq_ok, upto(j, NC, c + 1))
                    if c > 0:
                        pool.wait_ge(rms_rows_ok, upto(j, NC, c))
                    nc.gpsimd.tensor_tensor(rms[:, :], msq[:, :], minus_half[:, 0:2], ALU.pow).then_inc(rms_ok, 1)

            run(pool, do)

        @block.scalar
        def _(act):
            def layer_0():
                for v in V:
                    for t in range(v["tiles"]):
                        act.dma_start(v["adj"][:, t, :], adj_d[t * v["per_tile"]:(t + 1) * v["per_tile"], 0:v["nodes"], 0:v["nodes"]]
                                      ).then_inc(v_adj_in, 16)
                done_tr, gidx = 0, 0
                for s, v in enumerate(V):
                    r, tiles = v["rows"], v["tiles"]
                    for n in range(v["ng"] * tiles):
                        done_tr += 1
                        act.wait_ge(v_tr, done_tr)
                        g, t = divmod(n, tiles)
                        nc.scalar.activation(v["an_t"][:, g, t, :], ps[0:r, V_HID[done_tr % 2], 0:r], ACT.Copy,
                                             scale=v["deg"][:, 3, n:n + 1]).then_inc(v_ant, 1)
                    for n in range(v["ng"]):
                        g = v["groups"][n]
                        cols = r * tiles
                        for d in range(ND):
                            act.wait_ge(v_y_mm, ND * gidx + d + 1)
                            if gidx:
                                act.wait_ge(v_hid_mm, NK0 * gidx)
                            nc.scalar.activation(v_yt[:, d, 0:cols], ps[:, V_AGG[d], 0:cols], ACT.Copy).then_inc(v_y_ok, 1)
                        for step in first_transposes(gidx)[:1]:
                            do(step, -1, None, True)
                        if gidx == 0:
                            act.wait_ge(vectors_in, 16 * 9)
                        for k in range(NK0):
                            act.wait_ge(v_hid_mm, NK0 * gidx + k + 1)
                            if gidx:
                                act.wait_ge(v_done, gidx)
                            nc.scalar.activation(v_hid[:, k, 0:cols], ps[:, V_HID[k % 2], 0:cols], ACT.Relu,
                                                 bias=v_b1[:, g, k:k + 1]).then_inc(v_hid_ok, 1)
                        for step in first_transposes(gidx)[1:]:
                            do(step, -1, None, True)
                        if gidx == 0:
                            act.wait_ge(v_fw_sub, 1)
                            nc.scalar.activation(v_fw[:, 1, :], v_fw[:, 0, :], ACT.Exp, bias=v_red[:, 1:2], accum_out=v_red[:, 2:3]).then_inc(v_fw_exp, 1)
                            act.wait_ge(w_in, 64)
                        if gidx < 4:
                            hi, lo, st_ = main_weights[gidx]
                            nc.scalar.activation(hi[:, :, :], st_[:, :, :], ACT.Copy).then_inc(w_hi_ok, 1)
                        gidx += 1
                act.wait_ge(v_stored, 16 * V_TILES)
                act.wait_ge(w_ok, 4)

            def do(step, i, j, first):
                kind = step[0]
                pro = isinstance(i, int) and i < 0
                if kind == "table":
                    nc.scalar.activation(silu_once[:, :], minus_half[:, 0:1], ACT.Silu).then_inc(table_ok, 1)
                    act.wait_ge(table_ok, i)
                elif kind == "tr":
                    _, ahead, tile, g = step
                    b = i + ahead
                    n = 2 * tile + g
                    act.wait_ge(tr_mm, upto(b, 2 * NT, n + 1))
                    if not pro and g == 0 and tile % TH == 0:
                        if ahead:
                            act.wait_ge(agg_mm, upto(i, 12, 10))
                        elif not first:
                            act.wait_ge(agg_mm, upto(i, 12, 0))
                    nc.scalar.activation(adj_hi[:, g * TH:(g + 1) * TH, tile * P:(tile + 1) * P],
                                         bank(RING[n % 2]).rearrange("p (a b) -> p a b", b=P), ACT.Copy).then_inc(adj_hi_ok, 1)
                elif kind == "split":
                    _, L, t = step
                    n = (L - 1) * NT + t
                    act.wait_ge(y_ok, upto(i, 3 * NT, n + 1))
                    if t == 0 and not (first and L == 1):
                        act.wait_ge(agg_mm, upto(i, 12, 4 * (L - 1)))
                    nc.scalar.activation(h_hi[:, t, :], y[:, t % TH, :], ACT.Relu).then_inc(h_hi_ok, 1)
                elif kind == "pt":
                    _, L, c, d = step
                    n = agg_group(L, c, d)
                    act.wait_ge(agg_mm, upto(i, 12, n + 1))
                    if L < 3:
                        if c == 1:
                            act.wait_ge(w_mm, upto(i, 8, 4 * (L - 1) + 2))
                        elif L == 2:
                            act.wait_ge(w_mm, upto(i, 8, 4))
                        elif not first:
                            act.wait_ge(w_mm, upto(i, 8, 0))
                        nc.scalar.activation(pt_hi[:, d, :], bank(AGG[n % 3]), ACT.Copy).then_inc(pt_hi_ok, 1)
                    else:
                        if not first and c == 0 and d == 0:
                            act.wait_ge(ac_ok, upto(i, NC, 0))
                        nc.scalar.activation(agg[:, d, c * HALF:(c + 1) * HALF], bank(AGG[n % 3]), ACT.Copy).then_inc(agg_ok, 1)
                elif kind == "ht" and step[1] % 2:
                    c = step[1] // 2
                    act.wait_ge(ht_mm, upto(i, TH, 2 * c + 2))
                    if c == 1:
                        act.wait_ge(w_mm, upto(i, 8, 6))
                    elif not first:
                        act.wait_ge(w_mm, upto(i, 8, 0))
                    for d in range(ND):
                        nc.scalar.activation(ht_hi[:, d, :], bank(RING[d]), ACT.Copy).then_inc(ht_hi_ok, 1)
                elif kind == "up":
                    _, c, p = step
                    n = PAIRS * c + p
                    act.wait_ge(up_mm, upto(j, PAIRS * NC, n + 1))
                    hid, banks = hidden(j, c)
                    if last_graph(j) and c == 1:
                        act.wait_ge(rowsum_ok, upto(j, NT, NT))
                    elif last_graph(j) and c > 1:
                        act.wait_ge(act_ok, upto(j, PAIRS * NC, n - 2 * PAIRS + 1))
                    elif c > 0:
                        act.wait_ge(act_ok, upto(j, PAIRS * NC, n - PAIRS + 1))
                    elif p == 0 and not (isinstance(j, int) and j == 0):
                        act.wait_ge(act_ok, upto(j, PAIRS * NC, 0))
                    src = bank(banks[p % 2]).rearrange("p (a b) -> p a b", b=CH)
                    for q in range(2):
                        k = 2 * p + q
                        last = nc.scalar.activation(hid[:, k, :], src[:, q, :], ACT.Identity, bias=b1_col[:, k:k + 1])
                    last.then_inc(hid_ok, 1)
                    if not (isinstance(j, int) and j == 0 and n == 0):
                        act.wait_ge(sum_ok, upto(j, 2 * PAIRS * NC, 2 * n))
                    for q in range(2):
                        k = 2 * p + q
                        last = nc.scalar.activation(sq[:, q, :], src[:, q, :], ACT.Square, bias=b1_col[:, k:k + 1])
                    last.then_inc(sq_ok, 1)
                elif kind == "fix":
                    t = step[1]
                    act.wait_ge(fsum_ok, upto(i, 3 * NT, 3 * t + 3))
                    if t == 0:
                        act.wait_ge(agg_mm, upto(i, 12, 8))
                    nc.scalar.activation(adj_hi[:, t, t * P:(t + 1) * P], fixed[:, t % 2, :], ACT.Copy).then_inc(fix_hi_ok, 1)
                elif kind == "silu":
                    _, c, p = step
                    n = PAIRS * c + p
                    hid, banks = hidden(j, c)
                    act.wait_ge(scaled_ok, upto(j, PAIRS * NC, n + 1))
                    for q in range(2):
                        k = 2 * p + q
                        last = nc.scalar.activation(hid[:, k, :], hid[:, k, :], ACT.Silu, scale=rmsw_col[:, k:k + 1])
                    last.then_inc(silu_ok, 1)
                    act.wait_ge(silu_ok, upto(j, PAIRS * NC, n + 1))
                    if p >= 2:
                        act.wait_ge(down_mm, upto(j, PAIRS * NC, n - 1))
                    elif c > 0:
                        act.wait_ge(down_mm, upto(j, PAIRS * NC, PAIRS * c))
                    nc.scalar.activation(act_hi[:, p % 2], hid[:, 2 * p:2 * p + 2, :], ACT.Copy).then_inc(act_hi_ok, 1)

            layer_0()
            run(act, do)

        @block.vector
        def _(dve):
            vd = [0]

            def link(ins):
                vd[0] += 1
                ins.then_inc(v_dve, 1)
                dve.wait_ge(v_dve, vd[0])

            def layer_0():
                dve.wait_ge(v_x_in, 16 * V_TILES)
                for s, v in enumerate(V):
                    for t in range(v["tiles"]):
                        last = nc.vector.bn_stats(v["st"][:, t, :], v["x"][:, t, :])
                    link(last)
                    for t in range(v["tiles"]):
                        last = nc.vector.bn_aggr(v["mv"][:, t, :], v["st"][:, t, :])
                    link(last)
                    nc.vector.tensor_scalar(v["rs"][:, 0, :], v["mv"][:, :, 1], LN_EPS, None, ALU.add).then_inc(v_var_ok, 1)
                dve.wait_ge(const_in, 16 * V_CONSTS)
                dve.wait_ge(v_adj_in, 16 * V_TILES)
                for s, v in enumerate(V):
                    r, tiles, ng, nodes = v["rows"], v["tiles"], v["ng"], v["nodes"]
                    adj0, ag, dg = v["adj"], v["ag"], v["deg"]
                    link(nc.vector.tensor_tensor(adj0[:, :, :], adj0[:, :, :], v["self_"][:, :].unsqueeze(1).broadcast_to([r, tiles, nodes]), ALU.add))
                    for n in range(ng):
                        for t in range(tiles):
                            last = nc.vector.tensor_tensor(ag[:, n, t, :].rearrange("r (q u) -> r q u", u=nodes),
                                                           adj0[:, t, :].unsqueeze(1).broadcast_to([r, v["per_tile"], nodes]),
                                                           v["mask"][:, n, :].rearrange("r (q u) -> r q u", u=nodes), ALU.mult)
                    link(last)
                    agf = ag[:, :, :, :].rearrange("p g t m -> p (g t) m")
                    link(nc.vector.reduce_sum(dg[:, 0, :], agf, axis=AX.X))
                    link(nc.vector.tensor_scalar(dg[:, 3, :], dg[:, 0, :], 0.0, None, ALU.is_equal))
                    nc.vector.tensor_tensor(dg[:, 1, :], dg[:, 0, :], dg[:, 3, :], ALU.add).then_inc(v_deg_safe, 1)
                    dve.wait_ge(v_deg_safe, s + 1)
                    link(nc.vector.tensor_scalar(dg[:, 0, :], dg[:, 3, :], -1.0, 1.0, ALU.mult, ALU.add))
                    dve.wait_ge(v_rstd, s + 1)
                    for t in range(tiles):
                        last = nc.vector.tensor_scalar(v["h"][:, t, :], v["x"][:, t, :], v["mv"][:, t, 0:1], v["rs"][:, 1, t:t + 1],
                                                       ALU.subtract, ALU.mult)
                    link(last)
                    nc.vector.tensor_scalar(v["h"][:, :, :], v["h"][:, :, :], 0.0, None, ALU.max).then_inc(v_h_ok, 1)
                    dve.wait_ge(v_deg_pow, s + 1)
                    link(nc.vector.tensor_tensor(dg[:, 3, :], dg[:, 2, :], dg[:, 0, :], ALU.mult))
                    nc.vector.tensor_tensor(agf, agf, dg[:, 3, :].unsqueeze(2).broadcast_to([r, ng * tiles, r]), ALU.mult).then_inc(v_ag_ok, 1)
                dve.wait_ge(vectors_in, 16 * 9)
                link(nc.vector.reduce_max(v_red[:, 0:1], v_fw[:, 0, :], axis=AX.X))
                nc.vector.tensor_scalar(v_red[:, 1:2], v_red[:, 0:1], -1.0, None, ALU.mult).then_inc(v_fw_sub, 1)
                dve.wait_ge(v_fw_exp, 1)
                link(nc.vector.reciprocal(v_red[:, 3:4], v_red[:, 2:3]))
                link(nc.vector.tensor_scalar(v_fw[:, 3, :], v_fw[:, 1, :], v_red[:, 3:4], None, ALU.mult))
                for v in V:
                    g0, ng, r = v["groups"][0], v["ng"], v["rows"]
                    last = nc.vector.tensor_tensor(v["wm"][:, :], v["member"][:, :], v_fw[0:r, 3, g0:g0 + ng], ALU.mult)
                link(last)
                use, gidx = 0, 0
                for s, v in enumerate(V):
                    r, tiles = v["rows"], v["tiles"]
                    for n in range(v["ng"]):
                        g = v["groups"][n]
                        for step in first_transposes(gidx)[:1]:
                            do(step, -1, None, True)
                        for t in range(tiles):
                            use += 1
                            dve.wait_ge(v_ring_mm, use)
                            nc.vector.tensor_copy(v_s2[0:r, t, :], ps[0:r, V_OUT[use % 2], 0:D]).then_inc(v_ring_free, 1)
                        for step in first_transposes(gidx)[1:]:
                            do(step, -1, None, True)
                        for t in range(tiles):
                            use += 1
                            dve.wait_ge(v_ring_mm, use)
                            nc.vector.tensor_tensor(v_u[0:r, t % 2, :], ps[0:r, V_OUT[use % 2], 0:D], v_b2[0:r, g, :], ALU.add).then_inc(v_ring_free, 1)
                            dve.wait_ge(v_ring_free, use)
                            if s and n == 0:
                                last = nc.vector.tensor_scalar(v["acc"][:, t, :], v_u[0:r, t % 2, :], 0.0, v["wm"][:, n:n + 1], ALU.max, ALU.mult)
                            else:
                                link(nc.vector.tensor_scalar(v_u[0:r, t % 2, :], v_u[0:r, t % 2, :], 0.0, v["wm"][:, n:n + 1], ALU.max, ALU.mult))
                                last = nc.vector.tensor_tensor(v["acc"][:, t, :], v["acc"][:, t, :], v_u[0:r, t % 2, :], ALU.add)
                            if t + 1 < tiles:
                                link(last)
                        if s and n == 1:
                            link(last)
                            dve.wait_ge(v_acc_in, 16 * tiles)
                            last = nc.vector.tensor_tensor(v["acc"][:, :, :], v["acc"][:, :, :], v["x"][:, :, :], ALU.add)
                        gidx += 1
                        last.then_inc(v_done, 1)
                        dve.wait_ge(v_done, gidx)
                        if gidx <= 4:
                            hi, lo, st_ = main_weights[gidx - 1]
                            dve.wait_ge(w_hi_ok, gidx)
                            nc.vector.tensor_tensor(lo[:, :, :], st_[:, :, :], f(hi[:, :, :]), ALU.subtract).then_inc(w_ok, 1)
                dve.wait_ge(v_stored, 16 * V_TILES)

            def do(step, i, j, first):
                kind = step[0]
                pro = isinstance(i, int) and i < 0
                if kind == "tr":
                    _, ahead, tile, g = step
                    b = i + ahead
                    n = 2 * tile + g
                    dve.wait_ge(adj_hi_ok, upto(b, 2 * NT, n + 1))
                    nc.vector.tensor_tensor(adj_lo[:, g * TH:(g + 1) * TH, tile * P:(tile + 1) * P],
                                            bank(RING[n % 2]).rearrange("p (a b) -> p a b", b=P),
                                            f(adj_hi[:, g * TH:(g + 1) * TH, tile * P:(tile + 1) * P]), ALU.subtract).then_inc(ring_free, 1)
                    if g == 0:
                        dve.wait_ge(adj_in[tile % 2], upto(b, 16 * TH, 16 * (tile // 2 + 1)))
                        if tile == 0 and not pro:
                            dve.wait_ge(deg_ok, upto(b, 1, 0))
                        nc.vector.reduce_sum(deg[:, 0, tile:tile + 1], raw[:, tile % 2, :], axis=AX.X).then_inc(rowsum_ok, 1)
                elif kind == "deg":
                    dve.wait_ge(rowsum_ok, upto(i, NT, NT))
                    if not first:
                        dve.wait_ge(hs_ok, upto(i, NT, 0))
                    nc.vector.tensor_scalar(deg[:, 1, :], deg[:, 0, :], DEG_EPS, None, ALU.add).then_inc(deg_ok, 1)
                    dve.wait_ge(deg_ok, upto(i, 1, 1))
                    nc.vector.reciprocal(inv_deg[:, :], deg[:, 1, :]).then_inc(inv_ok, 1)
                    dve.wait_ge(inv_ok, upto(i, 1, 1))
                elif kind == "stats":
                    _, L, t = step
                    if t % 2 == 0:
                        b = i + 1
                        if t == 0:
                            dve.wait_ge(x_in[0], upto(b, 16 * X_DMAS, 16 * X_DMAS))
                        if t == TH:
                            dve.wait_ge(x_in[1], upto(b, 16, 16))
                        layer_stats(b, t, t, pro)
                elif kind == "norm":
                    _, L, t = step
                    half = t // TH
                    b = i + 1 if (L == 1 and half == 0) else i
                    n = (L - 1) * NT + t
                    if t % TH == 0:
                        dve.wait_ge(rstd_ok, upto(b, 6, 2 * (L - 1) + half + 1))
                        if L == 2 and half == 1:
                            dve.wait_ge(hs_ok, upto(b, NT, TH))
                        if L == 3 and half == 0:
                            dve.wait_ge(hs_ok, upto(b, NT, NT))
                    if not (pro and n < TH):
                        dve.wait_ge(h_ok, upto(b, 3 * NT, n - TH + 1))
                    nc.vector.tensor_scalar(y[:, t % TH, :], x[:, t, :], mv[:, t, 0:1], rstd[:, t % TH:t % TH + 1],
                                            ALU.subtract, ALU.mult).then_inc(y_ok, 1)
                elif kind == "split":
                    _, L, t = step
                    n = (L - 1) * NT + t
                    dve.wait_ge(h_hi_ok, upto(i, 3 * NT, n + 1))
                    nc.vector.scalar_tensor_tensor(out=h_lo[:, t, :], in0=y[:, t % TH, :], scalar=0.0, in1=f(h_hi[:, t, :]),
                                                   op0=ALU.max, op1=ALU.subtract).then_inc(h_ok, 1)
                elif kind == "pt":
                    _, L, c, d = step
                    if L < 3:
                        n = agg_group(L, c, d)
                        dve.wait_ge(pt_hi_ok, upto(i, 8, n + 1))
                        nc.vector.tensor_tensor(pt_lo[:, d, :], bank(AGG[n % 3]), f(pt_hi[:, d, :]), ALU.subtract).then_inc(pt_ok, 1)
                elif kind == "ht" and step[1] % 2:
                    c = step[1] // 2
                    for d in range(ND):
                        dve.wait_ge(ht_hi_ok, upto(i, 4, 2 * c + d + 1))
                        nc.vector.tensor_tensor(ht_lo[:, d, :], bank(RING[d]), f(ht_hi[:, d, :]), ALU.subtract).then_inc(ring_free, 1)
                elif kind == "w":
                    _, L, c, p = step
                    u = ring_use(i, ring_of["w", L, c] + p)
                    dve.wait_ge(w_mm, upto(i, 8, 4 * (L - 1) + 2 * c + p + 1))
                    t0 = c * TH + 2 * p
                    o = bank(RING[p]).rearrange("p (a b) -> p a b", b=D)
                    if L == 1:
                        dve.wait_ge(xb_ok, upto(i, NT, t0 + 2))
                        nc.vector.tensor_tensor(x[:, t0:t0 + 2, :], o, x[:, t0:t0 + 2, :], ALU.add).then_inc(ring_free, 1)
                    else:
                        for q in range(2):
                            last = nc.vector.scalar_tensor_tensor(out=o[:, q, :], in0=o[:, q, :], scalar=inv_deg[:, t0 + q:t0 + q + 1],
                                                                  in1=bias2[:, :], op0=ALU.mult, op1=ALU.add)
                        last.then_inc(relu_ok, 1)
                        dve.wait_ge(relu_ok, upto(i, NT // 2, t0 // 2 + 1))
                        dve.wait_ge(y_ok, upto(i, 3 * NT, NT + t0 + 2))
                        nc.vector.scalar_tensor_tensor(out=x[:, t0:t0 + 2, :], in0=o, scalar=0.0, in1=x[:, t0:t0 + 2, :],
                                                       op0=ALU.max, op1=ALU.add).then_inc(ring_free, 1)
                    dve.wait_ge(ring_free, u + 1)
                    layer_stats(i, L * NT + t0, t0, False)
                elif kind == "fix":
                    t = step[1]
                    dh, dl = adj_hi[:, t, t * P:(t + 1) * P], adj_lo[:, t, t * P:(t + 1) * P]
                    dve.wait_ge(fix_hi_ok, upto(i, NT, t + 1))
                    nc.vector.tensor_tensor(dl, fixed[:, t % 2, :], f(dh), ALU.subtract).then_inc(fix_ok, 1)
                elif kind == "chunk_split":
                    c = step[1]
                    if c % 2 == 0:
                        dve.wait_ge(agg_ok, upto(j, 4, 2 * (c // 2) + 2))
                    if c == 0 and not (isinstance(j, int) and j == 0):
                        dve.wait_ge(rms_ok, upto(j, NC, 0))
                        dve.wait_ge(bcast_mm, upto(j, NC, 0))
                    if not (isinstance(j, int) and j == 0 and c == 0):
                        dve.wait_ge(up_mm, upto(j, PAIRS * NC, PAIRS * c))
                    src = agg[:, :, c * CH:(c + 1) * CH]
                    nc.vector.tensor_copy(ac_hi[:, :, :], src).then_inc(ac_hi_ok, 1)
                    dve.wait_ge(ac_hi_ok, upto(j, NC, c + 1))
                    nc.vector.tensor_tensor(ac_lo[:, :, :], src, f(ac_hi[:, :, :]), ALU.subtract).then_inc(ac_ok, 1)
                elif kind == "sumsq":
                    c = step[1]
                    dve.wait_ge(col_mm, upto(j, NC, c + 1))
                    if c > 0:
                        dve.wait_ge(rms_ok, upto(j, NC, c))
                    nc.vector.tensor_scalar(msq[:, :], bank(hidden(j, c)[1][0], 2), 1.0 / H, RMS_EPS, ALU.mult, ALU.add).then_inc(msq_ok, 1)
                elif kind == "rms_rows":
                    c = step[1]
                    dve.wait_ge(rms_ok, upto(j, NC, c + 1))
                    if c > 0:
                        dve.wait_ge(bcast_mm, upto(j, NC, c))
                    for q in range(2):
                        last = nc.vector.tensor_scalar(rms_rows[:, q, :], ident[:, :], 0.0, rms[:, q:q + 1], ALU.mult, ALU.add)
                    last.then_inc(rms_rows_ok, 1)
                elif kind == "scale":
                    _, c, p = step
                    dve.wait_ge(bcast_mm, upto(j, NC, c + 1))
                    dve.wait_ge(hid_ok, upto(j, PAIRS * NC, PAIRS * c + p + 1))
                    hid, banks = hidden(j, c)
                    part = hid[:, 2 * p:2 * p + 2, :]
                    nc.vector.tensor_tensor(part, part, bank(banks[1], CH).unsqueeze(1).broadcast_to([P, 2, CH]), ALU.mult).then_inc(scaled_ok, 1)
                elif kind == "act":
                    _, c, p = step
                    n = PAIRS * c + p
                    dve.wait_ge(act_hi_ok, upto(j, PAIRS * NC, n + 1))
                    hid, banks = hidden(j, c)
                    nc.vector.tensor_tensor(act_lo[:, p % 2], hid[:, 2 * p:2 * p + 2, :], f(act_hi[:, p % 2]), ALU.subtract).then_inc(act_ok, 1)
                elif kind == "result":
                    c = step[1]
                    dve.wait_ge(down_mm, upto(j, PAIRS * NC, PAIRS * (c + 1)))
                    dve.wait_ge(tail_ok, upto(j, NT, 2 * c + 2))
                    t2 = tail[:, 2 * c:2 * c + 2, :]
                    nc.vector.tensor_tensor(t2, bank(DOWN).rearrange("p (a b) -> p a b", b=D), t2, ALU.add).then_inc(res_ok, 1)

            def layer_stats(b, n, t, pro):
                if not pro and n == 0:
                    dve.wait_ge(y_ok, upto(b, 3 * NT, 0))
                for q in range(2):
                    last = nc.vector.bn_stats(st[:, t + q, :], x[:, t + q, :])
                last.then_inc(bn_ok, 1)
                wait_apart(dve, bn_ok, upto(b, 3 * NT // 2, n // 2 + 1))
                for q in range(2):
                    nc.vector.bn_aggr(mv[:, t + q, :], st[:, t + q, :]).then_inc(stats_ok, 1)

            layer_0()
            run(dve, do)

        @block.tensor
        def _(pe):
            def layer_0():
                pe.wait_ge(const_in, 16 * V_CONSTS)
                pe.wait_ge(const_ok, 2)
                done_tr, gidx, use = 0, 0, 0
                for s, v in enumerate(V):
                    r, tiles = v["rows"], v["tiles"]
                    cols = r * tiles
                    pe.wait_ge(v_ag_ok, s + 1)
                    for n in range(v["ng"] * tiles):
                        done_tr += 1
                        if done_tr > 2:
                            pe.wait_ge(v_ant, done_tr - 2)
                        g, t = divmod(n, tiles)
                        nc.tensor.transpose(ps[0:r, V_HID[done_tr % 2], 0:r], v["ag"][:, g, t, :], ident[0:r, 0:r]).then_inc(v_tr, 1)
                    pe.wait_ge(v_h_ok, s + 1)
                    pe.wait_ge(v_ant, done_tr)
                    for n in range(v["ng"]):
                        for d in range(ND):
                            for t in range(tiles):
                                last = nc.tensor.matmul(ps[:, V_AGG[d], t * r:(t + 1) * r], v["h"][:, t, d * P:(d + 1) * P], v["an_t"][:, n, t, :],
                                                        start=True, stop=True)
                            last.then_inc(v_y_mm, 1)
                        for step in first_transposes(gidx)[:1]:
                            do(step, -1, None, True)
                        pe.wait_ge(v_w_in[gidx % 2], 32 * (gidx // 2 + 1))
                        pe.wait_ge(v_y_ok, ND * (gidx + 1))
                        for k in range(NK0):
                            if NK0 * gidx + k >= 2:
                                pe.wait_ge(v_hid_ok, NK0 * gidx + k - 1)
                            for d in range(ND):
                                last = nc.tensor.matmul(ps[:, V_HID[k % 2], 0:cols], v_w1[:, gidx % 2, d, k * P:(k + 1) * P], v_yt[:, d, 0:cols],
                                                        start=(d == 0), stop=(d == ND - 1))
                            last.then_inc(v_hid_mm, 1)
                        for step in first_transposes(gidx)[1:]:
                            do(step, -1, None, True)
                        pe.wait_ge(v_hid_ok, NK0 * (gidx + 1))
                        for t in range(tiles):
                            use += 1
                            if use > 2:
                                pe.wait_ge(v_ring_free, use - 2)
                            for k in range(NK0):
                                last = nc.tensor.matmul(ps[0:r, V_OUT[use % 2], 0:D], v_hid[:, k, t * r:(t + 1) * r], v_w2[:, gidx % 2, k, :],
                                                        start=(k == 0), stop=(k == NK0 - 1))
                            last.then_inc(v_ring_mm, 1)
                        for t in range(tiles):
                            use += 1
                            pe.wait_ge(v_ring_free, max(use - 2, use - tiles))
                            nc.tensor.matmul(ps[0:r, V_OUT[use % 2], 0:D], v["an_t"][:, n, t, :], v_s2[0:r, t, :], start=True, stop=True).then_inc(v_ring_mm, 1)
                        gidx += 1
                pe.wait_ge(v_stored, 16 * V_TILES)
                pe.wait_ge(w_ok, 4)

            def three(o, w_hi, w_lo, m_hi, m_lo, start, stop, skip=False):
                nc.tensor.matmul(o, w_hi, m_hi, start=start, stop=False, skip_group_check=skip)
                nc.tensor.matmul(o, w_hi, m_lo, start=False, stop=False, skip_group_check=skip)
                return nc.tensor.matmul(o, w_lo, m_hi, start=False, stop=stop, skip_group_check=skip)

            def ring_wait(u):
                if not (isinstance(u, int) and u < 2):
                    pe.wait_ge(ring_free, u - 1)

            def agg_free(i, L, c, d, first):
                n = agg_group(L, c, d) - 3
                if n >= 8:
                    pe.wait_ge(agg_ok, upto(i, 4, n - 7))
                elif n >= 0:
                    pe.wait_ge(pt_ok, upto(i, 8, n + 1))
                elif not first:
                    pe.wait_ge(agg_ok, upto(i, 4, n + 1) if not isinstance(i, int) else 4 * i + n + 1)

            def agg_unit(L, c, d, m):
                rhs = slice(c * HALF, (c + 1) * HALF)
                w = slice(d * P, (d + 1) * P)
                return three(bank(AGG[agg_group(L, c, d) % 3]), h_hi[:, m, w], h_lo[:, m, w], adj_hi[:, m, rhs], adj_lo[:, m, rhs],
                             m == 0, m == NT - 1)

            def do(step, i, j, first):
                kind = step[0]
                if kind == "tr":
                    _, ahead, tile, g = step
                    b = i + ahead
                    if g == 0:
                        pe.wait_ge(adj_in[tile % 2], upto(b, 16 * TH, 16 * (tile // 2 + 1)))
                    ring_wait(tr_use(b, tile, g))
                    for q in range(TH):
                        m = g * TH + q
                        last = nc.tensor.transpose(bank(RING[g])[:, q * P:(q + 1) * P], raw[:, tile % 2, m * P:(m + 1) * P], ident[:, :])
                    last.then_inc(tr_mm, 1)
                elif kind == "agg2":
                    _, L, m = step
                    pe.wait_ge(h_ok, upto(i, 3 * NT, (L - 1) * NT + m + 1))
                    if m == 0 and L == 1:
                        pe.wait_ge(ring_free, ring_use(i, 0))
                    if L == 3 and m < TH:
                        pe.wait_ge(fix_ok, upto(i, NT, m + 1))
                    for d in range(ND):
                        if m == 0:
                            agg_free(i, L, 0, d, first)
                        last = agg_unit(L, 0, d, m)
                        if m == NT - 1:
                            last.then_inc(agg_mm, 1)
                elif kind == "agg1":
                    _, L, d, m = step
                    if m == 0:
                        if L == 1 and d == 0:
                            pe.wait_ge(ring_free, ring_use(i, 8))
                        agg_free(i, L, 1, d, first)
                        if L == 3 and d == 0:
                            pe.wait_ge(fix_ok, upto(i, NT, NT))
                    last = agg_unit(L, 1, d, m)
                    if m == NT - 1:
                        last.then_inc(agg_mm, 1)
                elif kind == "ht":
                    pair = step[1]
                    c, second = divmod(pair, 2)
                    pe.wait_ge(hs_ok, upto(i, NT, 2 * pair + 2))
                    for d in range(ND):
                        if not second:
                            ring_wait(ring_use(i, ring_of["ht", 2, c] + d))
                        for q in range(2):
                            at = slice((2 * second + q) * P, (2 * second + q + 1) * P)
                            last = nc.tensor.transpose(bank(RING[d])[:, at], hs[:, q, d * P:(d + 1) * P], ident[:, :])
                    last.then_inc(ht_mm, 1)
                elif kind == "w":
                    _, L, c, p = step
                    if p == 0:
                        pe.wait_ge(pt_ok, upto(i, 8, 4 * (L - 1) + 2 * c + 2))
                        if L == 2:
                            pe.wait_ge(ring_free, ring_use(i, ring_of["ht", 2, c] + 2))
                    ring_wait(ring_use(i, ring_of["w", L, c] + p))
                    for q in range(2):
                        o = bank(RING[p])[:, q * D:(q + 1) * D]
                        at = slice((2 * p + q) * P, (2 * p + q + 1) * P)
                        for d in range(ND):
                            if L == 1:
                                last = three(o, pt_hi[:, d, at], pt_lo[:, d, at], wa_hi[:, d, :], wa_lo[:, d, :], d == 0, d == ND - 1)
                            else:
                                three(o, ht_hi[:, d, at], ht_lo[:, d, at], wb_hi[:, d, :], wb_lo[:, d, :], d == 0, False)
                                last = three(o, pt_hi[:, d, at], pt_lo[:, d, at], wb_hi[:, ND + d, :], wb_lo[:, ND + d, :], False, d == ND - 1)
                    last.then_inc(w_mm, 1)
                elif kind == "up":
                    _, c, p = step
                    zero = isinstance(j, int) and j == 0 and c == 0
                    turns = last_graph(j) and c > 0
                    if p == 0:
                        pe.wait_ge(ac_ok, upto(j, NC, c + 1))
                        if turns and c == 1:
                            pe.wait_ge(agg_ok, upto(j, 4, 4))
                        elif turns:
                            pe.wait_ge(msq_ok, upto(j, NC, c - 1))
                        elif not zero:
                            pe.wait_ge(msq_ok, upto(j, NC, c))
                            if c == 0:
                                pe.wait_ge(res_ok, upto(j, NC, 0))
                    elif p == 1:
                        if not zero and not (turns and c == 1):
                            pe.wait_ge(scaled_ok, upto(j, PAIRS * NC, PAIRS * (c - turns)))
                    else:
                        pe.wait_ge(sq_ok, upto(j, PAIRS * NC, PAIRS * c + p - 1))
                    for q in range(2):
                        k = 2 * p + q
                        o = bank(hidden(j, c)[1][p % 2])[:, q * CH:(q + 1) * CH]
                        for d in range(ND):
                            last = three(o, w1_hi[:, d, k * P:(k + 1) * P], w1_lo[:, d, k * P:(k + 1) * P], ac_hi[:, d, :], ac_lo[:, d, :],
                                         d == 0, d == ND - 1)
                    last.then_inc(up_mm, 1)
                elif kind == "sumsq":
                    c = step[1]
                    pe.wait_ge(sum_ok, upto(j, 2 * PAIRS * NC, 2 * PAIRS * (c + 1)))
                    for q in range(2):
                        last = nc.tensor.matmul(bank(hidden(j, c)[1][0])[:, q:q + 1], sq_sum[:, q * P:(q + 1) * P], ones[:, 0:1], start=True, stop=True)
                    last.then_inc(col_mm, 1)
                elif kind == "bcast":
                    c = step[1]
                    pe.wait_ge(rms_rows_ok, upto(j, NC, c + 1))
                    for q in range(2):
                        last = nc.tensor.matmul(bank(hidden(j, c)[1][1])[:, q * P:(q + 1) * P], rms_rows[:, q, :], ident[:, :], start=True, stop=True)
                    last.then_inc(bcast_mm, 1)
                elif kind == "down":
                    _, c, p = step
                    n = PAIRS * c + p
                    if p == 0 and c > 0:
                        pe.wait_ge(res_ok, upto(j, NC, c))
                    pe.wait_ge(act_ok, upto(j, PAIRS * NC, n + 1))
                    for a in range(2):
                        k = 2 * p + a
                        for q in range(2):
                            at = slice(q * P, (q + 1) * P)
                            last = three(bank(DOWN)[:, q * D:(q + 1) * D], act_hi[:, p % 2, a, at], act_lo[:, p % 2, a, at],
                                         w2_hi[:, k, :], w2_lo[:, k, :], k == 0 and q == 0, k == NH - 1, skip=True)
                    last.then_inc(down_mm, 1)

            layer_0()
            run(pe, do)


_INS = ["x", "adj", "L0_gnn_W1", "L0_gnn_b1", "L0_gnn_W2", "L0_gnn_b2", "L0_gnn_fusion_w", "L1_gnn_weight", "L1_gnn_bias",
        "L2_gnn_weight", "L2_gnn_bias", "L3_gnn_epsilon", "L3_gnn_W1", "L3_gnn_b1", "L3_gnn_rms_weight", "L3_gnn_W2",
        "L3_gnn_b2"]


def build(nc, arrays):
    f32 = mybir.dt.float32
    t_in = {n: nc.dram_tensor(f"in_{n}", a.shape, f32, kind="ExternalInput").ap() for n, a in arrays.items()}
    shape = arrays["x"].shape
    out = nc.dram_tensor("out_x", shape, f32, kind="ExternalOutput").ap()
    scratch = nc.dram_tensor("scratch_rows", (shape[0], SPACES[0][0], shape[2]), f32, kind="Internal").ap()
    gnn_stack(nc, t_in, out, scratch)


def kernel(**inputs):
    import concourse.bacc as bacc
    from concourse.bass_utils import run_bass_kernel_spmd

    arrays = {n: np.ascontiguousarray(inputs[n]) for n in _INS}
    arrays["L3_gnn_epsilon"] = arrays["L3_gnn_epsilon"].reshape(1)
    arrays.update(shape_constants())
    nc = bacc.Bacc("TRN2", target_bir_lowering=False, num_devices=1)
    build(nc, arrays)
    r = run_bass_kernel_spmd(nc, [{f"in_{n}": a for n, a in arrays.items()}], core_ids=[0])
    return r.results[0]["out_x"]
```
